# Optimizing a Trainium2 kernel written in Bass

```python
import numpy as np
import jax
import jax.numpy as jnp

def _softmax(x, axis=-1):
    return jax.nn.softmax(x, axis=axis)

def _gelu(x):
    return jax.nn.gelu(x, approximate=True)

def _silu(x):
    return jax.nn.silu(x)

def _sigmoid(x):
    return jax.nn.sigmoid(x)

def _layernorm(x, axis=-1, eps=1e-05):
    m = jnp.mean(x, axis=axis, keepdims=True)
    v = jnp.var(x, axis=axis, keepdims=True)
    return (x - m) / jnp.sqrt(v + eps)

def _scatter_add(tgt, idx, src, axis=0):
    return tgt.at[idx].add(src)

def _segment_sum(src, seg, n):
    return jax.ops.segment_sum(src, seg, n)
kernel_name = 'mk_gps_d1_gnn_r8_9a4c16'

def setup_inputs(seed: int=0):
    np.random.seed(seed)
    _w = jnp.asarray

    def _rec_inputs():
        import jax
        import jax.numpy as jnp
        _gk = jax.random.key(seed)
        x = -0.0003713 + 1 * jax.random.normal(jax.random.fold_in(_gk, 1), (6250, 256), jnp.float32)
        _s = jax.random.randint(jax.random.fold_in(_gk, 2), (50000,), 0, 6250, jnp.int32)
        _d = jax.random.randint(jax.random.fold_in(_gk, 3), (50000,), 0, 6250, jnp.int32)
        _loop = jnp.arange(6250, dtype=jnp.int32)
        src = jnp.concatenate([_s, _d, _loop])
        dst = jnp.concatenate([_d, _s, _loop])
        _o = jnp.argsort(dst, stable=True)
        src = src[_o]
        dst = dst[_o]
        return (x, src, dst)
    x, src, dst = _rec_inputs()

    def _L0_gnn_setup():
        import jax, jax.numpy as jnp
        import numpy as np
        HIDDEN = 256
        HEADS = 8
        HEAD_DIM = HIDDEN // HEADS
        N_NODES = 6250
        N_EDGES = 100000
        key = jax.random.key(seed)
        ks = jax.random.split(key, 12)
        h = jax.random.normal(ks[0], (N_NODES, HIDDEN), dtype=jnp.float32)
        row = jax.random.randint(ks[1], (N_EDGES,), 0, N_NODES, dtype=jnp.int64 if jax.config.jax_enable_x64 else jnp.int32)
        col = jax.random.randint(ks[2], (N_EDGES,), 0, N_NODES, dtype=jnp.int64 if jax.config.jax_enable_x64 else jnp.int32)

        def lin(kw, kb):
            W = jax.random.normal(kw, (HIDDEN, HIDDEN), dtype=jnp.float32) * 0.02
            b = jax.random.normal(kb, (HIDDEN,), dtype=jnp.float32) * 0.02
            return (W, b)
        Wq, bq = lin(ks[3], ks[4])
        Wk, bk = lin(ks[5], ks[6])
        Wv, bv = lin(ks[7], ks[8])
        Wo, bo = lin(ks[9], ks[10])
        return {'h': h, 'row': row, 'col': col, 'Wq': Wq, 'bq': bq, 'Wk': Wk, 'bk': bk, 'Wv': Wv, 'bv': bv, 'Wo': Wo, 'bo': bo}
    _L0_gnn_all = _L0_gnn_setup()
    _L0_gnn_in = {k: v for k, v in _L0_gnn_all.items() if k in ('Wq', 'bq', 'Wk', 'bk', 'Wv', 'bv', 'Wo', 'bo')}
    del _L0_gnn_all

    def _L0_mix_setup():
        import jax, jax.numpy as jnp
        import numpy as np
        B, N, C, H = (8, 2048, 256, 8)
        D = C // H
        GH = C // 4
        key = jax.random.key(seed)
        ks = jax.random.split(key, 6)
        s = 0.02
        return {'x': jax.random.normal(ks[0], (B, N, C), dtype=jnp.float32), 'Wqkv': jax.random.normal(ks[1], (C, 3 * C), dtype=jnp.float32) * s, 'Wproj': jax.random.normal(ks[2], (C, C), dtype=jnp.float32) * s, 'bproj': jnp.zeros((C,), dtype=jnp.float32), 'ln_g': jnp.ones((C,), dtype=jnp.float32), 'ln_b': jnp.zeros((C,), dtype=jnp.float32), 'Wg1': jax.random.normal(ks[3], (C, GH), dtype=jnp.float32) * s, 'bg1': jnp.zeros((GH,), dtype=jnp.float32), 'Wg2': jax.random.normal(ks[4], (GH, C), dtype=jnp.float32) * s, 'bg2': jnp.zeros((C,), dtype=jnp.float32)}
    _L0_mix_all = _L0_mix_setup()
    _L0_mix_in = {k: v for k, v in _L0_mix_all.items() if k in ('Wqkv', 'Wproj', 'bproj', 'ln_g', 'ln_b', 'Wg1', 'bg1', 'Wg2', 'bg2')}
    del _L0_mix_all

    def _L0_ffn_setup():
        import jax, jax.numpy as jnp
        import numpy as np
        B, S, D, E, H, K = (4, 512, 256, 8, 512, 2)
        key = jax.random.key(seed)
        ks = jax.random.split(key, 6)
        x = jax.random.normal(ks[0], (B, S, D), jnp.float32)
        Wg = jax.random.normal(ks[1], (D, E), jnp.float32) * 0.02
        bg = jnp.zeros((E,), jnp.float32)
        W1 = jax.random.normal(ks[2], (E, D, H), jnp.float32) * 0.02
        b1 = jnp.zeros((E, H), jnp.float32)
        W2 = jax.random.normal(ks[3], (E, H, D), jnp.float32) * 0.02
        b2 = jnp.zeros((E, D), jnp.float32)
        return {'x': x, 'Wg': Wg, 'bg': bg, 'W1': W1, 'b1': b1, 'W2': W2, 'b2': b2}
    _L0_ffn_all = _L0_ffn_setup()
    _L0_ffn_in = {k: v for k, v in _L0_ffn_all.items() if k in ('Wg', 'bg', 'W1', 'b1', 'W2', 'b2')}
    del _L0_ffn_all
    return {'x': x, 'src': src, 'dst': dst, 'L0_gnn_Wq': _L0_gnn_in['Wq'], 'L0_gnn_bq': _L0_gnn_in['bq'], 'L0_gnn_Wk': _L0_gnn_in['Wk'], 'L0_gnn_bk': _L0_gnn_in['bk'], 'L0_gnn_Wv': _L0_gnn_in['Wv'], 'L0_gnn_bv': _L0_gnn_in['bv'], 'L0_gnn_Wo': _L0_gnn_in['Wo'], 'L0_gnn_bo': _L0_gnn_in['bo'], 'L0_mix_Wqkv': _L0_mix_in['Wqkv'], 'L0_mix_Wproj': _L0_mix_in['Wproj'], 'L0_mix_bproj': _L0_mix_in['bproj'], 'L0_mix_ln_g': _L0_mix_in['ln_g'], 'L0_mix_ln_b': _L0_mix_in['ln_b'], 'L0_mix_Wg1': _L0_mix_in['Wg1'], 'L0_mix_bg1': _L0_mix_in['bg1'], 'L0_mix_Wg2': _L0_mix_in['Wg2'], 'L0_mix_bg2': _L0_mix_in['bg2'], 'L0_ffn_Wg': _L0_ffn_in['Wg'], 'L0_ffn_bg': _L0_ffn_in['bg'], 'L0_ffn_W1': _L0_ffn_in['W1'], 'L0_ffn_b1': _L0_ffn_in['b1'], 'L0_ffn_W2': _L0_ffn_in['W2'], 'L0_ffn_b2': _L0_ffn_in['b2']}

def reference(x, src, dst, L0_gnn_Wq, L0_gnn_bq, L0_gnn_Wk, L0_gnn_bk, L0_gnn_Wv, L0_gnn_bv, L0_gnn_Wo, L0_gnn_bo, L0_mix_Wqkv, L0_mix_Wproj, L0_mix_bproj, L0_mix_ln_g, L0_mix_ln_b, L0_mix_Wg1, L0_mix_bg1, L0_mix_Wg2, L0_mix_bg2, L0_ffn_Wg, L0_ffn_bg, L0_ffn_W1, L0_ffn_b1, L0_ffn_W2, L0_ffn_b2):
    import jax
    import jax.numpy as jnp

    def _L0_gnn_ref(h, row, col, Wq, bq, Wk, bk, Wv, bv, Wo, bo):
        import jax, jax.numpy as jnp
        import numpy as np
        HIDDEN = 256
        HEADS = 8
        HEAD_DIM = HIDDEN // HEADS
        N_NODES = 6250
        N_EDGES = 100000
        N = h.shape[0]
        scaling = HEAD_DIM ** (-0.5)
        q = (h @ Wq.T + bq).reshape(N, HEAD_DIM, HEADS) * scaling
        k = (h @ Wk.T + bk).reshape(N, HEAD_DIM, HEADS)
        v = (h @ Wv.T + bv).reshape(N, HEAD_DIM, HEADS)
        s = jnp.einsum('edh,edh->eh', q[row], k[col])
        m = jax.ops.segment_max(s, row, num_segments=N)
        e = jnp.exp(s - m[row])
        z = jax.ops.segment_sum(e, row, num_segments=N)
        attn = e / z[row]
        out = jax.ops.segment_sum(attn[:, None, :] * v[col], row, num_segments=N)
        return out.reshape(N, -1) @ Wo.T + bo

    def _L0_mix_ref(x, Wqkv, Wproj, bproj, ln_g, ln_b, Wg1, bg1, Wg2, bg2):
        import jax, jax.numpy as jnp
        import numpy as np
        B, N, C, H = (8, 2048, 256, 8)
        D = C // H
        GH = C // 4
        b, n, c = x.shape
        h, d = (H, D)
        qkv = (x @ Wqkv).reshape(b, n, 3, h, d)
        q, k, v = (qkv[:, :, 0], qkv[:, :, 1], qkv[:, :, 2])
        k = jax.nn.softmax(k, axis=1)
        context = jnp.einsum('bnhd,bnhv->bhdv', k, v)
        out = jnp.einsum('bnhd,bhdv->bnhv', q, context).reshape(b, n, c)
        mu = jnp.mean(x, axis=-1, keepdims=True)
        var = jnp.var(x, axis=-1, keepdims=True)
        xn = (x - mu) * jax.lax.rsqrt(var + 1e-05) * ln_g + ln_b
        hgate = jax.nn.gelu(xn @ Wg1 + bg1, approximate=False)
        gate = jax.nn.sigmoid(hgate @ Wg2 + bg2)
        return out * gate @ Wproj + bproj

    def _L0_ffn_ref(x, Wg, bg, W1, b1, W2, b2):
        import jax, jax.numpy as jnp
        import numpy as np
        B, S, D, E, H, K = (4, 512, 256, 8, 512, 2)
        Bv, Sv, Dv = x.shape
        gate_scores = x @ Wg + bg
        _, idx = jax.lax.top_k(gate_scores, K)
        mask = jax.nn.one_hot(idx, E, dtype=x.dtype).sum(axis=-2)
        xf = x.reshape(-1, Dv)
        mf = mask.reshape(-1, E)
        h = jax.nn.gelu(jnp.einsum('td,edh->teh', xf, W1) + b1[None], approximate=False)
        y = jnp.einsum('teh,ehd->ted', h, W2) + b2[None]
        out = jnp.einsum('ted,te->td', y, mf)
        return out.reshape(Bv, Sv, Dv)
    xn = _layernorm(x, axis=-1)
    x = x + _L0_gnn_ref(xn, src, dst, L0_gnn_Wq, L0_gnn_bq, L0_gnn_Wk, L0_gnn_bk, L0_gnn_Wv, L0_gnn_bv, L0_gnn_Wo, L0_gnn_bo) + _L0_mix_ref(xn[None], L0_mix_Wqkv, L0_mix_Wproj, L0_mix_bproj, L0_mix_ln_g, L0_mix_ln_b, L0_mix_Wg1, L0_mix_bg1, L0_mix_Wg2, L0_mix_bg2)[0]
    x = x + _L0_ffn_ref(_layernorm(x, axis=-1)[None], L0_ffn_Wg, L0_ffn_bg, L0_ffn_W1, L0_ffn_b1, L0_ffn_W2, L0_ffn_b2)[0]
    return x

_drawn_inputs = setup_inputs


def setup_inputs(seed=0):
    import zlib

    import numpy as np

    out = dict(_drawn_inputs(seed))
    spreads = {'L0_mix_bproj': (0.0, 0.476),
     'L0_mix_ln_g': (1.0, 0.6),
     'L0_mix_ln_b': (0.0, 0.8),
     'L0_mix_bg1': (0.0, 0.8),
     'L0_mix_bg2': (0.0, 0.8),
     'L0_ffn_bg': (0.0, 0.549),
     'L0_ffn_b1': (0.0, 0.8),
     'L0_ffn_b2': (0.0, 0.362)}
    factors = {'L0_gnn_Wq': 33.181,
     'L0_gnn_bq': 64.0,
     'L0_gnn_Wk': 28.29,
     'L0_gnn_bk': 64.0,
     'L0_gnn_bv': 30.464,
     'L0_mix_Wqkv': 6.603,
     'L0_mix_Wproj': 7.73,
     'L0_mix_Wg1': 8.0,
     'L0_mix_Wg2': 8.0,
     'L0_gnn_Wv': 4.407,
     'L0_gnn_Wo': 4.239,
     'L0_gnn_bo': 8.0,
     'L0_ffn_W1': 3.347,
     'L0_ffn_W2': 3.132}
    for name, (base, spread) in spreads.items():
        noise = np.random.default_rng([zlib.crc32(name.encode()), seed]).standard_normal(out[name].shape)
        drawn = base * np.exp(spread * noise) if base else spread * noise
        out[name] = jnp.asarray(drawn.astype(out[name].dtype))
    for name, factor in factors.items():
        out[name] = (out[name] * factor).astype(out[name].dtype)
    return out
```

```python
from contextlib import ExitStack, contextmanager

import concourse.bass as bass
from concourse import mybir

F32 = mybir.dt.float32
BF16 = mybir.dt.bfloat16
I32 = mybir.dt.int32
U32 = mybir.dt.uint32
ALU = mybir.AluOpType
ACT = mybir.ActivationFunctionType
AX = mybir.AxisListType.X

P = 128
N = 6250
C = 256
H = 8
D = C // H
E = 106250
KC = C // P

NT = (N + P - 1) // P
TPG = 4
GN = TPG * P
NG = (NT + TPG - 1) // TPG
NPAD = NG * GN
NTP = NG * TPG

EL = 125
ET = E // EL
SB_ = 10
CH = 16
ST_NEED = (E + NT * (P - 1)) // P
GPC = (ST_NEED + CH - 1) // CH
ST = CH * GPC
HB = 4
NHB = ST // HB
STM = (ST + P - 1) // P * P
STX = ST + 2 * HB
ROWPAD = 8191
BIG = 1e30
NEXP = 8
HID = 512
HC = HID // P
GH = 64
EPS = 1e-5
SCALE = float(D) ** -0.5


def rows(ap, i):
    return ap[bass.ds(i * GN, GN), :].rearrange("(j p) c -> p j c", p=P)


@contextmanager
def stage(nc):
    with ExitStack() as cx:
        used = []

        def sem(name):
            used.append(cx.enter_context(nc.semaphore(name)))
            return used[-1]
        yield sem
        with nc.Block() as block:
            @block.gpsimd
            def _(g):
                for one in used:
                    g.sem_clear(one)


def counter(eng, name, first):
    reg = eng.alloc_register(name)
    eng.reg_mov(reg, first)
    return reg


def passed(eng, semaphore, reg, step):
    eng.wait_ge(semaphore, eng.snap(reg))
    eng.reg_add(reg, reg, step)


def bc(ap, shape):
    return ap.broadcast_to(shape)


def build(nc, A, out):
    ctx = ExitStack()
    with ctx:
        def sem(name):
            return ctx.enter_context(nc.semaphore(name))

        def sbp(name, shape, dt):
            return ctx.enter_context(nc.sbuf_tensor(name, shape, dt))

        def dram(name, shape, dt):
            return nc.dram_tensor(name, shape, dt).ap()

        W = dict(
            k=dram("k_tab", [NPAD, C], F32), v=dram("v_tab", [NPAD, C], F32),
            km=dram("kvmix", [NPAD, 2 * C], F32),
            xnT=dram("xnT_d", [P, KC, NPAD], F32), xmT=dram("xmT_d", [P, KC, NPAD], F32),
            sorted=dram("sorted_edges", [ST * P, 2], I32), tmap=dram("tile_map", [1, STM], I32),
            x2=dram("x2_d", [NPAD, C], F32), x2T=dram("x2T_d", [P, KC, NPAD], F32),
            ends=dram("chunk_ends", [2, P, 3], F32), carry=dram("chunk_carry", [2, CH, H], F32),
            mask=dram("expert_mask", [NPAD, NEXP], F32),
        )
        ident = sbp("ident", [P, P], F32)
        S = {}
        s_const = sem("const_loaded")
        with nc.Block() as block:
            @block.sync
            def _(sp):
                sp.dma_start(ident[:, :], A["ident"]).then_inc(s_const, 16)
                sp.wait_ge(s_const, 16)
        ctxbd = sbp("ctxbd", [P, KC, C], F32)
        kmax = sbp("kmax", [P, C], F32)
        score = sbp("score", [P, ST, H], F32)
        rowf = sbp("row_sorted", [P, ST], F32)
        rowl = sbp("row_in_tile", [P, STX], F32)
        coli = sbp("col_sorted", [P, STX], I32)
        tmap = sbp("tile_map_sb", [1, STM], I32)
        with ExitStack() as qx:
            q_sb = qx.enter_context(nc.sbuf_tensor("q_sb", [P, NTP, C], F32))
            with stage(nc) as sem:
                node_tables(nc, A, W, sem, ident, q_sb, kmax)
            with stage(nc) as sem:
                mix_context(nc, A, W, sem, ident, kmax, ctxbd)
            with ExitStack() as bx:
                pos_base = bx.enter_context(nc.sbuf_tensor("pos_base", [P, NT], F32))
                rc = bx.enter_context(nc.sbuf_tensor("rowcol", [EL, ET, 2], I32))
                lo = bx.enter_context(nc.sbuf_tensor("row_lo", [EL, ET], F32))
                hi = bx.enter_context(nc.sbuf_tensor("row_hi", [EL, ET], F32))
                with stage(nc) as sem:
                    histogram(nc, A, W, sem, ident, rc, lo, hi, pos_base)
                with stage(nc) as sem:
                    sort_edges(nc, A, W, sem, ident, rc, lo, hi, pos_base)
            with stage(nc) as sem:
                load_sorted(nc, A, W, sem, ident, rowf, rowl, coli, tmap)
            with stage(nc) as sem:
                edge_scores(nc, A, W, sem, rowl, coli, tmap, q_sb, score)
        with stage(nc) as sem:
            softmax_edges(nc, A, W, sem, ident, rowf, score)
        with ExitStack() as ax:
            acc = ax.enter_context(nc.sbuf_tensor("acc", [P, NTP, C + H], F32))
            with stage(nc) as sem:
                aggregate(nc, A, W, sem, rowl, coli, tmap, score, acc)
            with stage(nc) as sem:
                combine(nc, A, W, sem, ident, ctxbd, acc)
        with stage(nc) as sem:
            experts(nc, A, W, sem, ident, out)


def node_tables(nc, A, W, sem, ident, q_sb, kmax):
    with ExitStack() as cx:
        def sb(n, s, d=F32):
            return cx.enter_context(nc.sbuf_tensor("n_" + n, s, d))

        def ps(n, s, d=F32):
            return cx.enter_context(nc.psum_tensor("n_" + n, s, d))
        wall = sb("wall", [P, KC, 5 * C])
        bq = sb("bq", [P, C])
        bkv = sb("bkv", [P, 2 * C])
        lng = sb("lng", [P, KC])
        lnb = sb("lnb", [P, KC])
        vmask = sb("vmask", [P, NTP])
        xg = sb("xg", [P, TPG, C])
        xn = sb("xn", [P, TPG, C])
        xm = sb("xm", [P, TPG, C])
        st1 = sb("st1", [P, TPG, 6])
        st2 = sb("st2", [P, TPG, 6])
        mv1 = sb("mv1", [P, TPG, 2])
        mv2 = sb("mv2", [P, TPG, 2])
        ve1 = sb("ve1", [P, TPG])
        ve2 = sb("ve2", [P, TPG])
        sd1 = sb("sd1", [P, TPG])
        sd2 = sb("sd2", [P, TPG])
        rs1 = sb("rs1", [P, TPG])
        rs2 = sb("rs2", [P, TPG])
        xnT = sb("xnT", [P, KC, GN])
        xmT = sb("xmT", [P, KC, GN])
        kv = sb("kv", [P, TPG, 2 * C])
        kvm = sb("kvm", [P, TPG, 2 * C])
        pT = ps("pT", [P, KC, GN])
        pM = ps("pM", [P, KC, GN])
        pA = ps("pA", [P, 2 * C])
        pB = ps("pB", [P, 2 * C])
        pC = ps("pC", [P, C])
        w_in = sem("n_weights_in")
        x_in = sem("n_x_in")
        stats1 = sem("n_stats1")
        aggr1 = sem("n_aggr1")
        var1 = sem("n_var1")
        std1 = sem("n_std1")
        rstd1 = sem("n_rstd1")
        xn_done = sem("n_xn_done")
        stats2 = sem("n_stats2")
        aggr2 = sem("n_aggr2")
        var2 = sem("n_var2")
        std2 = sem("n_std2")
        rstd2 = sem("n_rstd2")
        xm_done = sem("n_xm_done")
        xn_turned = sem("n_xn_turned")
        xm_turned = sem("n_xm_turned")
        xnT_done = sem("n_xnT_done")
        xmT_done = sem("n_xmT_done")
        xT_stored = sem("n_xT_stored")
        kv_stored = sem("n_kv_stored")
        kvm_stored = sem("n_kvm_stored")
        proj = sem("n_proj")
        proj_read = sem("n_proj_read")
        vm_read = sem("n_vm_read")
        kmax_step = sem("n_kmax_step")
        km_done = sem("n_km_done")

        with nc.Block() as block:
            @block.sync
            def _(sp):
                for dst, name in ((wall, "wall"), (bq, "bq"), (bkv, "bkv"), (lng, "lng"), (lnb, "lnb"), (vmask, "vmask")):
                    d = dst[:, :, :] if name == "wall" else dst[:, :]
                    sp.dma_start(d, A[name]).then_inc(w_in, 16)
                sp.dma_start(xg[:, :, :], rows(A["x"], 0)).then_inc(x_in, 16)

                def store(i):
                    sp.wait_ge(xnT_done, i + 1)
                    sp.dma_start(W["xnT"][:, :, bass.ds(i * GN, GN)], xnT[:, :, :]).then_inc(xT_stored, 16)
                    sp.wait_ge(xmT_done, 2 * i + 2)
                    sp.dma_start(W["xmT"][:, :, bass.ds(i * GN, GN)], xmT[:, :, :]).then_inc(xT_stored, 16)
                    sp.wait_ge(proj_read, 4 * i + 4)
                    sp.dma_start(rows(W["k"], i), kv[:, :, 0:C]).then_inc(kv_stored, 16)
                    sp.dma_start(rows(W["v"], i), kv[:, :, C:2 * C]).then_inc(kv_stored, 16)
                    sp.wait_ge(vm_read, 4 * i + 4)
                    sp.wait_ge(km_done, 4 * i + 4)
                    sp.dma_start(rows(W["km"], i), kvm[:, :, :]).then_inc(kvm_stored, 16)

                with sp.Fori(0, NG - 1) as i:
                    sp.wait_ge(xn_done, 4 * i + 4)
                    sp.dma_start(xg[:, :, :], rows(A["x"], i + 1)).then_inc(x_in, 16)
                    store(i)
                store(NG - 1)
                sp.wait_ge(xT_stored, 32 * NG + 32)
                sp.wait_ge(kv_stored, 32 * NG + 32)
                sp.wait_ge(kvm_stored, 16 * NG + 16)

            @block.vector
            def _(v):
                v.memset(kmax[:, :], -BIG).then_inc(kmax_step, 1)
                v.memset(st1[:, 0, :], 0.0).then_inc(xn_turned, 1)
                v.memset(st2[:, 0, :], 0.0).then_inc(xm_turned, 1)
                v.memset(kv[:, 0, 0:1], 0.0).then_inc(kv_stored, 32)
                v.memset(kvm[:, 0, 0:1], 0.0).then_inc(kvm_stored, 16)
                v.wait_ge(w_in, 96)
                v.wait_ge(xn_turned, 1)
                v.wait_ge(xm_turned, 1)
                want1 = counter(v, "stats1_want", TPG)
                want2 = counter(v, "stats2_want", TPG)
                with v.Fori(0, NG) as i:
                    v.wait_ge(x_in, 16 * i + 16)
                    for j in range(TPG):
                        v.bn_stats(st1[:, j, :], xg[:, j, :]).then_inc(stats1, 1)
                    passed(v, stats1, want1, TPG)
                    for j in range(TPG):
                        v.bn_aggr(mv1[:, j, :], st1[:, j, :]).then_inc(aggr1, 1)
                    v.wait_ge(aggr1, TPG * i + TPG)
                    v.tensor_scalar(ve1[:, :], mv1[:, :, 1], EPS, None, ALU.add).then_inc(var1, 1)
                    v.wait_ge(std1, i + 1)
                    v.reciprocal(rs1[:, :], sd1[:, :]).then_inc(rstd1, 1)
                    v.wait_ge(rstd1, i + 1)
                    v.wait_ge(xn_turned, i + 1)
                    for j in range(TPG):
                        v.tensor_scalar(xn[:, j, :], xg[:, j, :], mv1[:, j, 0:1], rs1[:, j:j + 1],
                                        ALU.subtract, ALU.mult).then_inc(xn_done, 1)
                    for j in range(TPG):
                        v.wait_ge(xn_done, TPG * i + j + 1)
                        v.bn_stats(st2[:, j, :], xn[:, j, :]).then_inc(stats2, 1)
                    passed(v, stats2, want2, TPG)
                    for j in range(TPG):
                        v.bn_aggr(mv2[:, j, :], st2[:, j, :]).then_inc(aggr2, 1)
                    v.wait_ge(aggr2, TPG * i + TPG)
                    v.tensor_scalar(ve2[:, :], mv2[:, :, 1], EPS, None, ALU.add).then_inc(var2, 1)
                    v.wait_ge(std2, i + 1)
                    v.reciprocal(rs2[:, :], sd2[:, :]).then_inc(rstd2, 1)
                    v.wait_ge(rstd2, i + 1)
                    v.wait_ge(xm_turned, i + 1)
                    for j in range(TPG):
                        v.tensor_scalar(xm[:, j, :], xn[:, j, :], mv2[:, j, 0:1], rs2[:, j:j + 1],
                                        ALU.subtract, ALU.mult).then_inc(xm_done, 1)
                    v.wait_ge(kv_stored, 32 * i + 32)
                    v.wait_ge(kvm_stored, 16 * i + 16)
                    for j in range(TPG):
                        v.wait_ge(proj, TPG * i + j + 1)
                        v.tensor_tensor(q_sb[:, bass.ds(TPG * i + j, 1), :], pA[:, 0:C].unsqueeze(1),
                                        bq[:, :].unsqueeze(1), ALU.add)
                        v.tensor_scalar(kvm[:, j, 0:C], pA[:, C:2 * C], vmask[:, bass.ds(TPG * i + j, 1)], None,
                                        ALU.add).then_inc(km_done, 1)
                        v.tensor_tensor(kv[:, j, :], pB[:, :], bkv[:, :], ALU.add).then_inc(proj_read, 1)
                        v.wait_ge(km_done, TPG * i + j + 1)
                        v.wait_ge(kmax_step, TPG * i + j + 1)
                        v.tensor_tensor(kmax[:, :], kmax[:, :], kvm[:, j, 0:C], ALU.max).then_inc(kmax_step, 1)

            @block.scalar
            def _(a):
                a.wait_ge(w_in, 96)
                with a.Fori(0, NG) as i:
                    a.wait_ge(var1, i + 1)
                    a.activation(sd1[:, :], ve1[:, :], ACT.Sqrt).then_inc(std1, 1)
                    a.wait_ge(xn_turned, i + 2)
                    a.wait_ge(xT_stored, 32 * i + 32)
                    a.copy(xnT[:, :, :], pT[:, :, :]).then_inc(xnT_done, 1)
                    a.wait_ge(var2, i + 1)
                    a.activation(sd2[:, :], ve2[:, :], ACT.Sqrt).then_inc(std2, 1)
                    a.wait_ge(xm_turned, i + 2)
                    for k in range(KC):
                        a.activation(xmT[:, k, :], pM[:, k, :], ACT.Identity, bias=lnb[:, k:k + 1],
                                     scale=lng[:, k:k + 1]).then_inc(xmT_done, 1)
                    a.wait_ge(kvm_stored, 16 * i + 16)
                    for j in range(TPG):
                        a.wait_ge(proj, TPG * i + j + 1)
                        a.copy(kvm[:, j, C:2 * C], pC[:, :]).then_inc(vm_read, 1)

            @block.gpsimd
            def _(g):
                g.memset(xnT[:, 0, 0:1], 0.0).then_inc(xT_stored, 32)

            @block.tensor
            def _(pe):
                pe.wait_ge(w_in, 96)
                with pe.Fori(0, NG) as i:
                    pe.wait_ge(xn_done, TPG * i + TPG)
                    for j in range(TPG):
                        for k in range(KC):
                            t = pe.transpose(pT[:, k, j * P:(j + 1) * P], xn[:, j, k * P:(k + 1) * P], ident[:, :])
                    t.then_inc(xn_turned, 1)
                    pe.wait_ge(xm_done, TPG * i + TPG)
                    for j in range(TPG):
                        for k in range(KC):
                            t = pe.transpose(pM[:, k, j * P:(j + 1) * P], xm[:, j, k * P:(k + 1) * P], ident[:, :])
                    t.then_inc(xm_turned, 1)
                    pe.wait_ge(xnT_done, i + 1)
                    for j in range(TPG):
                        if j:
                            pe.wait_ge(proj_read, TPG * i + j)
                            pe.wait_ge(vm_read, TPG * i + j)
                        for dst, c0, c1 in ((pA, 0, 2 * C), (pB, 2 * C, 4 * C), (pC, 4 * C, 5 * C)):
                            for k in range(KC):
                                m = pe.matmul(dst[:, :], xnT[:, k, j * P:(j + 1) * P], wall[:, k, c0:c1],
                                              start=(k == 0), stop=(k == KC - 1))
                        m.then_inc(proj, 1)
                    pe.wait_ge(proj_read, TPG * i + TPG)
                    pe.wait_ge(vm_read, TPG * i + TPG)
                    pe.wait_ge(xmT_done, 2 * i + 2)


def mix_context(nc, A, W, sem, ident, kmax, ctxbd):
    with ExitStack() as cx:
        def sb(n, s, d=F32):
            return cx.enter_context(nc.sbuf_tensor("m_" + n, s, d))

        def ps(n, s, d=F32):
            return cx.enter_context(nc.psum_tensor("m_" + n, s, d))
        ones = sb("ones", [P, P])
        zero = sb("zero", [P, P])
        bd = sb("bd", [P, KC, C])
        kcol = sb("kcol", [P, KC])
        diag = sb("diag", [P, C])
        krow = sb("krow", [P, C])
        km = sb("km", [P, TPG, 2 * C + 1])
        e = sb("e", [P, TPG, C])
        rsum = sb("rsum", [P, KC])
        pk = ps("pk", [P, C])
        prow = ps("prow", [P, C])
        pctx = ps("pctx", [P, KC, 512])
        bd_in = sem("m_bd_in")
        filled = sem("m_filled")
        turned = sem("m_turned")
        colmax = sem("m_colmax")
        diag_done = sem("m_diag")
        row_ps = sem("m_row_ps")
        row_done = sem("m_row")
        km_in = sem("m_km_in")
        sub_done = sem("m_sub")
        e_done = sem("m_e")
        ctx_step = sem("m_ctx_step")
        rs_done = sem("m_rs")
        bd_done = sem("m_bd_done")
        with nc.Block() as block:
            @block.sync
            def _(sp):
                sp.dma_start(bd[:, :, :], A["bdmask"]).then_inc(bd_in, 16)
                sp.dma_start(km[:, :, 0:2 * C], rows(W["km"], 0)).then_inc(km_in, 16)
                with sp.Fori(0, NG - 1) as i:
                    sp.wait_ge(ctx_step, i + 1)
                    sp.dma_start(km[:, :, 0:2 * C], rows(W["km"], i + 1)).then_inc(km_in, 16)

            @block.gpsimd
            def _(g):
                g.memset(ones[:, :], 1.0).then_inc(filled, 1)
                g.memset(zero[:, :], 0.0).then_inc(filled, 1)
                g.memset(km[:, :, 2 * C:2 * C + 1], 1.0).then_inc(filled, 1)

            @block.vector
            def _(v):
                v.wait_ge(turned, 1)
                v.tensor_reduce(kcol[:, :], pk[:, :].rearrange("p (k n) -> p k n", k=KC), AX, ALU.max).then_inc(colmax, 1)
                v.wait_ge(colmax, 1)
                for k in range(KC):
                    v.tensor_scalar(diag[:, k * P:(k + 1) * P], ident[:, :], kcol[:, k:k + 1], None,
                                    ALU.mult).then_inc(diag_done, 1)
                v.wait_ge(row_ps, 1)
                v.tensor_copy(krow[:, :], prow[:, :]).then_inc(row_done, 1)
                v.wait_ge(row_done, 1)
                with v.Fori(0, NG) as i:
                    v.wait_ge(km_in, 16 * i + 16)
                    v.tensor_tensor(e[:, :, :], km[:, :, 0:C], bc(krow[:, :].unsqueeze(1), [P, TPG, C]),
                                    ALU.subtract).then_inc(sub_done, 1)
                v.wait_ge(ctx_step, NG + 1)
                v.reciprocal(rsum[:, :], pctx[:, :, C]).then_inc(rs_done, 1)
                v.wait_ge(rs_done, 1)
                v.wait_ge(bd_in, 16)
                for k in range(KC):
                    v.scalar_tensor_tensor(out=ctxbd[:, k, :], in0=pctx[:, k, 0:C], scalar=rsum[:, k:k + 1],
                                           in1=bd[:, k, :], op0=ALU.mult, op1=ALU.mult).then_inc(bd_done, 1)

            @block.scalar
            def _(a):
                with a.Fori(0, NG) as i:
                    a.wait_ge(sub_done, i + 1)
                    a.activation(e[:, :, :], e[:, :, :], ACT.Exp).then_inc(e_done, 1)

            @block.tensor
            def _(pe):
                for k in range(KC):
                    t = pe.transpose(pk[:, k * P:(k + 1) * P], kmax[:, k * P:(k + 1) * P], ident[:, :])
                t.then_inc(turned, 1)
                pe.wait_ge(filled, 3)
                pe.wait_ge(diag_done, KC)
                pe.matmul(prow[:, :], ones[:, :], diag[:, :], start=True, stop=True).then_inc(row_ps, 1)
                for k in range(KC):
                    pe.matmul(pctx[:, k, 0:P], zero[:, :], zero[:, :], start=True, stop=False, skip_group_check=True)
                    pe.matmul(pctx[:, k, P:2 * P], zero[:, :], zero[:, :], start=False, stop=False, skip_group_check=True)
                    pe.matmul(pctx[:, k, 2 * P:2 * P + 1], zero[:, :], zero[:, 0:1], start=False, stop=False,
                              skip_group_check=True)
                with pe.Fori(0, NG) as i:
                    pe.wait_ge(e_done, i + 1)
                    for j in range(TPG):
                        for k in range(KC):
                            m = pe.matmul(pctx[:, k, 0:C + 1], e[:, j, k * P:(k + 1) * P], km[:, j, C:2 * C + 1],
                                          start=False, stop=False, skip_group_check=True)
                    m.then_inc(ctx_step, 1)
                for k in range(KC):
                    m = pe.matmul(pctx[:, k, 0:1], zero[:, :], zero[:, 0:1], start=False, stop=True,
                                  skip_group_check=True)
                m.then_inc(ctx_step, 1)


def histogram(nc, A, W, sem, ident, rc, lo, hi, pos_base):
    with ExitStack() as cx:
        def sb(n, s, d=F32):
            return cx.enter_context(nc.sbuf_tensor("h_" + n, s, d))

        def ps(n, s, d=F32):
            return cx.enter_context(nc.psum_tensor("h_" + n, s, d))
        ei = sb("ei", [EL, 2, ET], I32)
        ti = sb("ti", [EL, 2, ET], I32)
        iota = sb("iota", [P, P])
        triu = sb("triu", [P, P])
        jt = sb("jt", [P, STM // P])
        ones = sb("ones", [P, P])
        zero = sb("zero", [P, P])
        fill = sb("fill", [P, ST, 2], I32)
        ohlo = sb("ohlo", [EL, SB_, P], BF16)
        ohhi = sb("ohhi", [EL, SB_, NT], BF16)
        cnt = sb("cnt", [P, NT])
        tot = sb("tot", [P, NT], I32)
        tot2 = sb("tot2", [P, NT], I32)
        tot3 = sb("tot3", [P, NT], I32)
        tiles = sb("tiles", [P, NT])
        incl = sb("incl", [P, NT])
        excl = sb("excl", [P, NT])
        cmp = sb("cmp", [P, STM // P, NT])
        tmf = sb("tmf", [P, STM // P])
        tmi = sb("tmi", [P, STM // P], I32)
        pcnt = ps("pcnt", [P, NT])
        ptot = ps("ptot", [P, NT])
        pbef = ps("pbef", [P, NT])
        e_in = sem("h_e_in")
        c_in = sem("h_c_in")
        fill_done = sem("h_fill")
        fill_out = sem("h_fill_out")
        filled = sem("h_filled")
        bits = sem("h_bits")
        fields = sem("h_fields")
        oh = sem("h_onehots")
        counted = sem("h_counted")
        cnt_done = sem("h_cnt")
        tot_ps = sem("h_tot_ps")
        tot_done = sem("h_tot")
        tiles_done = sem("h_tiles")
        incl_done = sem("h_incl")
        excl_done = sem("h_excl")
        base_done = sem("h_base")
        cmp_done = sem("h_cmp")
        tmf_done = sem("h_tmf")
        tmf2_done = sem("h_tmf2")
        tmi_done = sem("h_tmi")
        tm_out = sem("h_tm_out")
        with nc.Block() as block:
            @block.sync
            def _(sp):
                sp.dma_start(ei[:, 0, :], A["src"].rearrange("(p t) -> p t", p=EL)).then_inc(e_in, 16)
                sp.dma_start(ei[:, 1, :], A["dst"].rearrange("(p t) -> p t", p=EL)).then_inc(e_in, 16)
                for d, n in ((iota, "iota"), (triu, "triu"), (jt, "jtile")):
                    sp.dma_start(d[:, :], A[n]).then_inc(c_in, 16)
                sp.wait_ge(fill_done, 2)
                sp.dma_start(W["sorted"].rearrange("(p t) k -> p t k", p=P), fill[:, :, :]).then_inc(fill_out, 16)
                sp.wait_ge(tmi_done, 1)
                sp.dma_start(W["tmap"].rearrange("a (p c) -> p (a c)", p=P), tmi[:, :]).then_inc(tm_out, 16)
                sp.wait_ge(fill_out, 16)
                sp.wait_ge(tm_out, 16)

            @block.gpsimd
            def _(g):
                g.memset(ones[:, :], 1.0).then_inc(filled, 1)
                g.memset(zero[:, :], 0.0).then_inc(filled, 1)
                g.memset(fill[:, :, 0], ROWPAD).then_inc(fill_done, 1)
                g.memset(fill[:, :, 1], 0).then_inc(fill_done, 1)

            @block.vector
            def _(v):
                v.wait_ge(e_in, 32)
                v.wait_ge(c_in, 48)
                v.tensor_scalar(ti[:, 0, :], ei[:, 0, :], P - 1, None, ALU.bitwise_and).then_inc(bits, 1)
                v.tensor_scalar(ti[:, 1, :], ei[:, 0, :], 7, None, ALU.logical_shift_right).then_inc(bits, 1)
                v.tensor_copy(rc[:, :, :], ei[:, :, :].rearrange("p k t -> p t k")).then_inc(fields, 1)
                v.wait_ge(bits, 2)
                v.tensor_copy(lo[:, :], ti[:, 0, :]).then_inc(fields, 1)
                v.tensor_copy(hi[:, :], ti[:, 1, :]).then_inc(fields, 1)
                v.wait_ge(fields, 3)
                v.memset(ohlo[:, 0, 0:1], 0.0).then_inc(counted, 1)
                with v.Fori(0, ET // SB_) as i:
                    v.wait_ge(counted, i + 1)
                    v.tensor_tensor(ohlo[:, :, :], bc(iota[0:EL, :].unsqueeze(1), [EL, SB_, P]),
                                    bc(lo[:, bass.ds(i * SB_, SB_)].unsqueeze(2), [EL, SB_, P]),
                                    ALU.is_equal).then_inc(oh, 1)
                    v.tensor_tensor(ohhi[:, :, :], bc(iota[0:EL, 0:NT].unsqueeze(1), [EL, SB_, NT]),
                                    bc(hi[:, bass.ds(i * SB_, SB_)].unsqueeze(2), [EL, SB_, NT]),
                                    ALU.is_equal).then_inc(oh, 1)
                v.wait_ge(counted, ET // SB_ + 2)
                v.tensor_copy(cnt[:, :], pcnt[:, :]).then_inc(cnt_done, 1)
                v.wait_ge(tot_ps, 2)
                v.tensor_copy(tot[:, :], ptot[:, :]).then_inc(tot_done, 1)
                v.wait_ge(tot_done, 1)
                v.tensor_scalar(tot2[:, :], tot[:, :], P - 1, None, ALU.add).then_inc(tot_done, 1)
                v.wait_ge(tot_done, 2)
                v.tensor_scalar(tot3[:, :], tot2[:, :], 7, None, ALU.logical_shift_right).then_inc(tot_done, 1)
                v.wait_ge(tot_done, 3)
                v.tensor_copy(tiles[:, :], tot3[:, :]).then_inc(tiles_done, 1)
                v.wait_ge(tiles_done, 1)
                v.wait_ge(filled, 2)
                v.tensor_tensor_scan(incl[:, :], zero[:, 0:NT], tiles[:, :], 0.0, ALU.add, ALU.add).then_inc(incl_done, 1)
                v.wait_ge(incl_done, 1)
                v.tensor_tensor(excl[:, :], incl[:, :], tiles[:, :], ALU.subtract).then_inc(excl_done, 1)
                v.wait_ge(excl_done, 1)
                v.scalar_tensor_tensor(out=pos_base[:, :], in0=excl[:, :], scalar=float(P), in1=pbef[:, :],
                                       op0=ALU.mult, op1=ALU.add).then_inc(base_done, 1)
                sh = [P, STM // P, NT]
                v.tensor_tensor(cmp[:, :, :], bc(incl[:, :].unsqueeze(1), sh), bc(jt[:, :].unsqueeze(2), sh),
                                ALU.is_le).then_inc(cmp_done, 1)
                v.wait_ge(cmp_done, 1)
                v.tensor_reduce(tmf[:, :], cmp[:, :, :], AX, ALU.add).then_inc(tmf_done, 1)
                v.wait_ge(tmf_done, 1)
                v.tensor_scalar(tmf[:, :], tmf[:, :], float(NT - 1), None, ALU.min).then_inc(tmf2_done, 1)
                v.wait_ge(tmf2_done, 1)
                v.tensor_copy(tmi[:, :], tmf[:, :]).then_inc(tmi_done, 1)

            @block.tensor
            def _(pe):
                pe.wait_ge(filled, 2)
                pe.matmul(pcnt[:, :], zero[:, :], zero[:, 0:NT], start=True, stop=False, skip_group_check=True)
                with pe.Fori(0, ET // SB_) as i:
                    pe.wait_ge(oh, 2 * i + 2)
                    for s in range(SB_):
                        m = pe.matmul(pcnt[:, :], ohlo[:, s, :], ohhi[:, s, :], start=False, stop=False,
                                      skip_group_check=True)
                    m.then_inc(counted, 1)
                pe.matmul(pcnt[:, 0:1], zero[:, :], zero[:, 0:1], start=False, stop=True,
                          skip_group_check=True).then_inc(counted, 1)
                pe.wait_ge(cnt_done, 1)
                pe.matmul(ptot[:, :], ones[:, :], cnt[:, :], start=True, stop=True).then_inc(tot_ps, 1)
                pe.matmul(pbef[:, :], triu[:, :], cnt[:, :], start=True, stop=True).then_inc(tot_ps, 1)


def sort_edges(nc, A, W, sem, ident, rc, lo, hi, pos_base):
    with ExitStack() as cx:
        def sb(n, s, d=F32):
            return cx.enter_context(nc.sbuf_tensor("s_" + n, s, d))

        def ps(n, s, d=F32):
            return cx.enter_context(nc.psum_tensor("s_" + n, s, d))
        iota = sb("iota", [P, P])
        triu = sb("triu", [P, P])
        idb = sb("idb", [P, P], BF16)
        ohlo = sb("ohlo", [EL, SB_, P], BF16)
        ohhi = sb("ohhi", [EL, SB_, NT], BF16)
        oht = sb("oht", [P, SB_, EL], BF16)
        ohtf = sb("ohtf", [P, SB_, EL])
        before = sb("before", [EL, SB_, EL], BF16)
        seen = sb("seen", [P, SB_, NT])
        picked = sb("picked", [EL, SB_, NT])
        posf = sb("posf", [EL, SB_])
        posi = sb("posi", [EL, SB_], I32)
        rcs = sb("rcs", [EL, SB_, 2], I32)
        pseen = ps("pseen", [P, NT])
        pt = ps("pt", [P, SB_, P], BF16)
        plo = ps("plo", [P, SB_, P])
        prank = ps("prank", [P, SB_, NT])
        c_in = sem("s_c_in")
        idb_done = sem("s_idb")
        seeded = sem("s_seeded")
        oh = sem("s_onehots")
        turned = sem("s_turned")
        oht_done = sem("s_oht")
        lo_ps = sem("s_lo_ps")
        bef_done = sem("s_before")
        snap = sem("s_snap")
        step = sem("s_step")
        rank = sem("s_rank")
        pick = sem("s_pick")
        pos = sem("s_pos")
        staged = sem("s_staged")
        landed = sem("s_landed")
        NB = ET // SB_
        with nc.Block() as block:
            @block.sync
            def _(sp):
                sp.dma_start(iota[:, :], A["iota"]).then_inc(c_in, 16)
                sp.dma_start(triu[:, :], A["triu"]).then_inc(c_in, 16)
                sp.wait_ge(landed, 16 * SB_ * NB)

            @block.vector
            def _(v):
                v.wait_ge(c_in, 32)
                v.tensor_copy(idb[:, :], ident[:, :]).then_inc(idb_done, 1)
                v.memset(posf[:, 0:1], 0.0).then_inc(pos, 1)

                def batch(i, first):
                    v.wait_ge(pos, i + 1)
                    v.tensor_tensor(ohlo[:, :, :], bc(iota[0:EL, :].unsqueeze(1), [EL, SB_, P]),
                                    bc(lo[:, bass.ds(i * SB_, SB_)].unsqueeze(2), [EL, SB_, P]),
                                    ALU.is_equal).then_inc(oh, 1)
                    v.tensor_tensor(ohhi[:, :, :], bc(iota[0:EL, 0:NT].unsqueeze(1), [EL, SB_, NT]),
                                    bc(hi[:, bass.ds(i * SB_, SB_)].unsqueeze(2), [EL, SB_, NT]),
                                    ALU.is_equal).then_inc(oh, 1)
                    v.wait_ge(lo_ps, i + 1)
                    v.tensor_tensor(before[:, :, :], plo[0:EL, :, 0:EL], bc(triu[0:EL, 0:EL].unsqueeze(1), [EL, SB_, EL]),
                                    ALU.mult).then_inc(bef_done, 1)
                    v.wait_ge(rank, i + 1)
                    v.wait_ge(oh, 2 * i + 2)
                    v.tensor_tensor(picked[:, :, :], prank[0:EL, :, :], ohhi[:, :, :], ALU.mult).then_inc(pick, 1)
                    v.wait_ge(pick, i + 1)
                    v.tensor_reduce(posf[:, :], picked[:, :, :], AX, ALU.add).then_inc(pos, 1)
                    v.wait_ge(pos, i + 2)
                    if not first:
                        v.wait_ge(landed, 16 * SB_ * i)
                    v.tensor_copy(posi[:, :], posf[:, :]).then_inc(staged, 1)
                    v.tensor_copy(rcs[:, :, :], rc[:, bass.ds(i * SB_, SB_), :]).then_inc(staged, 1)

                batch(0, True)
                with v.Fori(1, NB) as i:
                    batch(i, False)

            @block.scalar
            def _(a):
                with a.Fori(0, NB) as i:
                    a.wait_ge(turned, i + 1)
                    a.copy(oht[:, :, :], pt[:, :, 0:EL]).then_inc(oht_done, 1)
                    for s in range(SB_):
                        a.wait_ge(step, i * SB_ + s + 1)
                        a.copy(seen[:, s, :], pseen[:, :]).then_inc(snap, 1)
                        if s == 0:
                            a.copy(ohtf[:, :, :], pt[:, :, 0:EL]).then_inc(oht_done, 1)

            @block.gpsimd
            def _(g):
                want = counter(g, "staged_want", 2)
                with g.Fori(0, NB) as i:
                    passed(g, staged, want, 2)
                    for s in range(SB_):
                        g.indirect_dma_start(W["sorted"], bass.IndirectOffsetOnAxis(ap=posi[:, s:s + 1], axis=0),
                                             rcs[:, s, :], None).then_inc(landed, 16)

            @block.tensor
            def _(pe):
                pe.wait_ge(idb_done, 1)
                pe.matmul(pseen[:, :], ident[:, :], pos_base[:, :], start=True, stop=False,
                          skip_group_check=True).then_inc(step, 1)
                with pe.Fori(0, NB) as i:
                    pe.wait_ge(oh, 2 * i + 2)
                    for s in range(SB_):
                        t = pe.transpose(pt[:, s, 0:EL], ohlo[:, s, :], idb[0:EL, 0:EL])
                    t.then_inc(turned, 1)
                    pe.wait_ge(oht_done, 2 * i + 1)
                    for s in range(SB_):
                        m = pe.matmul(plo[0:EL, s, 0:EL], oht[:, s, :], oht[:, s, :], start=True, stop=True)
                    m.then_inc(lo_ps, 1)
                    for s in range(SB_):
                        pe.wait_ge(snap, i * SB_ + s + 1)
                        pe.matmul(pseen[:, :], ohlo[:, s, :], ohhi[:, s, :], start=False, stop=False,
                                  skip_group_check=True).then_inc(step, 1)
                    pe.wait_ge(oht_done, 2 * i + 2)
                    for s in range(SB_):
                        pe.matmul(prank[0:EL, s, :], ohtf[:, s, :], seen[:, s, :], start=(s == 0), stop=False,
                                  skip_group_check=True)
                    pe.wait_ge(bef_done, i + 1)
                    for s in range(SB_):
                        m = pe.matmul(prank[0:EL, s, :], before[:, s, :], ohhi[:, s, :], start=False,
                                      stop=(s == SB_ - 1), skip_group_check=True)
                    m.then_inc(rank, 1)


def load_sorted(nc, A, W, sem, ident, rowf, rowl, coli, tmap):
    LP = ST // 8
    with ExitStack() as cx:
        def sb(n, s, d=F32):
            return cx.enter_context(nc.sbuf_tensor("l_" + n, s, d))

        def ps(n, s, d=F32):
            return cx.enter_context(nc.psum_tensor("l_" + n, s, d))
        li = sb("li", [LP, 8, 2 * P], I32)
        lf = sb("lf", [LP, 2, 8, P])
        ri = sb("ri", [P, ST], I32)
        rl = sb("rl", [P, ST], I32)
        far = sb("far", [P, ST])
        rm = sb("rm", [P, ST])
        pr = ps("pr", [P, 8, P])
        pc = ps("pc", [P, 8, P])
        s_in = sem("l_in")
        lf_done = sem("l_lf")
        turned = sem("l_turned")
        ri_done = sem("l_ri")
        rl_done = sem("l_rl")
        rm_done = sem("l_rm")
        far_done = sem("l_far")
        end = sem("l_end")
        with nc.Block() as block:
            @block.sync
            def _(sp):
                sp.dma_start(li[:, :, :], W["sorted"].rearrange("(c p e) k -> p c (e k)", c=8, p=LP)).then_inc(s_in, 16)
                sp.dma_start(tmap[:, :], W["tmap"]).then_inc(s_in, 16)
                sp.wait_ge(s_in, 32)

            @block.vector
            def _(v):
                v.wait_ge(s_in, 32)
                for k in range(2):
                    v.tensor_copy(lf[:, k, :, :], li[:, :, :].rearrange("p c (e k) -> p c e k", k=2)[:, :, :, k]).then_inc(lf_done, 1)
                v.wait_ge(turned, 1)
                v.tensor_copy(rowf[:, :].rearrange("p (c n) -> p c n", c=8), pr[:, :, 0:LP]).then_inc(ri_done, 1)
                v.tensor_copy(ri[:, :].rearrange("p (c n) -> p c n", c=8), pr[:, :, 0:LP]).then_inc(ri_done, 1)
                v.tensor_copy(coli[:, 0:ST].rearrange("p (c n) -> p c n", c=8), pc[:, :, 0:LP]).then_inc(end, 1)
                v.memset(coli[:, ST:STX], 0).then_inc(end, 1)
                v.memset(rowl[:, ST:STX], 0.0).then_inc(end, 1)
                v.wait_ge(ri_done, 2)
                v.tensor_scalar(rl[:, :], ri[:, :], P - 1, None, ALU.bitwise_and).then_inc(rl_done, 1)
                v.tensor_scalar(far[:, :], rowf[:, :], float(N), 1000.0, ALU.is_ge, ALU.mult).then_inc(far_done, 1)
                v.wait_ge(rl_done, 1)
                v.tensor_copy(rm[:, :], rl[:, :]).then_inc(rm_done, 1)
                v.wait_ge(rm_done, 1)
                v.wait_ge(far_done, 1)
                v.tensor_tensor(rowl[:, 0:ST], rm[:, :], far[:, :], ALU.add).then_inc(end, 1)

            @block.tensor
            def _(pe):
                pe.wait_ge(lf_done, 2)
                for k, dst in ((0, pr), (1, pc)):
                    for c in range(8):
                        t = pe.transpose(dst[:, c, 0:LP], lf[:, k, c, :], ident[0:LP, 0:LP])
                t.then_inc(turned, 1)


def edge_scores(nc, A, W, sem, rowl, coli, tmap, q_sb, score):
    with ExitStack() as cx:
        def sb(n, s, d=F32):
            return cx.enter_context(nc.sbuf_tensor("e_" + n, s, d))

        def ps(n, s, d=F32):
            return cx.enter_context(nc.psum_tensor("e_" + n, s, d))
        iota = sb("iota", [P, P])
        idb = sb("idb", [P, P], BF16)
        oh = sb("oh", [P, 2, HB, P], BF16)
        oht = sb("oht", [P, 2, HB, P])
        kb = sb("kb", [P, 2, HB, C])
        prod = sb("prod", [P, HB, C])
        idx = sb("idx", [P, 2, HB], I32)
        pt = ps("pt", [P, 2, HB, P], BF16)
        pq = ps("pq", [P, 2, HB, C])
        c_in = sem("e_c_in")
        idb_done = sem("e_idb")
        ohs = sem("e_onehots")
        turned = sem("e_turned")
        oht_done = sem("e_oht")
        q_picked = sem("e_q_picked")
        k_in = [sem(f"e_k_in{x}") for x in range(2)]
        prod_done = sem("e_prod")
        score_done = sem("e_score")
        staged = sem("e_staged")
        with nc.Block() as block:
            @block.sync
            def _(sp):
                sp.dma_start(iota[:, :], A["iota"]).then_inc(c_in, 16)
                sp.dma_start(prod[:, 0, 0:P], A["ident"]).then_inc(c_in, 16)

            @block.gpsimd
            def _(g):
                want = counter(g, "e_staged_want", 1)
                with g.Fori(0, NHB // 2) as i:
                    for x in range(2):
                        passed(g, staged, want, 1)
                        for s in range(HB):
                            g.indirect_dma_start(kb[:, x, s, :], None, W["k"],
                                                 bass.IndirectOffsetOnAxis(ap=idx[:, x, s:s + 1], axis=0))\
                             .then_inc(k_in[x], 16)

            @block.vector
            def _(v):
                sh = [P, HB, P]

                def onehot(hb, x):
                    v.tensor_tensor(oh[:, x, :, :], bc(iota[:, :].unsqueeze(1), sh),
                                    bc(rowl[:, bass.ds(hb * HB, HB)].unsqueeze(2), sh), ALU.is_equal).then_inc(ohs, 1)

                def stage(hb, x):
                    v.tensor_copy(idx[:, x, :], coli[:, bass.ds(hb * HB, HB)]).then_inc(staged, 1)

                for x in range(2):
                    stage(x, x)
                v.wait_ge(c_in, 32)
                v.tensor_copy(idb[:, :], prod[:, 0, 0:P]).then_inc(idb_done, 1)
                onehot(0, 0)
                v.wait_ge(idb_done, 1)

                def pair(i, first):
                    for x in range(2):
                        hb = 2 * i + x
                        if not (first and x == 0):
                            v.wait_ge(turned, hb)
                            v.wait_ge(score_done, hb)
                        onehot(hb + 1, 1 - x)
                        v.wait_ge(q_picked, hb + 1)
                        v.wait_ge(k_in[x], 16 * HB * i + 16 * HB)
                        v.tensor_tensor(prod[:, :, :], pq[:, x, :, :], kb[:, x, :, :], ALU.mult).then_inc(prod_done, 1)
                        v.wait_ge(prod_done, hb + 1)
                        v.tensor_reduce(score[:, bass.ds(hb * HB, HB), :],
                                        prod[:, :, :].rearrange("p s (d h) -> p s h d", h=H), AX, ALU.add)\
                         .then_inc(score_done, 1)
                        stage(hb + 2, x)

                pair(0, True)
                with v.Fori(1, NHB // 2) as i:
                    pair(i, False)

            @block.scalar
            def _(a):
                with a.Fori(0, NHB // 2) as i:
                    for x in range(2):
                        a.wait_ge(turned, 2 * i + x + 1)
                        a.copy(oht[:, x, :, :], pt[:, x, :, :]).then_inc(oht_done, 1)

            @block.tensor
            def _(pe):
                pe.wait_ge(idb_done, 1)

                def pair(i, first):
                    for x in range(2):
                        hb = 2 * i + x
                        pe.wait_ge(ohs, hb + 1)
                        for s in range(HB):
                            t = pe.transpose(pt[:, x, s, :], oh[:, x, s, :], idb[:, :])
                        t.then_inc(turned, 1)
                        pe.wait_ge(oht_done, hb + 1)
                        if not first:
                            pe.wait_ge(prod_done, hb - 1)
                        for s in range(HB):
                            tile = pe.value_load(tmap[0:1, bass.ds(hb * HB + s, 1)], min_val=0, max_val=NT - 1)
                            m = pe.matmul(pq[:, x, s, :], oht[:, x, s, :], q_sb[:, bass.ds(tile, 1), :],
                                          start=True, stop=True)
                        m.then_inc(q_picked, 1)

                pair(0, True)
                with pe.Fori(1, NHB // 2) as i:
                    pair(i, False)


def softmax_edges(nc, A, W, sem, ident, rowf, score):
    L = GPC * P
    G = 5
    with ExitStack() as cx:
        def sb(n, s, d=F32):
            return cx.enter_context(nc.sbuf_tensor("x_" + n, s, d))

        def ps(n, s, d=F32):
            return cx.enter_context(nc.psum_tensor("x_" + n, s, d))
        sT = sb("sT", [P, L])
        rT = sb("rT", [P, L])
        cut = sb("cut", [P, L + 1])
        fwd = sb("fwd", [P, L])
        both = rT
        st_s = sb("st_s", [P, G, CH, H])
        st_r = sb("st_r", [P, G, CH, H])
        pack = sb("pack", [P, 2, 3])
        ch = sb("ch", [H, 2, CH, 3])
        one = sb("one", [H, 2, CH])
        link = sb("link", [H, 2, CH])
        join = sb("join", [H, 2, CH])
        gate = sb("gate", [H, 2, CH])
        lnk = sb("lnk", [H, 2, CH])
        state = sb("state", [H, 2, CH])
        car = sb("car", [H, 2, CH])
        carry = sb("carry", [P, 2])
        p_s = ps("p_s", [P, G + 3, P])
        p_r = ps("p_r", [P, G + 3, P])
        rows_staged = sem("x_rows_staged")
        s_staged = sem("x_s_staged")
        turned = sem("x_turned")
        sT_done = sem("x_sT")
        rT_done = sem("x_rT")
        cut_done = sem("x_cut")
        fwd_done = sem("x_fwd")
        both_done = sem("x_both")
        packed = sem("x_packed")
        ends_out = sem("x_ends_out")
        ends_in = sem("x_ends_in")
        chain = sem("x_chain")
        carry_out = sem("x_carry_out")
        carry_in = sem("x_carry_in")
        diff = sem("x_diff")
        exp_done = sem("x_exp")
        staged2 = sem("x_staged2")
        turned2 = sem("x_turned2")
        back = sem("x_back")
        s_view = score[:, :, :].rearrange("p (c g) h -> p g c h", c=CH)
        r_view = rowf[:, :].rearrange("p (c g) -> p g c", c=CH)
        with nc.Block() as block:
            @block.sync
            def _(sp):
                for w in range(2):
                    sp.wait_ge(packed, 5 + w)
                    sp.dma_start(W["ends"][w], pack[:, w, :]).then_inc(ends_out, 16)
                    sp.wait_ge(ends_out, 16 * w + 16)
                    sp.dma_start(ch[:, w, :, :], W["ends"][w].rearrange("(c h) k -> h c k", h=H)).then_inc(ends_in, 16)
                    sp.wait_ge(chain, (w + 1) * CHAIN)
                    sp.dma_start(W["carry"][w].rearrange("c h -> h c"), car[:, w, :], allow_slow_non_contiguous=True).then_inc(carry_out, 16)
                    sp.wait_ge(carry_out, 16 * w + 16)
                    sp.dma_start(carry[:, w:w + 1], W["carry"][w].rearrange("c (h o) -> (c h) o", o=1)).then_inc(carry_in, 16)
                sp.wait_ge(carry_in, 32)

            @block.vector
            def _(v):
                shr = [P, G, CH, H]
                v.memset(st_r[:, 0, 0, :], 0.0).then_inc(turned, 1)
                v.wait_ge(turned, 1)
                with v.Fori(0, GPC // G) as i:
                    v.wait_ge(turned, i + 1)
                    v.tensor_copy(st_r[:, :, :, :], bc(r_view[:, bass.ds(i * G, G), :].unsqueeze(3), shr)).then_inc(rows_staged, 1)
                    v.wait_ge(turned, i + 2)
                    v.tensor_copy(rT[:, bass.ds(i * G * P, G * P)].rearrange("p (g e) -> p g e", g=G),
                                  p_r[:, 0:G, :]).then_inc(rT_done, 1)
                v.memset(cut[:, 0:1], 0.0).then_inc(cut_done, 1)
                v.memset(cut[:, L:L + 1], 0.0).then_inc(cut_done, 1)
                v.wait_ge(rT_done, GPC // G)
                v.tensor_tensor(cut[:, 1:L], rT[:, 1:L], rT[:, 0:L - 1], ALU.not_equal).then_inc(cut_done, 1)
                v.wait_ge(cut_done, 3)
                v.tensor_scalar(cut[:, 1:L], cut[:, 1:L], -BIG, None, ALU.mult).then_inc(cut_done, 1)
                for w in range(2):
                    v.tensor_copy(pack[:, w, 1:2], rT[:, 0:1]).then_inc(packed, 1)
                    v.tensor_copy(pack[:, w, 2:3], rT[:, L - 1:L]).then_inc(packed, 1)
                v.wait_ge(cut_done, 4)
                v.wait_ge(sT_done, GPC // G)

                def carries(w):
                    n = [w * CHAIN]

                    def then(ins):
                        n[0] += 1
                        ins.then_inc(chain, 1)
                        v.wait_ge(chain, n[0])
                    v.wait_ge(ends_in, 16 * w + 16)
                    then(v.tensor_tensor(one[:, w, :], ch[:, w, :, 1], ch[:, w, :, 2], ALU.is_equal))
                    then(v.memset(link[:, w, 0:1], 0.0))
                    then(v.tensor_tensor(link[:, w, 1:CH], ch[:, w, 1:CH, 1], ch[:, w, 0:CH - 1, 2], ALU.is_equal))
                    then(v.tensor_scalar(lnk[:, w, :], link[:, w, :], -1.0, BIG, ALU.add, ALU.mult))
                    then(v.memset(join[:, w, :], 0.0))
                    if w == 0:
                        then(v.tensor_tensor(join[:, w, :], one[:, w, :], link[:, w, :], ALU.mult))
                    else:
                        then(v.tensor_tensor(join[:, w, 0:CH - 1], one[:, w, 0:CH - 1], link[:, w, 1:CH], ALU.mult))
                    then(v.tensor_scalar(gate[:, w, :], join[:, w, :], -1.0, BIG, ALU.add, ALU.mult))
                    then(v.memset(car[:, w, :], -BIG))
                    if w == 0:
                        then(v.tensor_tensor_scan(state[:, w, :], gate[:, w, :], ch[:, w, :, 0], -BIG, ALU.add, ALU.max))
                        then(v.tensor_tensor(car[:, w, 1:CH], state[:, w, 0:CH - 1], lnk[:, w, 1:CH], ALU.add))
                    else:
                        then(v.tensor_tensor_scan(state[:, w, ::-1], gate[:, w, ::-1], ch[:, w, ::-1, 0], -BIG,
                                                  ALU.add, ALU.max))
                        then(v.tensor_tensor(car[:, w, 0:CH - 1], state[:, w, 1:CH], lnk[:, w, 1:CH], ALU.add))
                    assert n[0] == (w + 1) * CHAIN
                    v.wait_ge(carry_in, 16 * w + 16)

                v.tensor_tensor_scan(fwd[:, :], cut[:, 0:L], sT[:, :], -BIG, ALU.add, ALU.max).then_inc(fwd_done, 1)
                v.wait_ge(fwd_done, 1)
                v.tensor_copy(pack[:, 0, 0:1], fwd[:, L - 1:L]).then_inc(packed, 1)
                v.wait_ge(packed, 5)
                carries(0)
                v.tensor_tensor_scan(fwd[:, :], cut[:, 0:L], sT[:, :], carry[:, 0:1], ALU.add, ALU.max).then_inc(fwd_done, 1)
                v.wait_ge(fwd_done, 2)
                v.tensor_tensor_scan(both[:, ::-1], cut[:, L:0:-1], fwd[:, ::-1], -BIG, ALU.add, ALU.max).then_inc(both_done, 1)
                v.wait_ge(both_done, 1)
                v.tensor_copy(pack[:, 1, 0:1], both[:, 0:1]).then_inc(packed, 1)
                v.wait_ge(packed, 6)
                carries(1)
                v.tensor_tensor_scan(both[:, ::-1], cut[:, L:0:-1], fwd[:, ::-1], carry[:, 1:2], ALU.add, ALU.max).then_inc(both_done, 1)
                v.wait_ge(both_done, 2)
                v.tensor_tensor(sT[:, :], sT[:, :], both[:, :], ALU.subtract).then_inc(diff, 1)
                with v.Fori(0, GPC // G) as i:
                    v.wait_ge(turned2, i + 1)
                    v.tensor_copy(s_view[:, bass.ds(i * G, G), :, :],
                                  p_s[:, 0:G, :].rearrange("p g (c h) -> p g c h", h=H)).then_inc(back, 1)

            @block.scalar
            def _(a):
                with a.Fori(0, GPC // G) as i:
                    a.wait_ge(turned, i + 1)
                    a.copy(st_s[:, :, :, :], s_view[:, bass.ds(i * G, G), :, :]).then_inc(s_staged, 1)
                    a.wait_ge(turned, i + 2)
                    a.copy(sT[:, bass.ds(i * G * P, G * P)].rearrange("p (g e) -> p g e", g=G),
                           p_s[:, 0:G, :]).then_inc(sT_done, 1)
                a.wait_ge(diff, 1)
                a.activation(fwd[:, :], sT[:, :], ACT.Exp, scale=SCALE).then_inc(exp_done, 1)
                a.wait_ge(exp_done, 1)
                a.copy(st_s[:, :, :, :].rearrange("p g c h -> p g (c h)"),
                       fwd[:, 0:G * P].rearrange("p (g e) -> p g e", g=G)).then_inc(staged2, 1)
                with a.Fori(0, GPC // G - 1) as i:
                    a.wait_ge(turned2, i + 1)
                    a.copy(st_s[:, :, :, :].rearrange("p g c h -> p g (c h)"),
                           fwd[:, bass.ds((i + 1) * G * P, G * P)].rearrange("p (g e) -> p g e", g=G)).then_inc(staged2, 1)

            @block.tensor
            def _(pe):
                with pe.Fori(0, GPC // G) as i:
                    pe.wait_ge(s_staged, i + 1)
                    pe.wait_ge(rows_staged, i + 1)
                    for g in range(G):
                        pe.transpose(p_s[:, g, :], st_s[:, g, :, :].rearrange("p c h -> p (c h)"), ident[:, :])
                        t = pe.transpose(p_r[:, g, :], st_r[:, g, :, :].rearrange("p c h -> p (c h)"), ident[:, :])
                    t.then_inc(turned, 1)
                    pe.wait_ge(sT_done, i + 1)
                    pe.wait_ge(rT_done, i + 1)
                with pe.Fori(0, GPC // G) as i:
                    pe.wait_ge(staged2, i + 1)
                    for g in range(G):
                        t = pe.transpose(p_s[:, g, :], st_s[:, g, :, :].rearrange("p c h -> p (c h)"), ident[:, :])
                    t.then_inc(turned2, 1)
                    pe.wait_ge(back, i + 1)


CHAIN = 10


def aggregate(nc, A, W, sem, rowl, coli, tmap, score, acc):
    with ExitStack() as cx:
        def sb(n, s, d=F32):
            return cx.enter_context(nc.sbuf_tensor("g_" + n, s, d))

        def ps(n, s, d=F32):
            return cx.enter_context(nc.psum_tensor("g_" + n, s, d))
        iota = sb("iota", [P, P])
        oh = sb("oh", [P, 2, HB, P])
        vb = sb("vb", [P, 2, HB, C])
        w = sb("w", [P, HB, C + H])
        idx = sb("idx", [P, 2, HB], I32)
        pa = ps("pa", [P, HB, 512])
        c_in = sem("g_c_in")
        zeroed = sem("g_zeroed")
        ohs = sem("g_onehots")
        v_in = [sem(f"g_v_in{x}") for x in range(2)]
        staged = sem("g_staged")
        weighted = sem("g_weighted")
        p_put = sem("g_p_put")
        summed = sem("g_summed")
        acc_done = sem("g_acc")
        with nc.Block() as block:
            @block.sync
            def _(sp):
                sp.dma_start(iota[:, :], A["iota"]).then_inc(c_in, 16)

            @block.gpsimd
            def _(g):
                want = counter(g, "g_staged_want", 1)
                with g.Fori(0, NHB // 2) as i:
                    for x in range(2):
                        passed(g, staged, want, 1)
                        for s in range(HB):
                            g.indirect_dma_start(vb[:, x, s, :], None, W["v"],
                                                 bass.IndirectOffsetOnAxis(ap=idx[:, x, s:s + 1], axis=0))\
                             .then_inc(v_in[x], 16)

            @block.scalar
            def _(a):
                with a.Fori(0, NHB) as i:
                    a.wait_ge(acc_done, HB * i + HB)
                    a.copy(w[:, :, C:C + H], score[:, bass.ds(i * HB, HB), :]).then_inc(p_put, 1)

            @block.vector
            def _(v):
                sh = [P, HB, P]
                shw = [P, HB, D, H]

                def onehot(hb, x):
                    v.tensor_tensor(oh[:, x, :, :], bc(iota[:, :].unsqueeze(1), sh),
                                    bc(rowl[:, bass.ds(hb * HB, HB)].unsqueeze(2), sh), ALU.is_equal).then_inc(ohs, 1)

                def stage(hb, x):
                    v.tensor_copy(idx[:, x, :], coli[:, bass.ds(hb * HB, HB)]).then_inc(staged, 1)

                for x in range(2):
                    stage(x, x)
                v.memset(acc[:, :, :], 0.0).then_inc(zeroed, 1)
                v.wait_ge(zeroed, 1)
                v.wait_ge(c_in, 16)
                onehot(0, 0)
                v.memset(w[:, 0, 0:1], 0.0).then_inc(acc_done, HB)
                v.wait_ge(acc_done, HB)
                with v.Fori(0, NHB // 2) as i:
                    for x in range(2):
                        hb = 2 * i + x
                        v.wait_ge(v_in[x], 16 * HB * i + 16 * HB)
                        v.tensor_tensor(w[:, :, 0:C].rearrange("p s (d h) -> p s d h", h=H),
                                        vb[:, x, :, :].rearrange("p s (d h) -> p s d h", h=H),
                                        bc(score[:, bass.ds(hb * HB, HB), :].unsqueeze(2), shw), ALU.mult)\
                         .then_inc(weighted, 1)
                        v.wait_ge(weighted, hb + 1)
                        stage(hb + 2, x)
                        onehot(hb + 1, 1 - x)
                        for s in range(HB):
                            tile = v.value_load(tmap[0:1, bass.ds(hb * HB + s, 1)], min_val=0, max_val=NT - 1)
                            v.wait_ge(summed, HB * hb + s + 1)
                            v.wait_ge(acc_done, HB * hb + s + HB)
                            at = acc[:, bass.ds(tile, 1), :]
                            v.tensor_tensor(at, at, pa[:, s, 0:C + H].unsqueeze(1), ALU.add).then_inc(acc_done, 1)
                        v.wait_ge(acc_done, HB * hb + 2 * HB)

            @block.tensor
            def _(pe):
                with pe.Fori(0, NHB // 2) as i:
                    for x in range(2):
                        hb = 2 * i + x
                        pe.wait_ge(ohs, hb + 1)
                        pe.wait_ge(weighted, hb + 1)
                        pe.wait_ge(p_put, hb + 1)
                        pe.wait_ge(acc_done, HB * hb + HB)
                        for s in range(HB):
                            pe.matmul(pa[:, s, 0:C + H], oh[:, x, s, :], w[:, s, :], start=True, stop=True).then_inc(summed, 1)


def combine(nc, A, W, sem, ident, ctxbd, acc):
    with ExitStack() as cx:
        def sb(n, s, d=F32):
            return cx.enter_context(nc.sbuf_tensor("c_" + n, s, d))

        def ps(n, s, d=F32):
            return cx.enter_context(nc.psum_tensor("c_" + n, s, d))
        wqm = sb("wqm", [P, KC, C])
        wpr = sb("wpr", [P, KC, C])
        wo = sb("wo", [P, KC, C])
        wg1 = sb("wg1", [P, KC, GH])
        wg2 = sb("wg2", [GH, C])
        bg1 = sb("bg1", [GH, 1])
        bg2 = sb("bg2", [P, KC])
        bo = sb("bo", [P, C])
        bpr = sb("bpr", [P, C])
        wgt = sb("wgt", [P, KC, NEXP])
        bgt = sb("bgt", [P, NEXP])
        iota = sb("iota", [P, NEXP])
        bsum = sb("bsum", [P, C])
        xnT = sb("xnT", [P, KC, GN])
        xmT = sb("xmT", [P, KC, GN])
        xg = sb("xg", [P, TPG, C])
        qmT = sb("qmT", [P, KC, GN])
        hgT = sb("hgT", [GH, GN])
        gT = sb("gT", [P, KC, GN])
        prT = sb("prT", [P, KC, GN])
        z = sb("z", [P, TPG, H])
        rz = sb("rz", [P, TPG, H])
        gn = sb("gn", [P, TPG, C])
        gnT = sb("gnT", [P, KC, GN])
        xb = sb("xb", [P, TPG, C])
        x2 = sb("x2", [P, TPG, C])
        st = sb("st", [P, TPG, 6])
        mv = sb("mv", [P, TPG, 2])
        ve = sb("ve", [P, TPG])
        sd = sb("sd", [P, TPG])
        rs = sb("rs", [P, TPG])
        xl = sb("xl", [P, TPG, C])
        xlT = sb("xlT", [P, KC, GN])
        gs = sb("gs", [P, TPG, NEXP])
        top = sb("top", [P, TPG, 8])
        tidx = sb("tidx", [P, TPG, 8], U32)
        tif = sb("tif", [P, TPG, 8])
        m1 = sb("m1", [P, TPG, NEXP])
        m2 = sb("m2", [P, TPG, NEXP])
        msk = sb("msk", [P, TPG, NEXP])
        pA = ps("pA", [P, KC, GN])
        pB = ps("pB", [P, KC, GN])
        pH = ps("pH", [P, GN])
        pD = ps("pD", [P, KC, GN])
        names = ["w_in", "x_in", "bsum_done", "qm_ps", "qm_done", "o_ps", "hg_ps", "hg_done", "g_ps", "g_done", "pr_done",
                 "z_done", "rz_done", "gn_done", "gn_turned", "gnT_done", "y_ps", "xb_done", "x2_done", "stats", "aggr", "var",
                 "std", "rstd", "xl_done", "xl_turned", "xlT_done", "gs_ps", "gs_done", "top_done", "tidx_done", "tif_done",
                 "m1_done", "m2_done", "msk_done", "stored"]
        s = {n: sem("c_" + n) for n in names}
        wnames = [(wqm, "wqm"), (wpr, "wpr"), (wo, "wo"), (wg1, "wg1"), (wg2, "wg2"), (bg1, "bg1"), (bg2, "bg2"), (bo, "bo"),
                  (bpr, "bpr"), (wgt, "wgt"), (bgt, "bgt"), (iota, "iota8")]
        with nc.Block() as block:
            @block.sync
            def _(sp):
                for dst, n in wnames:
                    full = dst[:, :, :] if len(dst.shape) == 3 else dst[:, :]
                    sp.dma_start(full, A[n]).then_inc(s["w_in"], 16)

                def load(i):
                    sp.dma_start(xnT[:, :, :], W["xnT"][:, :, bass.ds(i * GN, GN)]).then_inc(s["x_in"], 16)
                    sp.dma_start(xmT[:, :, :], W["xmT"][:, :, bass.ds(i * GN, GN)]).then_inc(s["x_in"], 16)
                    sp.dma_start(xg[:, :, :], rows(A["x"], i)).then_inc(s["x_in"], 16)

                def store(i):
                    sp.wait_ge(s["x2_done"], TPG * i + TPG)
                    sp.wait_ge(s["xlT_done"], i + 1)
                    sp.wait_ge(s["msk_done"], i + 1)
                    sp.dma_start(rows(W["x2"], i), x2[:, :, :]).then_inc(s["stored"], 16)
                    sp.dma_start(W["x2T"][:, :, bass.ds(i * GN, GN)], xlT[:, :, :]).then_inc(s["stored"], 16)
                    sp.dma_start(rows(W["mask"], i), msk[:, :, :]).then_inc(s["stored"], 16)
                load(0)
                with sp.Fori(0, NG - 1) as i:
                    sp.wait_ge(s["hg_ps"], i + 1)
                    sp.wait_ge(s["xb_done"], i + 1)
                    load(i + 1)
                    store(i)
                store(NG - 1)
                sp.wait_ge(s["stored"], 48 * NG + 48)

            @block.vector
            def _(v):
                v.wait_ge(s["w_in"], 16 * len(wnames))
                v.tensor_tensor(bsum[:, :], bo[:, :], bpr[:, :], ALU.add).then_inc(s["bsum_done"], 1)
                v.wait_ge(s["bsum_done"], 1)
                v.memset(x2[:, 0, 0:1], 0.0).then_inc(s["stored"], 48)
                v.wait_ge(s["stored"], 48)
                want_stats = counter(v, "x2_stats_want", TPG)
                want_gs = counter(v, "scores_want", 1)
                want_top = counter(v, "top_want", TPG)
                with v.Fori(0, NG) as i:
                    ga = acc[:, bass.ds(i * TPG, TPG), :]
                    v.tensor_scalar(z[:, :, :], ga[:, :, C:C + H], 1e-30, None, ALU.max).then_inc(s["z_done"], 1)
                    v.wait_ge(s["z_done"], i + 1)
                    v.reciprocal(rz[:, :, :], z[:, :, :]).then_inc(s["rz_done"], 1)
                    v.wait_ge(s["rz_done"], i + 1)
                    for j in range(TPG):
                        v.tensor_tensor(gn[:, j, :].rearrange("p (d h) -> p d h", h=H),
                                        acc[:, bass.ds(i * TPG + j, 1), 0:C].rearrange("p o (d h) -> p (o d) h", h=H),
                                        bc(rz[:, j, :].unsqueeze(1), [P, D, H]), ALU.mult).then_inc(s["gn_done"], 1)
                    v.wait_ge(s["x_in"], 48 * i + 48)
                    v.tensor_tensor(xb[:, :, :], xg[:, :, :], bc(bsum[:, :].unsqueeze(1), [P, TPG, C]), ALU.add)\
                     .then_inc(s["xb_done"], 1)
                    v.wait_ge(s["qm_ps"], i + 1)
                    v.tensor_copy(qmT[:, :, :], pA[:, :, :]).then_inc(s["qm_done"], 1)
                    v.wait_ge(s["o_ps"], i + 1)
                    v.wait_ge(s["g_done"], KC * i + KC)
                    v.tensor_tensor(prT[:, :, :], pB[:, :, :], gT[:, :, :], ALU.mult).then_inc(s["pr_done"], 1)
                    v.wait_ge(s["xb_done"], i + 1)
                    v.wait_ge(s["stored"], 48 * i + 48)
                    v.wait_ge(s["y_ps"], i + 1)
                    for j in range(TPG):
                        v.tensor_tensor(x2[:, j, :], xb[:, j, :], pD[:, j // 2, (j % 2) * C:(j % 2 + 1) * C], ALU.add)\
                         .then_inc(s["x2_done"], 1)
                    for j in range(TPG):
                        v.wait_ge(s["x2_done"], TPG * i + j + 1)
                        v.bn_stats(st[:, j, :], x2[:, j, :]).then_inc(s["stats"], 1)
                    passed(v, s["stats"], want_stats, TPG)
                    for j in range(TPG):
                        v.bn_aggr(mv[:, j, :], st[:, j, :]).then_inc(s["aggr"], 1)
                    v.wait_ge(s["aggr"], TPG * i + TPG)
                    v.tensor_scalar(ve[:, :], mv[:, :, 1], EPS, None, ALU.add).then_inc(s["var"], 1)
                    v.wait_ge(s["std"], i + 1)
                    v.reciprocal(rs[:, :], sd[:, :]).then_inc(s["rstd"], 1)
                    v.wait_ge(s["rstd"], i + 1)
                    for j in range(TPG):
                        v.tensor_scalar(xl[:, j, :], x2[:, j, :], mv[:, j, 0:1], rs[:, j:j + 1],
                                        ALU.subtract, ALU.mult).then_inc(s["xl_done"], 1)
                    v.wait_ge(s["gs_ps"], i + 1)
                    v.tensor_tensor(gs[:, :, :], pH[:, 0:TPG * NEXP].rearrange("p (j e) -> p j e", j=TPG),
                                    bc(bgt[:, :].unsqueeze(1), [P, TPG, NEXP]), ALU.add).then_inc(s["gs_done"], 1)
                    passed(v, s["gs_done"], want_gs, 1)
                    for j in range(TPG):
                        v.max(top[:, j, :], gs[:, j, :]).then_inc(s["top_done"], 1)
                    passed(v, s["top_done"], want_top, TPG)
                    for j in range(TPG):
                        v.max_index(tidx[:, j, :], top[:, j, :], gs[:, j, :]).then_inc(s["tidx_done"], 1)
                    v.wait_ge(s["tidx_done"], TPG * i + TPG)
                    v.tensor_copy(tif[:, :, :], tidx[:, :, :]).then_inc(s["tif_done"], 1)
                    v.wait_ge(s["tif_done"], i + 1)
                    sh = [P, TPG, NEXP]
                    v.tensor_tensor(m1[:, :, :], bc(iota[:, :].unsqueeze(1), sh), bc(tif[:, :, 0:1], sh), ALU.is_equal).then_inc(s["m1_done"], 1)
                    v.tensor_tensor(m2[:, :, :], bc(iota[:, :].unsqueeze(1), sh), bc(tif[:, :, 1:2], sh), ALU.is_equal).then_inc(s["m2_done"], 1)
                    v.wait_ge(s["m1_done"], i + 1)
                    v.wait_ge(s["m2_done"], i + 1)
                    v.tensor_tensor(msk[:, :, :], m1[:, :, :], m2[:, :, :], ALU.add).then_inc(s["msk_done"], 1)
                    v.wait_ge(s["msk_done"], i + 1)

            @block.scalar
            def _(a):
                a.wait_ge(s["w_in"], 16 * len(wnames))
                with a.Fori(0, NG) as i:
                    a.wait_ge(s["gn_turned"], i + 1)
                    a.copy(gnT[:, :, :], pD[:, :, :]).then_inc(s["gnT_done"], 1)
                    a.wait_ge(s["hg_ps"], i + 1)
                    a.activation(hgT[:, :], pH[0:GH, :], ACT.Gelu, bias=bg1[:, 0:1]).then_inc(s["hg_done"], 1)
                    a.wait_ge(s["g_ps"], i + 1)
                    for k in range(KC):
                        a.activation(gT[:, k, :], pD[:, k, :], ACT.Sigmoid, bias=bg2[:, k:k + 1]).then_inc(s["g_done"], 1)
                    a.wait_ge(s["var"], i + 1)
                    a.activation(sd[:, :], ve[:, :], ACT.Sqrt).then_inc(s["std"], 1)
                    a.wait_ge(s["xl_turned"], i + 1)
                    a.wait_ge(s["stored"], 48 * i + 48)
                    a.copy(xlT[:, :, :], pB[:, :, :]).then_inc(s["xlT_done"], 1)

            @block.tensor
            def _(pe):
                pe.wait_ge(s["w_in"], 16 * len(wnames))
                with pe.Fori(0, NG) as i:
                    pe.wait_ge(s["x_in"], 48 * i + 48)
                    for m in range(KC):
                        for k in range(KC):
                            t = pe.matmul(pA[:, m, :], wqm[:, k, m * P:(m + 1) * P], xnT[:, k, :], start=(k == 0), stop=(k == KC - 1))
                    t.then_inc(s["qm_ps"], 1)
                    pe.wait_ge(s["gn_done"], TPG * i + TPG)
                    for j in range(TPG):
                        for k in range(KC):
                            t = pe.transpose(pD[:, k, j * P:(j + 1) * P], gn[:, j, k * P:(k + 1) * P], ident[:, :])
                    t.then_inc(s["gn_turned"], 1)
                    for k in range(KC):
                        t = pe.matmul(pH[0:GH, :], wg1[:, k, :], xmT[:, k, :], start=(k == 0), stop=(k == KC - 1))
                    t.then_inc(s["hg_ps"], 1)
                    pe.wait_ge(s["qm_done"], i + 1)
                    for m in range(KC):
                        for k in range(KC):
                            t = pe.matmul(pB[:, m, :], ctxbd[:, k, m * P:(m + 1) * P], qmT[:, k, :], start=(k == 0), stop=(k == KC - 1))
                    t.then_inc(s["o_ps"], 1)
                    pe.wait_ge(s["hg_done"], i + 1)
                    pe.wait_ge(s["gnT_done"], i + 1)
                    for m in range(KC):
                        t = pe.matmul(pD[:, m, :], wg2[:, m * P:(m + 1) * P], hgT[:, :], start=True, stop=True)
                    t.then_inc(s["g_ps"], 1)
                    pe.wait_ge(s["pr_done"], i + 1)
                    pe.wait_ge(s["g_done"], KC * i + KC)
                    for j in range(TPG):
                        o = pD[:, j // 2, (j % 2) * C:(j % 2 + 1) * C]
                        for k in range(KC):
                            pe.matmul(o, prT[:, k, j * P:(j + 1) * P], wpr[:, k, :], start=(k == 0), stop=False)
                        for k in range(KC):
                            t = pe.matmul(o, gnT[:, k, j * P:(j + 1) * P], wo[:, k, :], start=False, stop=(k == KC - 1))
                    t.then_inc(s["y_ps"], 1)
                    pe.wait_ge(s["xl_done"], TPG * i + TPG)
                    for j in range(TPG):
                        for k in range(KC):
                            t = pe.transpose(pB[:, k, j * P:(j + 1) * P], xl[:, j, k * P:(k + 1) * P], ident[:, :])
                    t.then_inc(s["xl_turned"], 1)
                    pe.wait_ge(s["xlT_done"], i + 1)
                    for j in range(TPG):
                        for k in range(KC):
                            t = pe.matmul(pH[:, j * NEXP:(j + 1) * NEXP], xlT[:, k, j * P:(j + 1) * P], wgt[:, k, :],
                                          start=(k == 0), stop=(k == KC - 1))
                    t.then_inc(s["gs_ps"], 1)
                    pe.wait_ge(s["gs_done"], i + 1)


def experts(nc, A, W, sem, ident, out):
    with ExitStack() as cx:
        def sb(n, s, d=F32):
            return cx.enter_context(nc.sbuf_tensor("f_" + n, s, d))

        def ps(n, s, d=F32):
            return cx.enter_context(nc.psum_tensor("f_" + n, s, d))
        w1 = sb("w1", [P, NEXP, KC, HID])
        w2 = sb("w2", [P, NEXP, HC, C])
        b1 = sb("b1", [P, NEXP, HC])
        b2 = sb("b2", [NEXP, C])
        xT = sb("xT", [P, 2, KC, GN])
        x2 = sb("x2", [P, 2, TPG, C])
        mk = sb("mk", [P, 2, TPG, NEXP])
        mkT = sb("mkT", [NEXP, TPG, P])
        hT = sb("hT", [P, 2, HC, GN])
        o = sb("o", [P, TPG, C])
        pm = ps("pm", [P, TPG, P])
        ph = ps("ph", [P, HC, GN])
        py = ps("py", [P, TPG, C])
        w_in = sem("f_w_in")
        g_in = sem("f_g_in")
        m_turned = sem("f_m_turned")
        mT_done = sem("f_mT")
        b_ps = sem("f_b_ps")
        h_ps = sem("f_h_ps")
        h_done = sem("f_h")
        y_ps = sem("f_y_ps")
        o_done = sem("f_o")
        stored = sem("f_stored")
        with nc.Block() as block:
            @block.sync
            def _(sp):
                sp.dma_start(w1[:, :, :, :], A["w1"]).then_inc(w_in, 16)
                sp.dma_start(w2[:, :, :, :], A["w2"]).then_inc(w_in, 16)
                sp.dma_start(b1[:, :, :], A["b1"]).then_inc(w_in, 16)
                sp.dma_start(b2[:, :], A["b2"]).then_inc(w_in, 16)

                def load(i):
                    sp.dma_start(xT[:, 0, :, :], W["x2T"][:, :, bass.ds(i * GN, GN)]).then_inc(g_in, 16)
                    sp.dma_start(x2[:, 0, :, :], rows(W["x2"], i)).then_inc(g_in, 16)
                    sp.dma_start(mk[:, 0, :, :], rows(W["mask"], i)).then_inc(g_in, 16)

                def store(i):
                    sp.wait_ge(o_done, TPG * (NEXP + 1) * i + TPG * (NEXP + 1))
                    sp.dma_start(rows(out, i), o[:, :, :]).then_inc(stored, 16)
                load(0)
                with sp.Fori(0, NG - 1) as i:
                    store(i)
                    load(i + 1)
                store(NG - 1)
                sp.wait_ge(stored, 16 * NG + 16)

            @block.vector
            def _(v):
                v.memset(o[:, 0, 0:1], 0.0).then_inc(stored, 16)
                with v.Fori(0, NG) as i:
                    per = TPG * (NEXP + 1)
                    v.wait_ge(g_in, 48 * i + 48)
                    v.wait_ge(m_turned, i + 1)
                    v.tensor_copy(mkT[:, :, :], pm[0:NEXP, :, :]).then_inc(mT_done, 1)
                    v.wait_ge(stored, 16 * i + 16)
                    for j in range(TPG):
                        v.wait_ge(b_ps, TPG * i + (j | 1) + 1)
                        v.tensor_tensor(o[:, j, :], x2[:, 0, j, :], py[:, j, :], ALU.add).then_inc(o_done, 1)
                    for e in range(NEXP):
                        for j in range(TPG):
                            v.wait_ge(y_ps, i * TPG * NEXP + e * TPG + (j | 1) + 1)
                            v.wait_ge(o_done, per * i + e * TPG + j + 1)
                            v.scalar_tensor_tensor(out=o[:, j, :], in0=py[:, j, :], scalar=mk[:, 0, j, e:e + 1],
                                                   in1=o[:, j, :], op0=ALU.mult, op1=ALU.add).then_inc(o_done, 1)

            @block.scalar
            def _(a):
                a.wait_ge(w_in, 64)
                with a.Fori(0, NG) as i:
                    for e in range(NEXP):
                        for m in range(HC):
                            a.wait_ge(h_ps, (i * NEXP + e) * HC + m + 1)
                            a.activation(hT[:, e % 2, m, :], ph[:, m, :], ACT.Gelu, bias=b1[:, e, m:m + 1]).then_inc(h_done, 1)

            @block.tensor
            def _(pe):
                pe.wait_ge(w_in, 64)

                def up(i, e):
                    for m in range(HC):
                        if e:
                            pe.wait_ge(h_done, (i * NEXP + e - 1) * HC + m + 1)
                        for k in range(KC):
                            t = pe.matmul(ph[:, m, :], w1[:, e, k, m * P:(m + 1) * P], xT[:, 0, k, :],
                                          start=(k == 0), stop=(k == KC - 1))
                        t.then_inc(h_ps, 1)

                def down(i, e):
                    pe.wait_ge(h_done, (i * NEXP + e) * HC + HC)
                    for j in range(TPG):
                        if j % 2 == 0:
                            pe.wait_ge(o_done, TPG * (NEXP + 1) * i + e * TPG + j + 2)
                        for m in range(HC):
                            t = pe.matmul(py[:, j, :], hT[:, e % 2, m, j * P:(j + 1) * P], w2[:, e, m, :],
                                          start=(m == 0), stop=(m == HC - 1))
                        t.then_inc(y_ps, 1)
                with pe.Fori(0, NG) as i:
                    pe.wait_ge(g_in, 48 * i + 48)
                    for j in range(TPG):
                        t = pe.transpose(pm[0:NEXP, j, :], mk[:, 0, j, :], ident[:, :])
                    t.then_inc(m_turned, 1)
                    up(i, 0)
                    pe.wait_ge(mT_done, i + 1)
                    for j in range(TPG):
                        pe.matmul(py[:, j, :], mkT[:, j, :], b2[:, :], start=True, stop=True).then_inc(b_ps, 1)
                    for e in range(NEXP):
                        if e + 1 < NEXP:
                            up(i, e + 1)
                        down(i, e)
                    pe.wait_ge(o_done, TPG * (NEXP + 1) * i + TPG * (NEXP + 1))


def kernel(**inputs):
    import numpy as np
    import concourse.bacc as bacc
    from concourse.bass_utils import run_bass_kernel_spmd

    a = {k: np.ascontiguousarray(v) for k, v in inputs.items()}

    def halves(w):
        return np.ascontiguousarray(w.reshape(-1, P, w.shape[1]).transpose(1, 0, 2))

    def repeat(b):
        return np.ascontiguousarray(np.broadcast_to(b[None, :], (P, b.shape[0])))

    def columns(b):
        return np.ascontiguousarray(b.reshape(-1, P).T)

    f32 = np.float32
    x = np.zeros((NPAD, C), f32)
    x[:N] = a["x"]
    qkvm = a["L0_mix_Wqkv"]
    ar = np.arange
    g = "L0_gnn_"
    arrays = {
        "x": x, "src": a["src"], "dst": a["dst"],
        "wall": halves(np.concatenate([a[g + "Wq"].T, qkvm[:, C:2 * C], a[g + "Wk"].T, a[g + "Wv"].T, qkvm[:, 2 * C:]], 1)),
        "bq": repeat(a[g + "bq"]), "bkv": repeat(np.concatenate([a[g + "bk"], a[g + "bv"]])),
        "lng": columns(a["L0_mix_ln_g"]), "lnb": columns(a["L0_mix_ln_b"]),
        "vmask": np.where(ar(NTP)[None, :] * P + ar(P)[:, None] < N, 0.0, -BIG).astype(f32),
        "ident": np.eye(P, dtype=f32), "iota": np.broadcast_to(ar(P, dtype=f32)[None, :], (P, P)).copy(),
        "triu": np.triu(np.ones((P, P), f32), 1),
        "jtile": (ar(P)[:, None] * (STM // P) + ar(STM // P)[None, :]).astype(f32),
        "bdmask": halves((ar(C)[:, None] // D == ar(C)[None, :] // D).astype(f32)),
        "wqm": halves(qkvm[:, 0:C]), "wpr": halves(a["L0_mix_Wproj"]), "wo": halves(np.ascontiguousarray(a[g + "Wo"].T)),
        "wg1": halves(a["L0_mix_Wg1"]), "wg2": a["L0_mix_Wg2"], "bg1": a["L0_mix_bg1"].reshape(GH, 1),
        "bg2": columns(a["L0_mix_bg2"]), "bo": repeat(a[g + "bo"]), "bpr": repeat(a["L0_mix_bproj"]),
        "wgt": halves(a["L0_ffn_Wg"]), "bgt": repeat(a["L0_ffn_bg"]),
        "iota8": np.broadcast_to(ar(NEXP, dtype=f32)[None, :], (P, NEXP)).copy(),
        "w1": np.ascontiguousarray(a["L0_ffn_W1"].reshape(NEXP, KC, P, HID).transpose(2, 0, 1, 3)),
        "w2": np.ascontiguousarray(a["L0_ffn_W2"].reshape(NEXP, HC, P, C).transpose(2, 0, 1, 3)),
        "b1": np.ascontiguousarray(a["L0_ffn_b1"].reshape(NEXP, HC, P).transpose(2, 0, 1)),
        "b2": a["L0_ffn_b2"],
    }
    nc = bacc.Bacc("TRN2", target_bir_lowering=False, num_devices=1)
    A = {k: nc.dram_tensor("in_" + k, v.shape, mybir.dt.from_np(v.dtype), kind="ExternalInput").ap()
         for k, v in arrays.items()}
    out = nc.dram_tensor("out", (NPAD, C), F32, kind="ExternalOutput").ap()
    build(nc, A, out)
    r = run_bass_kernel_spmd(nc, [{"in_" + k: v for k, v in arrays.items()}], core_ids=[0])
    return np.ascontiguousarray(r.results[0]["out"][:N])
```

```python
from contextlib import ExitStack, contextmanager

import concourse.bass as bass
from concourse import mybir

F32 = mybir.dt.float32
BF16 = mybir.dt.bfloat16
I32 = mybir.dt.int32
U32 = mybir.dt.uint32
ALU = mybir.AluOpType
ACT = mybir.ActivationFunctionType
AX = mybir.AxisListType.X

P = 128
N = 6250
C = 256
H = 8
D = C // H
E = 106250
KC = C // P

NT = (N + P - 1) // P
TPG = 4
GN = TPG * P
NG = (NT + TPG - 1) // TPG
NPAD = NG * GN
NTP = NG * TPG

EL = 125
ET = E // EL
SB_ = 10
HB2 = (ET // SB_ - 1) // 2
assert ET == SB_ * (2 * HB2 + 1)
CH = 16
ST_NEED = (E + NT * (P - 1)) // P
GPC = (ST_NEED + CH - 1) // CH
ST = CH * GPC
HB = 4
NHB = ST // HB
STM = (ST + P - 1) // P * P
RING = 4
STX = ST + RING * HB
ROWPAD = 8191
BIG = 1e30
NEXP = 8
HID = 512
HC = HID // P
GH = 64
EPS = 1e-5
SCALE = float(D) ** -0.5


def rows(ap, i):
    return ap[bass.ds(i * GN, GN), :].rearrange("(j p) c -> p j c", p=P)


@contextmanager
def stage(nc):
    with ExitStack() as cx:
        used = []

        def sem(name):
            used.append(cx.enter_context(nc.semaphore(name)))
            return used[-1]
        yield sem
        with nc.Block() as block:
            @block.gpsimd
            def _(g):
                for one in used:
                    g.sem_clear(one)


def counter(eng, name, first):
    reg = eng.alloc_register(name)
    eng.reg_mov(reg, first)
    return reg


def passed(eng, semaphore, reg, step):
    eng.wait_ge(semaphore, eng.snap(reg))
    eng.reg_add(reg, reg, step)


def node_tiles(nc, engine, tmap, hb):
    return nc.values_load_multi_w_load_instructions(
        tmap[0:1, bass.ds(hb * HB, HB)], engines=[engine], min_val=0, max_val=NT - 1)[1]


def bc(ap, shape):
    return ap.broadcast_to(shape)


def build(nc, A, out):
    ctx = ExitStack()
    with ctx:
        def sem(name):
            return ctx.enter_context(nc.semaphore(name))

        def sbp(name, shape, dt):
            return ctx.enter_context(nc.sbuf_tensor(name, shape, dt))

        def dram(name, shape, dt):
            return nc.dram_tensor(name, shape, dt).ap()

        W = dict(
            k=dram("k_tab", [NPAD, C], F32), v=dram("v_tab", [NPAD, C], F32),
            km=dram("kvmix", [NPAD, 2 * C], F32),
            xnT=dram("xnT_d", [P, KC, NPAD], F32), xmT=dram("xmT_d", [P, KC, NPAD], F32),
            sorted=dram("sorted_edges", [ST * P, 2], I32), tmap=dram("tile_map", [1, STM], I32),
            x2=dram("x2_d", [NPAD, C], F32), xl=dram("x2_normed", [NPAD, C], F32),
            xs=dram("expert_rows", [DUMP + 2 * P, C], F32), ys=dram("expert_out", [EXT * P, C], F32),
            emap=dram("tile_experts", [1, EM], I32),
            ends=dram("chunk_ends", [2, P, 3], F32), carry=dram("chunk_carry", [2, CH, H], F32),
        )
        ident = sbp("ident", [P, P], F32)
        S = {}
        s_const = sem("const_loaded")
        with nc.Block() as block:
            @block.sync
            def _(sp):
                sp.dma_start(ident[:, :], A["ident"]).then_inc(s_const, 16)
                sp.wait_ge(s_const, 16)
        ctxbd = sbp("ctxbd", [P, KC, C], F32)
        kmax = sbp("kmax", [P, C], F32)
        score = sbp("score", [P, ST, H], F32)
        rowf = sbp("row_sorted", [P, ST], F32)
        rowl = sbp("row_in_tile", [P, STX], F32)
        coli = sbp("col_sorted", [P, STX], I32)
        tmap = sbp("tile_map_sb", [1, STM], I32)
        with ExitStack() as qx:
            q3 = qx.enter_context(nc.sbuf_tensor("q_parts", [P, NTP, 3, C], BF16))
            with stage(nc) as sem:
                node_tables(nc, A, W, sem, ident, q3, kmax)
            with stage(nc) as sem:
                mix_context(nc, A, W, sem, ident, kmax, ctxbd)
            with ExitStack() as bx:
                pos_base = bx.enter_context(nc.sbuf_tensor("pos_base", [P, NT], F32))
                rc = bx.enter_context(nc.sbuf_tensor("rowcol", [EL, ET, 2], I32))
                lo = bx.enter_context(nc.sbuf_tensor("row_lo", [EL, ET + 2 * SB_], F32))
                hi = bx.enter_context(nc.sbuf_tensor("row_hi", [EL, ET + 2 * SB_], F32))
                with stage(nc) as sem:
                    histogram(nc, A, W, sem, ident, rc, lo, hi, pos_base)
                with stage(nc) as sem:
                    sort_edges(nc, A, W, sem, ident, rc, lo, hi, pos_base)
            with stage(nc) as sem:
                load_sorted(nc, A, W, sem, ident, rowf, rowl, coli, tmap)
            with stage(nc) as sem:
                edge_scores(nc, A, W, sem, rowl, coli, tmap, q3, score)
        with stage(nc) as sem:
            softmax_edges(nc, A, W, sem, ident, rowf, score)
        first = sbp("first_expert", [P, NTP, NEXP], F32)
        second = sbp("second_expert", [P, NTP, NEXP], F32)
        with ExitStack() as ax:
            acc = ax.enter_context(nc.sbuf_tensor("acc", [P, NTP, C + H], F32))
            with stage(nc) as sem:
                aggregate(nc, A, W, sem, rowl, coli, tmap, score, acc)
            with stage(nc) as sem:
                combine(nc, A, W, sem, ident, ctxbd, acc, first, second)
        slot_i = sbp("slot_scatter", [P, 2, NT], I32)
        slot_g = sbp("slot_gather", [P, 2, NTP + 4], I32)
        emap = sbp("tile_experts_sb", [1, EM], I32)
        with stage(nc) as sem:
            route(nc, A, W, sem, ident, first, second, slot_i, slot_g, emap)
        with stage(nc) as sem:
            experts(nc, A, W, sem, ident, emap)
        with stage(nc) as sem:
            finish(nc, A, W, sem, slot_g, out)


def node_tables(nc, A, W, sem, ident, q3, kmax):
    with ExitStack() as cx:
        def sb(n, s, d=F32):
            return cx.enter_context(nc.sbuf_tensor("n_" + n, s, d))

        def ps(n, s, d=F32):
            return cx.enter_context(nc.psum_tensor("n_" + n, s, d))
        wall = sb("wall", [P, KC, 5 * C])
        bq = sb("bq", [P, C])
        bkv = sb("bkv", [P, 2 * C])
        lng = sb("lng", [P, KC])
        lnb = sb("lnb", [P, KC])
        vmask = sb("vmask", [P, NTP])
        xg = sb("xg", [P, TPG, C])
        xn = sb("xn", [P, TPG, C])
        xm = sb("xm", [P, TPG, C])
        st1 = sb("st1", [P, TPG, 6])
        st2 = sb("st2", [P, TPG, 6])
        mv1 = sb("mv1", [P, TPG, 2])
        mv2 = sb("mv2", [P, TPG, 2])
        ve1 = sb("ve1", [P, TPG])
        ve2 = sb("ve2", [P, TPG])
        sd1 = sb("sd1", [P, TPG])
        sd2 = sb("sd2", [P, TPG])
        rs1 = sb("rs1", [P, TPG])
        rs2 = sb("rs2", [P, TPG])
        xnT = sb("xnT", [P, KC, GN])
        xmT = sb("xmT", [P, KC, GN])
        kv = sb("kv", [P, TPG, 2 * C])
        kvm = sb("kvm", [P, TPG, 2 * C])
        qf = sb("qf", [P, TPG, C])
        qr = sb("qr", [P, TPG, C])
        pT = ps("pT", [P, KC, GN])
        pM = ps("pM", [P, KC, GN])
        pA = ps("pA", [P, 2 * C])
        pB = ps("pB", [P, 2 * C])
        pC = ps("pC", [P, C])
        w_in = sem("n_weights_in")
        x_in = sem("n_x_in")
        stats1 = sem("n_stats1")
        aggr1 = sem("n_aggr1")
        var1 = sem("n_var1")
        std1 = sem("n_std1")
        rstd1 = sem("n_rstd1")
        xn_done = sem("n_xn_done")
        stats2 = sem("n_stats2")
        aggr2 = sem("n_aggr2")
        var2 = sem("n_var2")
        std2 = sem("n_std2")
        rstd2 = sem("n_rstd2")
        xm_done = sem("n_xm_done")
        xn_turned = sem("n_xn_turned")
        xm_turned = sem("n_xm_turned")
        xnT_done = sem("n_xnT_done")
        xmT_done = sem("n_xmT_done")
        xT_stored = sem("n_xT_stored")
        kv_stored = sem("n_kv_stored")
        kvm_stored = sem("n_kvm_stored")
        proj = sem("n_proj")
        proj_read = sem("n_proj_read")
        vm_read = sem("n_vm_read")
        kmax_step = sem("n_kmax_step")
        km_done = sem("n_km_done")
        q_done = sem("n_q_done")
        q_high = sem("n_q_high")
        q_rest = sem("n_q_rest")
        q_mid = sem("n_q_mid")
        q_low = sem("n_q_low")

        with nc.Block() as block:
            @block.sync
            def _(sp):
                for dst, name in ((wall, "wall"), (bq, "bq"), (bkv, "bkv"), (lng, "lng"), (lnb, "lnb"), (vmask, "vmask")):
                    d = dst[:, :, :] if name == "wall" else dst[:, :]
                    sp.dma_start(d, A[name]).then_inc(w_in, 16)
                sp.dma_start(xg[:, :, :], rows(A["x"], 0)).then_inc(x_in, 16)

                def store(i):
                    sp.wait_ge(xnT_done, i + 1)
                    sp.dma_start(W["xnT"][:, :, bass.ds(i * GN, GN)], xnT[:, :, :]).then_inc(xT_stored, 16)
                    sp.wait_ge(xmT_done, 2 * i + 2)
                    sp.dma_start(W["xmT"][:, :, bass.ds(i * GN, GN)], xmT[:, :, :]).then_inc(xT_stored, 16)
                    sp.wait_ge(proj_read, 4 * i + 4)
                    sp.dma_start(rows(W["k"], i), kv[:, :, 0:C]).then_inc(kv_stored, 16)
                    sp.dma_start(rows(W["v"], i), kv[:, :, C:2 * C]).then_inc(kv_stored, 16)
                    sp.wait_ge(vm_read, 4 * i + 4)
                    sp.wait_ge(km_done, 4 * i + 4)
                    sp.dma_start(rows(W["km"], i), kvm[:, :, :]).then_inc(kvm_stored, 16)

                with sp.Fori(0, NG - 1) as i:
                    sp.wait_ge(xn_done, 4 * i + 4)
                    sp.dma_start(xg[:, :, :], rows(A["x"], i + 1)).then_inc(x_in, 16)
                    store(i)
                store(NG - 1)
                sp.wait_ge(xT_stored, 32 * NG + 32)
                sp.wait_ge(kv_stored, 32 * NG + 32)
                sp.wait_ge(kvm_stored, 16 * NG + 16)

            @block.vector
            def _(v):
                v.memset(kmax[:, :], -BIG).then_inc(kmax_step, 1)
                v.memset(st1[:, 0, :], 0.0).then_inc(xn_turned, 1)
                v.memset(st2[:, 0, :], 0.0).then_inc(xm_turned, 1)
                v.memset(kv[:, 0, 0:1], 0.0).then_inc(kv_stored, 32)
                v.memset(kvm[:, 0, 0:1], 0.0).then_inc(kvm_stored, 16)
                v.wait_ge(w_in, 96)
                v.wait_ge(xn_turned, 1)
                v.wait_ge(xm_turned, 1)
                want1 = counter(v, "stats1_want", TPG)
                want2 = counter(v, "stats2_want", TPG)
                with v.Fori(0, NG) as i:
                    v.wait_ge(x_in, 16 * i + 16)
                    for j in range(TPG):
                        v.bn_stats(st1[:, j, :], xg[:, j, :]).then_inc(stats1, 1)
                    passed(v, stats1, want1, TPG)
                    for j in range(TPG):
                        v.bn_aggr(mv1[:, j, :], st1[:, j, :]).then_inc(aggr1, 1)
                    v.wait_ge(aggr1, TPG * i + TPG)
                    v.tensor_scalar(ve1[:, :], mv1[:, :, 1], EPS, None, ALU.add).then_inc(var1, 1)
                    v.wait_ge(std1, i + 1)
                    v.reciprocal(rs1[:, :], sd1[:, :]).then_inc(rstd1, 1)
                    v.wait_ge(rstd1, i + 1)
                    v.wait_ge(xn_turned, i + 1)
                    for j in range(TPG):
                        v.tensor_scalar(xn[:, j, :], xg[:, j, :], mv1[:, j, 0:1], rs1[:, j:j + 1],
                                        ALU.subtract, ALU.mult).then_inc(xn_done, 1)
                    for j in range(TPG):
                        v.wait_ge(xn_done, TPG * i + j + 1)
                        v.bn_stats(st2[:, j, :], xn[:, j, :]).then_inc(stats2, 1)
                    passed(v, stats2, want2, TPG)
                    for j in range(TPG):
                        v.bn_aggr(mv2[:, j, :], st2[:, j, :]).then_inc(aggr2, 1)
                    v.wait_ge(aggr2, TPG * i + TPG)
                    v.tensor_scalar(ve2[:, :], mv2[:, :, 1], EPS, None, ALU.add).then_inc(var2, 1)
                    v.wait_ge(std2, i + 1)
                    v.reciprocal(rs2[:, :], sd2[:, :]).then_inc(rstd2, 1)
                    v.wait_ge(rstd2, i + 1)
                    v.wait_ge(xm_turned, i + 1)
                    for j in range(TPG):
                        v.tensor_scalar(xm[:, j, :], xn[:, j, :], mv2[:, j, 0:1], rs2[:, j:j + 1],
                                        ALU.subtract, ALU.mult).then_inc(xm_done, 1)
                    v.wait_ge(kv_stored, 32 * i + 32)
                    v.wait_ge(kvm_stored, 16 * i + 16)
                    for j in range(TPG):
                        v.wait_ge(proj, TPG * i + j + 1)
                        v.tensor_tensor(qf[:, j, :], pA[:, 0:C], bq[:, :], ALU.add).then_inc(q_done, 1)
                        v.tensor_scalar(kvm[:, j, 0:C], pA[:, C:2 * C], vmask[:, bass.ds(TPG * i + j, 1)], None,
                                        ALU.add).then_inc(km_done, 1)
                        v.tensor_tensor(kv[:, j, :], pB[:, :], bkv[:, :], ALU.add).then_inc(proj_read, 1)
                        v.wait_ge(km_done, TPG * i + j + 1)
                        v.wait_ge(kmax_step, TPG * i + j + 1)
                        v.tensor_tensor(kmax[:, :], kmax[:, :], kvm[:, j, 0:C], ALU.max).then_inc(kmax_step, 1)
                    qg = q3[:, bass.ds(TPG * i, TPG), :, :]
                    v.wait_ge(q_high, i + 1)
                    v.tensor_tensor(qr[:, :, :], qf[:, :, :], qg[:, :, 0, :], ALU.subtract).then_inc(q_rest, 1)
                    v.wait_ge(q_mid, i + 1)
                    v.tensor_tensor(qg[:, :, 2, :], qr[:, :, :], qg[:, :, 1, :], ALU.subtract).then_inc(q_low, 1)
                    v.wait_ge(q_low, i + 1)

            @block.scalar
            def _(a):
                a.wait_ge(w_in, 96)
                with a.Fori(0, NG) as i:
                    a.wait_ge(var1, i + 1)
                    a.activation(sd1[:, :], ve1[:, :], ACT.Sqrt).then_inc(std1, 1)
                    a.wait_ge(xn_turned, i + 2)
                    a.wait_ge(xT_stored, 32 * i + 32)
                    a.copy(xnT[:, :, :], pT[:, :, :]).then_inc(xnT_done, 1)
                    a.wait_ge(var2, i + 1)
                    a.activation(sd2[:, :], ve2[:, :], ACT.Sqrt).then_inc(std2, 1)
                    a.wait_ge(xm_turned, i + 2)
                    for k in range(KC):
                        a.activation(xmT[:, k, :], pM[:, k, :], ACT.Identity, bias=lnb[:, k:k + 1],
                                     scale=lng[:, k:k + 1]).then_inc(xmT_done, 1)
                    a.wait_ge(kvm_stored, 16 * i + 16)
                    for j in range(TPG):
                        a.wait_ge(proj, TPG * i + j + 1)
                        a.copy(kvm[:, j, C:2 * C], pC[:, :]).then_inc(vm_read, 1)
                    a.wait_ge(q_done, TPG * i + TPG)
                    a.copy(q3[:, bass.ds(TPG * i, TPG), 0, :], qf[:, :, :]).then_inc(q_high, 1)
                    a.wait_ge(q_rest, i + 1)
                    a.copy(q3[:, bass.ds(TPG * i, TPG), 1, :], qr[:, :, :]).then_inc(q_mid, 1)

            @block.gpsimd
            def _(g):
                g.memset(xnT[:, 0, 0:1], 0.0).then_inc(xT_stored, 32)

            @block.tensor
            def _(pe):
                pe.wait_ge(w_in, 96)
                with pe.Fori(0, NG) as i:
                    pe.wait_ge(xn_done, TPG * i + TPG)
                    for j in range(TPG):
                        for k in range(KC):
                            t = pe.transpose(pT[:, k, j * P:(j + 1) * P], xn[:, j, k * P:(k + 1) * P], ident[:, :])
                    t.then_inc(xn_turned, 1)
                    pe.wait_ge(xm_done, TPG * i + TPG)
                    for j in range(TPG):
                        for k in range(KC):
                            t = pe.transpose(pM[:, k, j * P:(j + 1) * P], xm[:, j, k * P:(k + 1) * P], ident[:, :])
                    t.then_inc(xm_turned, 1)
                    pe.wait_ge(xnT_done, i + 1)
                    for j in range(TPG):
                        if j:
                            pe.wait_ge(proj_read, TPG * i + j)
                            pe.wait_ge(vm_read, TPG * i + j)
                        for dst, c0, c1 in ((pA, 0, 2 * C), (pB, 2 * C, 4 * C), (pC, 4 * C, 5 * C)):
                            for k in range(KC):
                                m = pe.matmul(dst[:, :], xnT[:, k, j * P:(j + 1) * P], wall[:, k, c0:c1],
                                              start=(k == 0), stop=(k == KC - 1))
                        m.then_inc(proj, 1)
                    pe.wait_ge(proj_read, TPG * i + TPG)
                    pe.wait_ge(vm_read, TPG * i + TPG)
                    pe.wait_ge(xmT_done, 2 * i + 2)


def mix_context(nc, A, W, sem, ident, kmax, ctxbd):
    with ExitStack() as cx:
        def sb(n, s, d=F32):
            return cx.enter_context(nc.sbuf_tensor("m_" + n, s, d))

        def ps(n, s, d=F32):
            return cx.enter_context(nc.psum_tensor("m_" + n, s, d))
        ones = sb("ones", [P, P])
        zero = sb("zero", [P, P])
        bd = sb("bd", [P, KC, C])
        kcol = sb("kcol", [P, KC])
        diag = sb("diag", [P, C])
        krow = sb("krow", [P, C])
        km = sb("km", [P, TPG, 2 * C + 1])
        e = sb("e", [P, TPG, C])
        rsum = sb("rsum", [P, KC])
        pk = ps("pk", [P, C])
        prow = ps("prow", [P, C])
        pctx = ps("pctx", [P, KC, 512])
        bd_in = sem("m_bd_in")
        filled = sem("m_filled")
        turned = sem("m_turned")
        colmax = sem("m_colmax")
        diag_done = sem("m_diag")
        row_ps = sem("m_row_ps")
        row_done = sem("m_row")
        km_in = sem("m_km_in")
        sub_done = sem("m_sub")
        e_done = sem("m_e")
        ctx_step = sem("m_ctx_step")
        rs_done = sem("m_rs")
        bd_done = sem("m_bd_done")
        with nc.Block() as block:
            @block.sync
            def _(sp):
                sp.dma_start(bd[:, :, :], A["bdmask"]).then_inc(bd_in, 16)
                sp.dma_start(km[:, :, 0:2 * C], rows(W["km"], 0)).then_inc(km_in, 16)
                with sp.Fori(0, NG - 1) as i:
                    sp.wait_ge(ctx_step, i + 1)
                    sp.dma_start(km[:, :, 0:2 * C], rows(W["km"], i + 1)).then_inc(km_in, 16)

            @block.gpsimd
            def _(g):
                g.memset(ones[:, :], 1.0).then_inc(filled, 1)
                g.memset(zero[:, :], 0.0).then_inc(filled, 1)
                g.memset(km[:, :, 2 * C:2 * C + 1], 1.0).then_inc(filled, 1)

            @block.vector
            def _(v):
                v.wait_ge(turned, 1)
                v.tensor_reduce(kcol[:, :], pk[:, :].rearrange("p (k n) -> p k n", k=KC), AX, ALU.max).then_inc(colmax, 1)
                v.wait_ge(colmax, 1)
                for k in range(KC):
                    v.tensor_scalar(diag[:, k * P:(k + 1) * P], ident[:, :], kcol[:, k:k + 1], None,
                                    ALU.mult).then_inc(diag_done, 1)
                v.wait_ge(row_ps, 1)
                v.tensor_copy(krow[:, :], prow[:, :]).then_inc(row_done, 1)
                v.wait_ge(row_done, 1)
                with v.Fori(0, NG) as i:
                    v.wait_ge(km_in, 16 * i + 16)
                    v.tensor_tensor(e[:, :, :], km[:, :, 0:C], bc(krow[:, :].unsqueeze(1), [P, TPG, C]),
                                    ALU.subtract).then_inc(sub_done, 1)
                v.wait_ge(ctx_step, NG + 1)
                v.reciprocal(rsum[:, :], pctx[:, :, C]).then_inc(rs_done, 1)
                v.wait_ge(rs_done, 1)
                v.wait_ge(bd_in, 16)
                for k in range(KC):
                    v.scalar_tensor_tensor(out=ctxbd[:, k, :], in0=pctx[:, k, 0:C], scalar=rsum[:, k:k + 1],
                                           in1=bd[:, k, :], op0=ALU.mult, op1=ALU.mult).then_inc(bd_done, 1)

            @block.scalar
            def _(a):
                with a.Fori(0, NG) as i:
                    a.wait_ge(sub_done, i + 1)
                    a.activation(e[:, :, :], e[:, :, :], ACT.Exp).then_inc(e_done, 1)

            @block.tensor
            def _(pe):
                for k in range(KC):
                    t = pe.transpose(pk[:, k * P:(k + 1) * P], kmax[:, k * P:(k + 1) * P], ident[:, :])
                t.then_inc(turned, 1)
                pe.wait_ge(filled, 3)
                pe.wait_ge(diag_done, KC)
                pe.matmul(prow[:, :], ones[:, :], diag[:, :], start=True, stop=True).then_inc(row_ps, 1)
                for k in range(KC):
                    pe.matmul(pctx[:, k, 0:P], zero[:, :], zero[:, :], start=True, stop=False, skip_group_check=True)
                    pe.matmul(pctx[:, k, P:2 * P], zero[:, :], zero[:, :], start=False, stop=False, skip_group_check=True)
                    pe.matmul(pctx[:, k, 2 * P:2 * P + 1], zero[:, :], zero[:, 0:1], start=False, stop=False,
                              skip_group_check=True)
                with pe.Fori(0, NG) as i:
                    pe.wait_ge(e_done, i + 1)
                    for j in range(TPG):
                        for k in range(KC):
                            m = pe.matmul(pctx[:, k, 0:C + 1], e[:, j, k * P:(k + 1) * P], km[:, j, C:2 * C + 1],
                                          start=False, stop=False, skip_group_check=True)
                    m.then_inc(ctx_step, 1)
                for k in range(KC):
                    m = pe.matmul(pctx[:, k, 0:1], zero[:, :], zero[:, 0:1], start=False, stop=True,
                                  skip_group_check=True)
                m.then_inc(ctx_step, 1)


def histogram(nc, A, W, sem, ident, rc, lo, hi, pos_base):
    with ExitStack() as cx:
        def sb(n, s, d=F32):
            return cx.enter_context(nc.sbuf_tensor("h_" + n, s, d))

        def ps(n, s, d=F32):
            return cx.enter_context(nc.psum_tensor("h_" + n, s, d))
        ei = sb("ei", [EL, 2, ET], I32)
        ti = sb("ti", [EL, 2, ET], I32)
        iota = sb("iota", [P, P])
        triu = sb("triu", [P, P])
        jt = sb("jt", [P, STM // P])
        ones = sb("ones", [P, P])
        zero = sb("zero", [P, P])
        fill = sb("fill", [P, ST, 2], I32)
        ohlo = sb("ohlo", [EL, 2, SB_, P], BF16)
        ohhi = sb("ohhi", [EL, 2, SB_, NT], BF16)
        cnt = sb("cnt", [P, NT])
        tot = sb("tot", [P, NT], I32)
        tot2 = sb("tot2", [P, NT], I32)
        tot3 = sb("tot3", [P, NT], I32)
        tiles = sb("tiles", [P, NT])
        incl = sb("incl", [P, NT])
        excl = sb("excl", [P, NT])
        cmp = sb("cmp", [P, STM // P, NT])
        tmf = sb("tmf", [P, STM // P])
        tmi = sb("tmi", [P, STM // P], I32)
        pcnt = ps("pcnt", [P, NT])
        ptot = ps("ptot", [P, NT])
        pbef = ps("pbef", [P, NT])
        e_in = sem("h_e_in")
        c_in = sem("h_c_in")
        fill_done = sem("h_fill")
        fill_out = sem("h_fill_out")
        filled = sem("h_filled")
        bits = sem("h_bits")
        fields = sem("h_fields")
        oh = sem("h_onehots_lo")
        ohh = sem("h_onehots_hi")
        counted = sem("h_counted")
        cnt_done = sem("h_cnt")
        tot_ps = sem("h_tot_ps")
        tot_done = sem("h_tot")
        tiles_done = sem("h_tiles")
        incl_done = sem("h_incl")
        excl_done = sem("h_excl")
        base_done = sem("h_base")
        cmp_done = sem("h_cmp")
        tmf_done = sem("h_tmf")
        tmf2_done = sem("h_tmf2")
        tmi_done = sem("h_tmi")
        tm_out = sem("h_tm_out")
        with nc.Block() as block:
            @block.sync
            def _(sp):
                sp.dma_start(ei[:, 0, :], A["src"].rearrange("(p t) -> p t", p=EL)).then_inc(e_in, 16)
                sp.dma_start(ei[:, 1, :], A["dst"].rearrange("(p t) -> p t", p=EL)).then_inc(e_in, 16)
                for d, n in ((iota, "iota"), (triu, "triu"), (jt, "jtile")):
                    sp.dma_start(d[:, :], A[n]).then_inc(c_in, 16)
                sp.wait_ge(fill_done, 2)
                sp.dma_start(W["sorted"].rearrange("(p t) k -> p t k", p=P), fill[:, :, :]).then_inc(fill_out, 16)
                sp.wait_ge(tmi_done, 1)
                sp.dma_start(W["tmap"].rearrange("a (p c) -> p (a c)", p=P), tmi[:, :]).then_inc(tm_out, 16)
                sp.wait_ge(fill_out, 16)
                sp.wait_ge(tm_out, 16)

            @block.gpsimd
            def _(g):
                g.memset(ones[:, :], 1.0).then_inc(filled, 1)
                g.memset(zero[:, :], 0.0).then_inc(filled, 1)
                g.memset(fill[:, :, 0], ROWPAD).then_inc(fill_done, 1)
                g.memset(fill[:, :, 1], 0).then_inc(fill_done, 1)

            @block.vector
            def _(v):
                v.wait_ge(e_in, 32)
                v.wait_ge(c_in, 48)
                v.tensor_scalar(ti[:, 0, :], ei[:, 0, :], P - 1, None, ALU.bitwise_and).then_inc(bits, 1)
                v.tensor_scalar(ti[:, 1, :], ei[:, 0, :], 7, None, ALU.logical_shift_right).then_inc(bits, 1)
                v.tensor_copy(rc[:, :, :], ei[:, :, :].rearrange("p k t -> p t k")).then_inc(fields, 1)
                v.wait_ge(bits, 2)
                v.tensor_copy(lo[:, 0:ET], ti[:, 0, :]).then_inc(fields, 1)
                v.tensor_copy(hi[:, 0:ET], ti[:, 1, :]).then_inc(fields, 1)
                v.memset(lo[:, ET:], -1.0).then_inc(fields, 1)
                v.memset(hi[:, ET:], -1.0).then_inc(fields, 1)
                v.wait_ge(fields, 5)

                def onehots(i, x, first=False):
                    if not first:
                        v.wait_ge(counted, i - 1)
                    v.tensor_tensor(ohlo[:, x, :, :], bc(iota[0:EL, :].unsqueeze(1), [EL, SB_, P]),
                                    bc(lo[:, bass.ds(i * SB_, SB_)].unsqueeze(2), [EL, SB_, P]),
                                    ALU.is_equal).then_inc(oh, 1)
                    v.tensor_tensor(ohhi[:, x, :, :], bc(iota[0:EL, 0:NT].unsqueeze(1), [EL, SB_, NT]),
                                    bc(hi[:, bass.ds(i * SB_, SB_)].unsqueeze(2), [EL, SB_, NT]),
                                    ALU.is_equal).then_inc(ohh, 1)
                for i in range(3):
                    onehots(i, i % 2, first=(i < 2))
                with v.Fori(0, HB2 - 1) as k:
                    onehots(2 * k + 3, 1)
                    onehots(2 * k + 4, 0)
                v.wait_ge(counted, ET // SB_ + 1)
                v.tensor_copy(cnt[:, :], pcnt[:, :]).then_inc(cnt_done, 1)
                v.wait_ge(tot_ps, 2)
                v.tensor_copy(tot[:, :], ptot[:, :]).then_inc(tot_done, 1)
                v.wait_ge(tot_done, 1)
                v.tensor_scalar(tot2[:, :], tot[:, :], P - 1, None, ALU.add).then_inc(tot_done, 1)
                v.wait_ge(tot_done, 2)
                v.tensor_scalar(tot3[:, :], tot2[:, :], 7, None, ALU.logical_shift_right).then_inc(tot_done, 1)
                v.wait_ge(tot_done, 3)
                v.tensor_copy(tiles[:, :], tot3[:, :]).then_inc(tiles_done, 1)
                v.wait_ge(tiles_done, 1)
                v.wait_ge(filled, 2)
                v.tensor_tensor_scan(incl[:, :], zero[:, 0:NT], tiles[:, :], 0.0, ALU.add, ALU.add).then_inc(incl_done, 1)
                v.wait_ge(incl_done, 1)
                v.tensor_tensor(excl[:, :], incl[:, :], tiles[:, :], ALU.subtract).then_inc(excl_done, 1)
                v.wait_ge(excl_done, 1)
                v.scalar_tensor_tensor(out=pos_base[:, :], in0=excl[:, :], scalar=float(P), in1=pbef[:, :],
                                       op0=ALU.mult, op1=ALU.add).then_inc(base_done, 1)
                sh = [P, STM // P, NT]
                v.tensor_tensor(cmp[:, :, :], bc(incl[:, :].unsqueeze(1), sh), bc(jt[:, :].unsqueeze(2), sh),
                                ALU.is_le).then_inc(cmp_done, 1)
                v.wait_ge(cmp_done, 1)
                v.tensor_reduce(tmf[:, :], cmp[:, :, :], AX, ALU.add).then_inc(tmf_done, 1)
                v.wait_ge(tmf_done, 1)
                v.tensor_scalar(tmf[:, :], tmf[:, :], float(NT - 1), None, ALU.min).then_inc(tmf2_done, 1)
                v.wait_ge(tmf2_done, 1)
                v.tensor_copy(tmi[:, :], tmf[:, :]).then_inc(tmi_done, 1)

            @block.tensor
            def _(pe):
                pe.wait_ge(filled, 2)
                pe.matmul(pcnt[:, :], zero[:, :], zero[:, 0:NT], start=True, stop=False, skip_group_check=True)
                def count(i, x):
                    pe.wait_ge(oh, i + 1)
                    pe.wait_ge(ohh, i + 1)
                    for s in range(SB_):
                        m = pe.matmul(pcnt[:, :], ohlo[:, x, s, :], ohhi[:, x, s, :], start=False, stop=False,
                                      skip_group_check=True)
                    m.then_inc(counted, 1)
                count(0, 0)
                with pe.Fori(0, HB2) as k:
                    count(2 * k + 1, 1)
                    count(2 * k + 2, 0)
                pe.matmul(pcnt[:, 0:1], zero[:, :], zero[:, 0:1], start=False, stop=True,
                          skip_group_check=True).then_inc(counted, 1)
                pe.wait_ge(cnt_done, 1)
                pe.matmul(ptot[:, :], ones[:, :], cnt[:, :], start=True, stop=True).then_inc(tot_ps, 1)
                pe.matmul(pbef[:, :], triu[:, :], cnt[:, :], start=True, stop=True).then_inc(tot_ps, 1)


def sort_edges(nc, A, W, sem, ident, rc, lo, hi, pos_base):
    with ExitStack() as cx:
        def sb(n, s, d=F32):
            return cx.enter_context(nc.sbuf_tensor("s_" + n, s, d))

        def ps(n, s, d=F32):
            return cx.enter_context(nc.psum_tensor("s_" + n, s, d))
        iota = sb("iota", [P, P])
        triu = sb("triu", [P, P])
        idb = sb("idb", [P, P], BF16)
        ohlo = sb("ohlo", [EL, 2, SB_, P], BF16)
        ohhi = sb("ohhi", [EL, 2, SB_, NT], BF16)
        oht = sb("oht", [P, SB_, EL], BF16)
        ohtf = sb("ohtf", [P, SB_, EL])
        before = sb("before", [EL, SB_, EL], BF16)
        seen = sb("seen", [P, SB_, NT])
        picked = sb("picked", [EL, SB_, NT])
        posf = sb("posf", [EL, SB_])
        posi = sb("posi", [EL, 2, SB_], I32)
        rcs = sb("rcs", [EL, 2, SB_, 2], I32)
        pseen = ps("pseen", [P, 512])
        pt = ps("pt", [P, 16, P], BF16)
        plo = ps("plo", [P, 12, P])
        prank = ps("prank", [P, 512])
        c_in = sem("s_c_in")
        idb_done = sem("s_idb")
        oh = sem("s_onehots")
        turned = sem("s_turned")
        oht_done = sem("s_oht")
        ohtf_done = sem("s_ohtf")
        lo_ps = sem("s_lo_ps")
        bef_done = sem("s_before")
        snap = sem("s_snap")
        step = sem("s_step")
        rank = sem("s_rank")
        pick = sem("s_pick")
        pos = sem("s_pos")
        staged = sem("s_staged")
        landed = [sem(f"s_landed{x}") for x in range(2)]
        NB = ET // SB_
        rk = prank[0:EL, 0:SB_ * NT].rearrange("p (s t) -> p s t", s=SB_)
        with nc.Block() as block:
            @block.sync
            def _(sp):
                sp.dma_start(iota[:, :], A["iota"]).then_inc(c_in, 16)
                sp.dma_start(triu[:, :], A["triu"]).then_inc(c_in, 16)
                for x in range(2):
                    sp.wait_ge(landed[x], 16 * SB_ * ((NB + 1 - x) // 2))

            @block.vector
            def _(v):
                def onehots(i, x):
                    v.tensor_tensor(ohlo[:, x, :, :], bc(iota[0:EL, :].unsqueeze(1), [EL, SB_, P]),
                                    bc(lo[:, bass.ds(i * SB_, SB_)].unsqueeze(2), [EL, SB_, P]),
                                    ALU.is_equal).then_inc(oh, 1)
                    v.tensor_tensor(ohhi[:, x, :, :], bc(iota[0:EL, 0:NT].unsqueeze(1), [EL, SB_, NT]),
                                    bc(hi[:, bass.ds(i * SB_, SB_)].unsqueeze(2), [EL, SB_, NT]),
                                    ALU.is_equal).then_inc(oh, 1)

                def earlier(i):
                    v.wait_ge(lo_ps, i + 1)
                    v.tensor_tensor(before[:, :, :], plo[0:EL, 0:SB_, 0:EL], bc(triu[0:EL, 0:EL].unsqueeze(1), [EL, SB_, EL]),
                                    ALU.mult).then_inc(bef_done, 1)

                def batch(i, x, landings):
                    v.wait_ge(rank, i + 1)
                    v.tensor_tensor(picked[:, :, :], rk, ohhi[:, x, :, :], ALU.mult).then_inc(pick, 1)
                    v.wait_ge(pick, i + 1)
                    v.tensor_reduce(posf[:, :], picked[:, :, :], AX, ALU.add).then_inc(pos, 1)
                    v.wait_ge(pos, i + 1)
                    if landings is not None:
                        v.wait_ge(landed[x], 16 * SB_ * landings)
                    v.tensor_copy(posi[:, x, :], posf[:, :]).then_inc(staged, 1)
                    v.tensor_copy(rcs[:, x, :, :], rc[:, bass.ds(i * SB_, SB_), :]).then_inc(staged, 1)
                    onehots(i + 2, x)
                    earlier(i + 1)
                v.wait_ge(c_in, 32)
                v.tensor_copy(idb[:, :], ident[:, :]).then_inc(idb_done, 1)
                onehots(0, 0)
                onehots(1, 1)
                earlier(0)
                batch(0, 0, None)
                batch(1, 1, None)
                batch(2, 0, 1)
                with v.Fori(1, HB2) as k:
                    batch(2 * k + 1, 1, k)
                    batch(2 * k + 2, 0, k + 1)

            @block.scalar
            def _(a):
                def turned_copy(i):
                    a.wait_ge(turned, i + 1)
                    a.copy(oht[:, :, :], pt[:, 0:SB_, 0:EL]).then_inc(oht_done, 1)
                turned_copy(0)
                with a.Fori(0, NB) as i:
                    for s in range(SB_):
                        a.wait_ge(step, i * SB_ + s + 1)
                        a.copy(seen[:, s, :], pseen[:, 0:NT]).then_inc(snap, 1)
                        if s == 0:
                            a.copy(ohtf[:, :, :], pt[:, 0:SB_, 0:EL]).then_inc(ohtf_done, 1)
                    turned_copy(i + 1)

            @block.gpsimd
            def _(g):
                want = counter(g, "staged_want", 2)

                def scatter(x):
                    passed(g, staged, want, 2)
                    for s in range(SB_):
                        g.indirect_dma_start(W["sorted"], bass.IndirectOffsetOnAxis(ap=posi[:, x, s:s + 1], axis=0),
                                             rcs[:, x, s, :], None).then_inc(landed[x], 16)
                scatter(0)
                with g.Fori(0, HB2) as k:
                    scatter(1)
                    scatter(0)

            @block.tensor
            def _(pe):
                def turn(x, s):
                    return pe.transpose(pt[:, s, 0:EL], ohlo[:, x, s, :], idb[0:EL, 0:EL])

                def same_low(i):
                    pe.wait_ge(oht_done, i + 1)
                    for s in range(SB_):
                        m = pe.matmul(plo[0:EL, s, 0:EL], oht[:, s, :], oht[:, s, :], start=True, stop=True)
                    m.then_inc(lo_ps, 1)

                def batch(i, x, first=False):
                    for s in range(SB_):
                        pe.wait_ge(snap, i * SB_ + s + 1)
                        pe.matmul(pseen[:, 0:NT], ohlo[:, x, s, :], ohhi[:, x, s, :], start=False, stop=False,
                                  skip_group_check=True).then_inc(step, 1)
                        if s == 0:
                            pe.wait_ge(ohtf_done, i + 1)
                            if not first:
                                pe.wait_ge(pick, i)
                        pe.matmul(rk[:, s, :], ohtf[:, s, :], seen[:, s, :], start=(s == 0), stop=False,
                                  skip_group_check=True)
                        if s == 0:
                            pe.wait_ge(oh, 2 * i + 4)
                        t = turn(1 - x, s)
                    t.then_inc(turned, 1)
                    pe.wait_ge(bef_done, i + 1)
                    for s in range(SB_):
                        m = pe.matmul(rk[:, s, :], before[:, s, :], ohhi[:, x, s, :], start=False,
                                      stop=(s == SB_ - 1), skip_group_check=True)
                    m.then_inc(rank, 1)
                    same_low(i + 1)
                pe.wait_ge(idb_done, 1)
                pe.matmul(pseen[:, 0:NT], ident[:, :], pos_base[:, :], start=True, stop=False,
                          skip_group_check=True).then_inc(step, 1)
                pe.wait_ge(oh, 2)
                for s in range(SB_):
                    t = turn(0, s)
                t.then_inc(turned, 1)
                same_low(0)
                batch(0, 0, first=True)
                with pe.Fori(0, HB2) as k:
                    batch(2 * k + 1, 1)
                    batch(2 * k + 2, 0)


def load_sorted(nc, A, W, sem, ident, rowf, rowl, coli, tmap):
    LP = ST // 8
    with ExitStack() as cx:
        def sb(n, s, d=F32):
            return cx.enter_context(nc.sbuf_tensor("l_" + n, s, d))

        def ps(n, s, d=F32):
            return cx.enter_context(nc.psum_tensor("l_" + n, s, d))
        li = sb("li", [LP, 8, 2 * P], I32)
        lf = sb("lf", [LP, 2, 8, P])
        ri = sb("ri", [P, ST], I32)
        rl = sb("rl", [P, ST], I32)
        far = sb("far", [P, ST])
        rm = sb("rm", [P, ST])
        pr = ps("pr", [P, 8, P])
        pc = ps("pc", [P, 8, P])
        s_in = sem("l_in")
        lf_done = sem("l_lf")
        turned = sem("l_turned")
        ri_done = sem("l_ri")
        rl_done = sem("l_rl")
        rm_done = sem("l_rm")
        far_done = sem("l_far")
        end = sem("l_end")
        with nc.Block() as block:
            @block.sync
            def _(sp):
                sp.dma_start(li[:, :, :], W["sorted"].rearrange("(c p e) k -> p c (e k)", c=8, p=LP)).then_inc(s_in, 16)
                sp.dma_start(tmap[:, :], W["tmap"]).then_inc(s_in, 16)
                sp.wait_ge(s_in, 32)

            @block.vector
            def _(v):
                v.wait_ge(s_in, 32)
                for k in range(2):
                    v.tensor_copy(lf[:, k, :, :], li[:, :, :].rearrange("p c (e k) -> p c e k", k=2)[:, :, :, k]).then_inc(lf_done, 1)
                v.wait_ge(turned, 1)
                v.tensor_copy(rowf[:, :].rearrange("p (c n) -> p c n", c=8), pr[:, :, 0:LP]).then_inc(ri_done, 1)
                v.tensor_copy(ri[:, :].rearrange("p (c n) -> p c n", c=8), pr[:, :, 0:LP]).then_inc(ri_done, 1)
                v.tensor_copy(coli[:, 0:ST].rearrange("p (c n) -> p c n", c=8), pc[:, :, 0:LP]).then_inc(end, 1)
                v.memset(coli[:, ST:STX], 0).then_inc(end, 1)
                v.memset(rowl[:, ST:STX], 0.0).then_inc(end, 1)
                v.wait_ge(ri_done, 2)
                v.tensor_scalar(rl[:, :], ri[:, :], P - 1, None, ALU.bitwise_and).then_inc(rl_done, 1)
                v.tensor_scalar(far[:, :], rowf[:, :], float(N), 1000.0, ALU.is_ge, ALU.mult).then_inc(far_done, 1)
                v.wait_ge(rl_done, 1)
                v.tensor_copy(rm[:, :], rl[:, :]).then_inc(rm_done, 1)
                v.wait_ge(rm_done, 1)
                v.wait_ge(far_done, 1)
                v.tensor_tensor(rowl[:, 0:ST], rm[:, :], far[:, :], ALU.add).then_inc(end, 1)

            @block.tensor
            def _(pe):
                pe.wait_ge(lf_done, 2)
                for k, dst in ((0, pr), (1, pc)):
                    for c in range(8):
                        t = pe.transpose(dst[:, c, 0:LP], lf[:, k, c, :], ident[0:LP, 0:LP])
                t.then_inc(turned, 1)


def edge_scores(nc, A, W, sem, rowl, coli, tmap, q3, score):
    with ExitStack() as cx:
        def sb(n, s, d=F32):
            return cx.enter_context(nc.sbuf_tensor("e_" + n, s, d))

        def ps(n, s, d=F32):
            return cx.enter_context(nc.psum_tensor("e_" + n, s, d))
        iota = sb("iota", [P, P])
        idf = sb("idf", [P, P])
        idb = sb("idb", [P, P], BF16)
        oh = sb("oh", [P, RING, HB, P], BF16)
        oht = sb("oht", [P, 2, HB, P], BF16)
        kb = sb("kb", [P, RING, HB, C])
        prod = sb("prod", [P, HB, C])
        idx = sb("idx", [P, RING, HB], I32)
        pt = ps("pt", [P, 2, 1024], BF16)
        pq = ps("pq", [P, 2, HB, C])
        c_in = sem("e_c_in")
        idb_done = sem("e_idb")
        ohs = sem("e_onehots")
        turned = sem("e_turned")
        oht_done = sem("e_oht")
        q_picked = sem("e_q_picked")
        k_in = [sem(f"e_k_in{r}") for r in range(RING)]
        prod_done = sem("e_prod")
        score_done = sem("e_score")
        staged = sem("e_staged")
        with nc.Block() as block:
            @block.sync
            def _(sp):
                sp.dma_start(iota[:, :], A["iota"]).then_inc(c_in, 16)
                sp.dma_start(idf[:, :], A["ident"]).then_inc(c_in, 16)

            @block.gpsimd
            def _(g):
                want = counter(g, "e_staged_want", 1)
                with g.Fori(0, NHB // RING) as i:
                    for r in range(RING):
                        passed(g, staged, want, 1)
                        for s in range(HB):
                            g.indirect_dma_start(kb[:, r, s, :], None, W["k"],
                                                 bass.IndirectOffsetOnAxis(ap=idx[:, r, s:s + 1], axis=0))\
                             .then_inc(k_in[r], 16)

            @block.vector
            def _(v):
                sh = [P, HB, P]

                def onehot(hb, x):
                    v.tensor_tensor(oh[:, x, :, :], bc(iota[:, :].unsqueeze(1), sh),
                                    bc(rowl[:, bass.ds(hb * HB, HB)].unsqueeze(2), sh), ALU.is_equal).then_inc(ohs, 1)

                def stage(hb, r):
                    v.tensor_copy(idx[:, r, :], coli[:, bass.ds(hb * HB, HB)]).then_inc(staged, 1)

                def half(i, r, first=False):
                    hb = RING * i + r
                    v.wait_ge(q_picked, hb + 1)
                    v.wait_ge(k_in[r], 16 * HB * i + 16 * HB)
                    if not first:
                        v.wait_ge(score_done, hb)
                    v.tensor_tensor(prod[:, :, :], pq[:, r % 2, :, :], kb[:, r, :, :], ALU.mult).then_inc(prod_done, 1)
                    onehot(hb + RING - 1, (r + RING - 1) % RING)
                    v.wait_ge(prod_done, hb + 1)
                    stage(hb + RING, r)
                    v.tensor_reduce(score[:, bass.ds(hb * HB, HB), :],
                                    prod[:, :, :].rearrange("p s (d h) -> p s h d", h=H), AX, ALU.add)\
                     .then_inc(score_done, 1)

                for r in range(RING):
                    stage(r, r)
                v.wait_ge(c_in, 32)
                v.tensor_copy(idb[:, :], idf[:, :]).then_inc(idb_done, 1)
                for r in range(RING - 1):
                    onehot(r, r)
                for r in range(RING):
                    half(0, r, first=(r == 0))
                with v.Fori(1, NHB // RING) as i:
                    for r in range(RING):
                        half(i, r)

            @block.scalar
            def _(a):
                with a.Fori(0, NHB // 2) as i:
                    for x in range(2):
                        a.wait_ge(turned, 2 * i + x + 1)
                        a.copy(oht[:, x, :, :], pt[:, x, 0:HB * P].rearrange("p (s n) -> p s n", s=HB)).then_inc(oht_done, 1)
                a.wait_ge(turned, NHB + 1)

            @block.tensor
            def _(pe):
                pe.wait_ge(idb_done, 1)

                def turn(hb, r):
                    x = r % 2
                    pe.wait_ge(ohs, hb + 1)
                    for s in range(HB):
                        t = pe.transpose(pt[:, x, s * P:(s + 1) * P], oh[:, r, s, :], idb[:, :])
                    t.then_inc(turned, 1)

                def half(i, r, first=False):
                    hb = RING * i + r
                    x = r % 2
                    tiles = node_tiles(nc, mybir.EngineType.PE, tmap, hb)
                    turn(hb + 1, (r + 1) % RING)
                    pe.wait_ge(oht_done, hb + 1)
                    if not (first and r < 2):
                        pe.wait_ge(prod_done, hb - 1)
                    for s in range(HB):
                        for part in range(3):
                            m = pe.matmul(pq[:, x, s, :], oht[:, x, s, :],
                                          q3[:, bass.ds(tiles[s], 1), part, :],
                                          start=(part == 0), stop=(part == 2))
                    m.then_inc(q_picked, 1)

                turn(0, 0)
                for r in range(RING):
                    half(0, r, first=True)
                with pe.Fori(1, NHB // RING) as i:
                    for r in range(RING):
                        half(i, r)


def softmax_edges(nc, A, W, sem, ident, rowf, score):
    L = GPC * P
    G = 5
    with ExitStack() as cx:
        def sb(n, s, d=F32):
            return cx.enter_context(nc.sbuf_tensor("x_" + n, s, d))

        def ps(n, s, d=F32):
            return cx.enter_context(nc.psum_tensor("x_" + n, s, d))
        sT = sb("sT", [P, L])
        rT = sb("rT", [P, L])
        cut = sb("cut", [P, L + 1])
        fwd = sb("fwd", [P, L])
        both = rT
        st_s = sb("st_s", [P, G, CH, H])
        st_r = sb("st_r", [P, G, CH, H])
        pack = sb("pack", [P, 2, 3])
        ch = sb("ch", [H, 2, CH, 3])
        one = sb("one", [H, 2, CH])
        link = sb("link", [H, 2, CH])
        join = sb("join", [H, 2, CH])
        gate = sb("gate", [H, 2, CH])
        lnk = sb("lnk", [H, 2, CH])
        state = sb("state", [H, 2, CH])
        car = sb("car", [H, 2, CH])
        carry = sb("carry", [P, 2])
        p_s = ps("p_s", [P, G + 3, P])
        p_r = ps("p_r", [P, G + 3, P])
        rows_staged = sem("x_rows_staged")
        s_staged = sem("x_s_staged")
        turned = sem("x_turned")
        sT_done = sem("x_sT")
        rT_done = sem("x_rT")
        cut_done = sem("x_cut")
        fwd_done = sem("x_fwd")
        both_done = sem("x_both")
        packed = sem("x_packed")
        ends_out = sem("x_ends_out")
        ends_in = sem("x_ends_in")
        chain = sem("x_chain")
        carry_out = sem("x_carry_out")
        carry_in = sem("x_carry_in")
        diff = sem("x_diff")
        exp_done = sem("x_exp")
        staged2 = sem("x_staged2")
        turned2 = sem("x_turned2")
        back = sem("x_back")
        s_view = score[:, :, :].rearrange("p (c g) h -> p g c h", c=CH)
        r_view = rowf[:, :].rearrange("p (c g) -> p g c", c=CH)
        with nc.Block() as block:
            @block.sync
            def _(sp):
                for w in range(2):
                    sp.wait_ge(packed, 5 + w)
                    sp.dma_start(W["ends"][w], pack[:, w, :]).then_inc(ends_out, 16)
                    sp.wait_ge(ends_out, 16 * w + 16)
                    sp.dma_start(ch[:, w, :, :], W["ends"][w].rearrange("(c h) k -> h c k", h=H)).then_inc(ends_in, 16)
                    sp.wait_ge(chain, (w + 1) * CHAIN)
                    sp.dma_start(W["carry"][w].rearrange("c h -> h c"), car[:, w, :], allow_slow_non_contiguous=True).then_inc(carry_out, 16)
                    sp.wait_ge(carry_out, 16 * w + 16)
                    sp.dma_start(carry[:, w:w + 1], W["carry"][w].rearrange("c (h o) -> (c h) o", o=1)).then_inc(carry_in, 16)
                sp.wait_ge(carry_in, 32)

            @block.vector
            def _(v):
                shr = [P, G, CH, H]
                v.memset(st_r[:, 0, 0, :], 0.0).then_inc(turned, 1)
                v.wait_ge(turned, 1)
                with v.Fori(0, GPC // G) as i:
                    v.wait_ge(turned, i + 1)
                    v.tensor_copy(st_r[:, :, :, :], bc(r_view[:, bass.ds(i * G, G), :].unsqueeze(3), shr)).then_inc(rows_staged, 1)
                    v.wait_ge(turned, i + 2)
                    v.tensor_copy(rT[:, bass.ds(i * G * P, G * P)].rearrange("p (g e) -> p g e", g=G),
                                  p_r[:, 0:G, :]).then_inc(rT_done, 1)
                v.memset(cut[:, 0:1], 0.0).then_inc(cut_done, 1)
                v.memset(cut[:, L:L + 1], 0.0).then_inc(cut_done, 1)
                v.wait_ge(rT_done, GPC // G)
                v.tensor_tensor(cut[:, 1:L], rT[:, 1:L], rT[:, 0:L - 1], ALU.not_equal).then_inc(cut_done, 1)
                v.wait_ge(cut_done, 3)
                v.tensor_scalar(cut[:, 1:L], cut[:, 1:L], -BIG, None, ALU.mult).then_inc(cut_done, 1)
                for w in range(2):
                    v.tensor_copy(pack[:, w, 1:2], rT[:, 0:1]).then_inc(packed, 1)
                    v.tensor_copy(pack[:, w, 2:3], rT[:, L - 1:L]).then_inc(packed, 1)
                v.wait_ge(cut_done, 4)
                v.wait_ge(sT_done, GPC // G)

                def carries(w):
                    n = [w * CHAIN]

                    def then(ins):
                        n[0] += 1
                        ins.then_inc(chain, 1)
                        v.wait_ge(chain, n[0])
                    v.wait_ge(ends_in, 16 * w + 16)
                    then(v.tensor_tensor(one[:, w, :], ch[:, w, :, 1], ch[:, w, :, 2], ALU.is_equal))
                    then(v.memset(link[:, w, 0:1], 0.0))
                    then(v.tensor_tensor(link[:, w, 1:CH], ch[:, w, 1:CH, 1], ch[:, w, 0:CH - 1, 2], ALU.is_equal))
                    then(v.tensor_scalar(lnk[:, w, :], link[:, w, :], -1.0, BIG, ALU.add, ALU.mult))
                    then(v.memset(join[:, w, :], 0.0))
                    if w == 0:
                        then(v.tensor_tensor(join[:, w, :], one[:, w, :], link[:, w, :], ALU.mult))
                    else:
                        then(v.tensor_tensor(join[:, w, 0:CH - 1], one[:, w, 0:CH - 1], link[:, w, 1:CH], ALU.mult))
                    then(v.tensor_scalar(gate[:, w, :], join[:, w, :], -1.0, BIG, ALU.add, ALU.mult))
                    then(v.memset(car[:, w, :], -BIG))
                    if w == 0:
                        then(v.tensor_tensor_scan(state[:, w, :], gate[:, w, :], ch[:, w, :, 0], -BIG, ALU.add, ALU.max))
                        then(v.tensor_tensor(car[:, w, 1:CH], state[:, w, 0:CH - 1], lnk[:, w, 1:CH], ALU.add))
                    else:
                        then(v.tensor_tensor_scan(state[:, w, ::-1], gate[:, w, ::-1], ch[:, w, ::-1, 0], -BIG,
                                                  ALU.add, ALU.max))
                        then(v.tensor_tensor(car[:, w, 0:CH - 1], state[:, w, 1:CH], lnk[:, w, 1:CH], ALU.add))
                    assert n[0] == (w + 1) * CHAIN
                    v.wait_ge(carry_in, 16 * w + 16)

                v.tensor_tensor_scan(fwd[:, :], cut[:, 0:L], sT[:, :], -BIG, ALU.add, ALU.max).then_inc(fwd_done, 1)
                v.wait_ge(fwd_done, 1)
                v.tensor_copy(pack[:, 0, 0:1], fwd[:, L - 1:L]).then_inc(packed, 1)
                v.wait_ge(packed, 5)
                carries(0)
                v.tensor_tensor_scan(fwd[:, :], cut[:, 0:L], sT[:, :], carry[:, 0:1], ALU.add, ALU.max).then_inc(fwd_done, 1)
                v.wait_ge(fwd_done, 2)
                v.tensor_tensor_scan(both[:, ::-1], cut[:, L:0:-1], fwd[:, ::-1], -BIG, ALU.add, ALU.max).then_inc(both_done, 1)
                v.wait_ge(both_done, 1)
                v.tensor_copy(pack[:, 1, 0:1], both[:, 0:1]).then_inc(packed, 1)
                v.wait_ge(packed, 6)
                carries(1)
                v.tensor_tensor_scan(both[:, ::-1], cut[:, L:0:-1], fwd[:, ::-1], carry[:, 1:2], ALU.add, ALU.max).then_inc(both_done, 1)
                v.wait_ge(both_done, 2)
                v.tensor_tensor(sT[:, :], sT[:, :], both[:, :], ALU.subtract).then_inc(diff, 1)
                with v.Fori(0, GPC // G) as i:
                    v.wait_ge(turned2, i + 1)
                    v.tensor_copy(s_view[:, bass.ds(i * G, G), :, :],
                                  p_s[:, 0:G, :].rearrange("p g (c h) -> p g c h", h=H)).then_inc(back, 1)

            @block.scalar
            def _(a):
                with a.Fori(0, GPC // G) as i:
                    a.wait_ge(turned, i + 1)
                    a.copy(st_s[:, :, :, :], s_view[:, bass.ds(i * G, G), :, :]).then_inc(s_staged, 1)
                    a.wait_ge(turned, i + 2)
                    a.copy(sT[:, bass.ds(i * G * P, G * P)].rearrange("p (g e) -> p g e", g=G),
                           p_s[:, 0:G, :]).then_inc(sT_done, 1)
                a.wait_ge(diff, 1)
                a.activation(fwd[:, :], sT[:, :], ACT.Exp, scale=SCALE).then_inc(exp_done, 1)
                a.wait_ge(exp_done, 1)
                a.copy(st_s[:, :, :, :].rearrange("p g c h -> p g (c h)"),
                       fwd[:, 0:G * P].rearrange("p (g e) -> p g e", g=G)).then_inc(staged2, 1)
                with a.Fori(0, GPC // G - 1) as i:
                    a.wait_ge(turned2, i + 1)
                    a.copy(st_s[:, :, :, :].rearrange("p g c h -> p g (c h)"),
                           fwd[:, bass.ds((i + 1) * G * P, G * P)].rearrange("p (g e) -> p g e", g=G)).then_inc(staged2, 1)

            @block.tensor
            def _(pe):
                with pe.Fori(0, GPC // G) as i:
                    pe.wait_ge(s_staged, i + 1)
                    pe.wait_ge(rows_staged, i + 1)
                    for g in range(G):
                        pe.transpose(p_s[:, g, :], st_s[:, g, :, :].rearrange("p c h -> p (c h)"), ident[:, :])
                        t = pe.transpose(p_r[:, g, :], st_r[:, g, :, :].rearrange("p c h -> p (c h)"), ident[:, :])
                    t.then_inc(turned, 1)
                    pe.wait_ge(sT_done, i + 1)
                    pe.wait_ge(rT_done, i + 1)
                with pe.Fori(0, GPC // G) as i:
                    pe.wait_ge(staged2, i + 1)
                    for g in range(G):
                        t = pe.transpose(p_s[:, g, :], st_s[:, g, :, :].rearrange("p c h -> p (c h)"), ident[:, :])
                    t.then_inc(turned2, 1)
                    pe.wait_ge(back, i + 1)


CHAIN = 10


def aggregate(nc, A, W, sem, rowl, coli, tmap, score, acc):
    with ExitStack() as cx:
        def sb(n, s, d=F32):
            return cx.enter_context(nc.sbuf_tensor("g_" + n, s, d))

        def ps(n, s, d=F32):
            return cx.enter_context(nc.psum_tensor("g_" + n, s, d))
        iota = sb("iota", [P, P])
        oh = sb("oh", [P, 2, HB, P])
        vb = sb("vb", [P, RING, HB, C])
        w = sb("w", [P, 2, HB, C + H])
        idx = sb("idx", [P, RING, HB], I32)
        pa = ps("pa", [P, 2, HB, 512])
        c_in = sem("g_c_in")
        zeroed = sem("g_zeroed")
        ohs = sem("g_onehots")
        v_in = [sem(f"g_v_in{r}") for r in range(RING)]
        staged = sem("g_staged")
        weighted = sem("g_weighted")
        p_put = sem("g_p_put")
        summed = sem("g_summed")
        acc_done = sem("g_acc")
        with nc.Block() as block:
            @block.sync
            def _(sp):
                sp.dma_start(iota[:, :], A["iota"]).then_inc(c_in, 16)

            @block.gpsimd
            def _(g):
                want = counter(g, "g_staged_want", 1)
                with g.Fori(0, NHB // RING) as i:
                    for r in range(RING):
                        passed(g, staged, want, 1)
                        for s in range(HB):
                            g.indirect_dma_start(vb[:, r, s, :], None, W["v"],
                                                 bass.IndirectOffsetOnAxis(ap=idx[:, r, s:s + 1], axis=0))\
                             .then_inc(v_in[r], 16)

            @block.scalar
            def _(a):
                def put(i, x, first=False):
                    hb = 2 * i + x
                    if not first:
                        a.wait_ge(summed, HB * (hb - 1))
                    a.copy(w[:, x, :, C:C + H], score[:, bass.ds(hb * HB, HB), :]).then_inc(p_put, 1)
                for x in range(2):
                    put(0, x, first=True)
                with a.Fori(1, NHB // 2) as i:
                    for x in range(2):
                        put(i, x)

            @block.vector
            def _(v):
                def onehot(hb, x, s):
                    v.tensor_scalar(oh[:, x, s, :], iota[:, :], rowl[:, bass.ds(hb * HB + s, 1)], None,
                                    ALU.is_equal).then_inc(ohs, 1)

                def stage(hb, r):
                    v.tensor_copy(idx[:, r, :], coli[:, bass.ds(hb * HB, HB)]).then_inc(staged, 1)

                def weight(hb, r):
                    v.tensor_tensor(w[:, r % 2, :, 0:C].rearrange("p s (d h) -> p s d h", h=H),
                                    vb[:, r, :, :].rearrange("p s (d h) -> p s d h", h=H),
                                    bc(score[:, bass.ds(hb * HB, HB), :].unsqueeze(2), [P, HB, D, H]), ALU.mult)\
                     .then_inc(weighted, 1)

                def add(hb, x, s, tiles, first=False):
                    v.wait_ge(summed, HB * hb + s + 1)
                    if not first:
                        v.wait_ge(acc_done, HB * hb + s)
                    at = acc[:, bass.ds(tiles[s], 1), :]
                    v.tensor_tensor(at, at, pa[:, x, s, 0:C + H].unsqueeze(1), ALU.add).then_inc(acc_done, 1)

                def half(i, r, first=False):
                    hb = RING * i + r
                    v.wait_ge(v_in[r], 16 * HB * i + 16 * HB)
                    weight(hb, r)
                    late = not (first and r == 0)
                    tiles = node_tiles(nc, mybir.EngineType.DVE, tmap, hb - 1) if late else None
                    for s in range(HB):
                        if late:
                            add(hb - 1, 1 - r % 2, s, tiles, first and r == 1 and s == 0)
                        if s == 0:
                            v.wait_ge(weighted, hb + 1)
                            stage(hb + RING, r)
                        onehot(hb + 1, 1 - r % 2, s)

                for r in range(RING):
                    stage(r, r)
                v.memset(acc[:, :, :], 0.0).then_inc(zeroed, 1)
                v.wait_ge(c_in, 16)
                for s in range(HB):
                    onehot(0, 0, s)
                v.wait_ge(zeroed, 1)
                for r in range(RING):
                    half(0, r, first=True)
                with v.Fori(1, NHB // RING) as i:
                    for r in range(RING):
                        half(i, r)
                tiles = node_tiles(nc, mybir.EngineType.DVE, tmap, NHB - 1)
                for s in range(HB):
                    add(NHB - 1, 1, s, tiles)
                v.wait_ge(acc_done, HB * NHB)

            @block.tensor
            def _(pe):
                def half(i, x, first=False):
                    hb = 2 * i + x
                    pe.wait_ge(p_put, hb + 1)
                    if not first:
                        pe.wait_ge(acc_done, HB * (hb - 1))
                    pe.wait_ge(ohs, HB * hb + HB)
                    pe.wait_ge(weighted, hb + 1)
                    for s in range(HB):
                        pe.matmul(pa[:, x, s, 0:C + H], oh[:, x, s, :], w[:, x, s, :], start=True, stop=True).then_inc(summed, 1)
                for x in range(2):
                    half(0, x, first=True)
                with pe.Fori(1, NHB // 2) as i:
                    for x in range(2):
                        half(i, x)


def combine(nc, A, W, sem, ident, ctxbd, acc, first, second):
    with ExitStack() as cx:
        def sb(n, s, d=F32):
            return cx.enter_context(nc.sbuf_tensor("c_" + n, s, d))

        def ps(n, s, d=F32):
            return cx.enter_context(nc.psum_tensor("c_" + n, s, d))
        wqm = sb("wqm", [P, KC, C])
        wpr = sb("wpr", [P, KC, C])
        wo = sb("wo", [P, KC, C])
        wg1 = sb("wg1", [P, KC, GH])
        wg2 = sb("wg2", [GH, C])
        bg1 = sb("bg1", [GH, 1])
        bg2 = sb("bg2", [P, KC])
        bo = sb("bo", [P, C])
        bpr = sb("bpr", [P, C])
        wgt = sb("wgt", [P, KC, NEXP])
        bgt = sb("bgt", [P, NEXP])
        iota = sb("iota", [P, NEXP])
        bsum = sb("bsum", [P, C])
        xnT = sb("xnT", [P, KC, GN])
        xmT = sb("xmT", [P, KC, GN])
        xg = sb("xg", [P, TPG, C])
        qmT = sb("qmT", [P, KC, GN])
        hgT = sb("hgT", [GH, GN])
        gT = sb("gT", [P, KC, GN])
        prT = sb("prT", [P, KC, GN])
        z = sb("z", [P, TPG, H])
        rz = sb("rz", [P, TPG, H])
        gn = sb("gn", [P, TPG, C])
        gnT = sb("gnT", [P, KC, GN])
        xb = sb("xb", [P, TPG, C])
        x2 = sb("x2", [P, TPG, C])
        st = sb("st", [P, TPG, 6])
        mv = sb("mv", [P, TPG, 2])
        ve = sb("ve", [P, TPG])
        sd = sb("sd", [P, TPG])
        rs = sb("rs", [P, TPG])
        xl = sb("xl", [P, TPG, C])
        xlT = sb("xlT", [P, KC, GN])
        gs = sb("gs", [P, TPG, NEXP])
        top = sb("top", [P, TPG, 8])
        tidx = sb("tidx", [P, TPG, 8], U32)
        tif = sb("tif", [P, TPG, 8])
        zero = sb("zero", [P, XROWS // P, C])
        pA = ps("pA", [P, KC, GN])
        pB = ps("pB", [P, KC, GN])
        pH = ps("pH", [P, GN])
        pD = ps("pD", [P, KC, GN])
        names = ["w_in", "x_in", "bsum_done", "qm_ps", "qm_done", "o_ps", "hg_ps", "hg_done", "g_ps", "g_done", "pr_done",
                 "z_done", "rz_done", "gn_done", "gn_turned", "gnT_done", "y_ps", "xb_done", "x2_done", "stats", "aggr", "var",
                 "std", "rstd", "xl_done", "xl_turned", "xlT_done", "gs_ps", "gs_done", "top_done", "tidx_done", "tif_done",
                 "m1_done", "m2_done", "stored", "zero_done", "xs_filled"]
        s = {n: sem("c_" + n) for n in names}
        wnames = [(wqm, "wqm"), (wpr, "wpr"), (wo, "wo"), (wg1, "wg1"), (wg2, "wg2"), (bg1, "bg1"), (bg2, "bg2"), (bo, "bo"),
                  (bpr, "bpr"), (wgt, "wgt"), (bgt, "bgt"), (iota, "iota8")]
        with nc.Block() as block:
            @block.sync
            def _(sp):
                for dst, n in wnames:
                    full = dst[:, :, :] if len(dst.shape) == 3 else dst[:, :]
                    sp.dma_start(full, A[n]).then_inc(s["w_in"], 16)

                def load(i):
                    sp.dma_start(xnT[:, :, :], W["xnT"][:, :, bass.ds(i * GN, GN)]).then_inc(s["x_in"], 16)
                    sp.dma_start(xmT[:, :, :], W["xmT"][:, :, bass.ds(i * GN, GN)]).then_inc(s["x_in"], 16)
                    sp.dma_start(xg[:, :, :], rows(A["x"], i)).then_inc(s["x_in"], 16)

                def store(i):
                    sp.wait_ge(s["x2_done"], TPG * i + TPG)
                    sp.wait_ge(s["xl_done"], TPG * i + TPG)
                    sp.dma_start(rows(W["x2"], i), x2[:, :, :]).then_inc(s["stored"], 16)
                    sp.dma_start(rows(W["xl"], i), xl[:, :, :]).then_inc(s["stored"], 16)
                load(0)
                sp.wait_ge(s["zero_done"], 1)
                for n in range(XFILL):
                    sp.dma_start(W["xs"][n * XROWS:(n + 1) * XROWS, :].rearrange("(p t) c -> p t c", p=P),
                                 zero[:, :, :]).then_inc(s["xs_filled"], 16)
                with sp.Fori(0, NG - 1) as i:
                    sp.wait_ge(s["hg_ps"], i + 1)
                    sp.wait_ge(s["xb_done"], i + 1)
                    load(i + 1)
                    store(i)
                store(NG - 1)
                sp.wait_ge(s["stored"], 32 * NG + 32)
                sp.wait_ge(s["xs_filled"], 16 * XFILL)

            @block.vector
            def _(v):
                v.wait_ge(s["w_in"], 16 * len(wnames))
                v.tensor_tensor(bsum[:, :], bo[:, :], bpr[:, :], ALU.add).then_inc(s["bsum_done"], 1)
                v.wait_ge(s["bsum_done"], 1)
                v.memset(x2[:, 0, 0:1], 0.0).then_inc(s["stored"], 32)
                v.wait_ge(s["stored"], 32)
                want_stats = counter(v, "x2_stats_want", TPG)
                want_gs = counter(v, "scores_want", 1)
                want_top = counter(v, "top_want", TPG)
                with v.Fori(0, NG) as i:
                    ga = acc[:, bass.ds(i * TPG, TPG), :]
                    v.tensor_scalar(z[:, :, :], ga[:, :, C:C + H], 1e-30, None, ALU.max).then_inc(s["z_done"], 1)
                    v.wait_ge(s["z_done"], i + 1)
                    v.reciprocal(rz[:, :, :], z[:, :, :]).then_inc(s["rz_done"], 1)
                    v.wait_ge(s["rz_done"], i + 1)
                    for j in range(TPG):
                        v.tensor_tensor(gn[:, j, :].rearrange("p (d h) -> p d h", h=H),
                                        acc[:, bass.ds(i * TPG + j, 1), 0:C].rearrange("p o (d h) -> p (o d) h", h=H),
                                        bc(rz[:, j, :].unsqueeze(1), [P, D, H]), ALU.mult).then_inc(s["gn_done"], 1)
                    v.wait_ge(s["x_in"], 48 * i + 48)
                    v.tensor_tensor(xb[:, :, :], xg[:, :, :], bc(bsum[:, :].unsqueeze(1), [P, TPG, C]), ALU.add)\
                     .then_inc(s["xb_done"], 1)
                    v.wait_ge(s["qm_ps"], i + 1)
                    v.tensor_copy(qmT[:, :, :], pA[:, :, :]).then_inc(s["qm_done"], 1)
                    v.wait_ge(s["o_ps"], i + 1)
                    v.wait_ge(s["g_done"], KC * i + KC)
                    v.tensor_tensor(prT[:, :, :], pB[:, :, :], gT[:, :, :], ALU.mult).then_inc(s["pr_done"], 1)
                    v.wait_ge(s["xb_done"], i + 1)
                    v.wait_ge(s["stored"], 32 * i + 32)
                    v.wait_ge(s["y_ps"], i + 1)
                    for j in range(TPG):
                        v.tensor_tensor(x2[:, j, :], xb[:, j, :], pD[:, j // 2, (j % 2) * C:(j % 2 + 1) * C], ALU.add)\
                         .then_inc(s["x2_done"], 1)
                    for j in range(TPG):
                        v.wait_ge(s["x2_done"], TPG * i + j + 1)
                        v.bn_stats(st[:, j, :], x2[:, j, :]).then_inc(s["stats"], 1)
                    passed(v, s["stats"], want_stats, TPG)
                    for j in range(TPG):
                        v.bn_aggr(mv[:, j, :], st[:, j, :]).then_inc(s["aggr"], 1)
                    v.wait_ge(s["aggr"], TPG * i + TPG)
                    v.tensor_scalar(ve[:, :], mv[:, :, 1], EPS, None, ALU.add).then_inc(s["var"], 1)
                    v.wait_ge(s["std"], i + 1)
                    v.reciprocal(rs[:, :], sd[:, :]).then_inc(s["rstd"], 1)
                    v.wait_ge(s["rstd"], i + 1)
                    for j in range(TPG):
                        v.tensor_scalar(xl[:, j, :], x2[:, j, :], mv[:, j, 0:1], rs[:, j:j + 1],
                                        ALU.subtract, ALU.mult).then_inc(s["xl_done"], 1)
                    v.wait_ge(s["gs_ps"], i + 1)
                    v.tensor_tensor(gs[:, :, :], pH[:, 0:TPG * NEXP].rearrange("p (j e) -> p j e", j=TPG),
                                    bc(bgt[:, :].unsqueeze(1), [P, TPG, NEXP]), ALU.add).then_inc(s["gs_done"], 1)
                    passed(v, s["gs_done"], want_gs, 1)
                    for j in range(TPG):
                        v.max(top[:, j, :], gs[:, j, :]).then_inc(s["top_done"], 1)
                    passed(v, s["top_done"], want_top, TPG)
                    for j in range(TPG):
                        v.max_index(tidx[:, j, :], top[:, j, :], gs[:, j, :]).then_inc(s["tidx_done"], 1)
                    v.wait_ge(s["tidx_done"], TPG * i + TPG)
                    v.tensor_copy(tif[:, :, :], tidx[:, :, :]).then_inc(s["tif_done"], 1)
                    v.wait_ge(s["tif_done"], i + 1)
                    sh = [P, TPG, NEXP]
                    v.tensor_tensor(first[:, bass.ds(i * TPG, TPG), :], bc(iota[:, :].unsqueeze(1), sh), bc(tif[:, :, 0:1], sh), ALU.is_equal).then_inc(s["m1_done"], 1)
                    v.tensor_tensor(second[:, bass.ds(i * TPG, TPG), :], bc(iota[:, :].unsqueeze(1), sh), bc(tif[:, :, 1:2], sh), ALU.is_equal).then_inc(s["m2_done"], 1)
                    v.wait_ge(s["m1_done"], i + 1)
                    v.wait_ge(s["m2_done"], i + 1)

            @block.gpsimd
            def _(g):
                g.memset(zero[:, :, :], 0.0).then_inc(s["zero_done"], 1)

            @block.scalar
            def _(a):
                a.wait_ge(s["w_in"], 16 * len(wnames))
                with a.Fori(0, NG) as i:
                    a.wait_ge(s["gn_turned"], i + 1)
                    a.copy(gnT[:, :, :], pD[:, :, :]).then_inc(s["gnT_done"], 1)
                    a.wait_ge(s["hg_ps"], i + 1)
                    a.activation(hgT[:, :], pH[0:GH, :], ACT.Gelu, bias=bg1[:, 0:1]).then_inc(s["hg_done"], 1)
                    a.wait_ge(s["g_ps"], i + 1)
                    for k in range(KC):
                        a.activation(gT[:, k, :], pD[:, k, :], ACT.Sigmoid, bias=bg2[:, k:k + 1]).then_inc(s["g_done"], 1)
                    a.wait_ge(s["var"], i + 1)
                    a.activation(sd[:, :], ve[:, :], ACT.Sqrt).then_inc(s["std"], 1)
                    a.wait_ge(s["xl_turned"], i + 1)
                    a.copy(xlT[:, :, :], pB[:, :, :]).then_inc(s["xlT_done"], 1)

            @block.tensor
            def _(pe):
                pe.wait_ge(s["w_in"], 16 * len(wnames))
                with pe.Fori(0, NG) as i:
                    pe.wait_ge(s["x_in"], 48 * i + 48)
                    for m in range(KC):
                        for k in range(KC):
                            t = pe.matmul(pA[:, m, :], wqm[:, k, m * P:(m + 1) * P], xnT[:, k, :], start=(k == 0), stop=(k == KC - 1))
                    t.then_inc(s["qm_ps"], 1)
                    pe.wait_ge(s["gn_done"], TPG * i + TPG)
                    for j in range(TPG):
                        for k in range(KC):
                            t = pe.transpose(pD[:, k, j * P:(j + 1) * P], gn[:, j, k * P:(k + 1) * P], ident[:, :])
                    t.then_inc(s["gn_turned"], 1)
                    for k in range(KC):
                        t = pe.matmul(pH[0:GH, :], wg1[:, k, :], xmT[:, k, :], start=(k == 0), stop=(k == KC - 1))
                    t.then_inc(s["hg_ps"], 1)
                    pe.wait_ge(s["qm_done"], i + 1)
                    for m in range(KC):
                        for k in range(KC):
                            t = pe.matmul(pB[:, m, :], ctxbd[:, k, m * P:(m + 1) * P], qmT[:, k, :], start=(k == 0), stop=(k == KC - 1))
                    t.then_inc(s["o_ps"], 1)
                    pe.wait_ge(s["hg_done"], i + 1)
                    pe.wait_ge(s["gnT_done"], i + 1)
                    for m in range(KC):
                        t = pe.matmul(pD[:, m, :], wg2[:, m * P:(m + 1) * P], hgT[:, :], start=True, stop=True)
                    t.then_inc(s["g_ps"], 1)
                    pe.wait_ge(s["pr_done"], i + 1)
                    pe.wait_ge(s["g_done"], KC * i + KC)
                    for j in range(TPG):
                        o = pD[:, j // 2, (j % 2) * C:(j % 2 + 1) * C]
                        for k in range(KC):
                            pe.matmul(o, prT[:, k, j * P:(j + 1) * P], wpr[:, k, :], start=(k == 0), stop=False)
                        for k in range(KC):
                            t = pe.matmul(o, gnT[:, k, j * P:(j + 1) * P], wo[:, k, :], start=False, stop=(k == KC - 1))
                    t.then_inc(s["y_ps"], 1)
                    pe.wait_ge(s["xl_done"], TPG * i + TPG)
                    for j in range(TPG):
                        for k in range(KC):
                            t = pe.transpose(pB[:, k, j * P:(j + 1) * P], xl[:, j, k * P:(k + 1) * P], ident[:, :])
                    t.then_inc(s["xl_turned"], 1)
                    pe.wait_ge(s["xlT_done"], i + 1)
                    for j in range(TPG):
                        for k in range(KC):
                            t = pe.matmul(pH[:, j * NEXP:(j + 1) * NEXP], xlT[:, k, j * P:(j + 1) * P], wgt[:, k, :],
                                          start=(k == 0), stop=(k == KC - 1))
                    t.then_inc(s["gs_ps"], 1)
                    pe.wait_ge(s["gs_done"], i + 1)


def route(nc, A, W, sem, ident, first, second, slot_i, slot_g, emap):
    TE = NT * NEXP
    with ExitStack() as cx:
        def sb(n, s, d=F32):
            return cx.enter_context(nc.sbuf_tensor("r_" + n, s, d))

        def ps(n, s, d=F32):
            return cx.enter_context(nc.psum_tensor("r_" + n, s, d))
        valid = sb("valid", [P, NT])
        dump = sb("dump", [P, 2, NT])
        triu = sb("triu", [P, P])
        jcol = sb("jcol", [P, 1])
        ones = sb("ones", [P, P])
        zero = sb("zero", [P, NT])
        pick = sb("pick", [P, 2, NT, NEXP])
        both = sb("both", [P, NT, NEXP])
        incl = sb("incl", [P, NT, NEXP])
        tot = sb("tot", [P, NT, NEXP])
        t1 = sb("t1", [P, NEXP], I32)
        t2 = sb("t2", [P, NEXP], I32)
        t3 = sb("t3", [P, NEXP], I32)
        tiles = sb("tiles", [P, NEXP])
        tincl = sb("tincl", [P, NEXP])
        base = sb("base", [P, NEXP])
        at0 = sb("at0", [P, NT, NEXP])
        at1 = sb("at1", [P, NT, NEXP])
        at = sb("at", [P, NT, NEXP])
        own = sb("own", [P, 2, NT, NEXP])
        slot = sb("slot", [P, 2, NT])
        slotd = sb("slotd", [P, 2, NT])
        cmp = sb("cmp", [P, NEXP])
        ecol = sb("ecol", [P, 1])
        ecol2 = sb("ecol2", [P, 1])
        ecoli = sb("ecoli", [P, 1], I32)
        xr = sb("xr", [P, 2, RT, C])
        ix = sb("ix", [P, 2, RT, 2], I32)
        pw = ps("pw", [P, TE])
        pt = ps("pt", [P, TE])
        c_in = sem("r_c_in")
        filled = sem("r_filled")
        step = sem("r_step")
        counted = sem("r_counted")
        e_out = sem("r_e_out")
        x_in = [sem(f"r_x_in{x}") for x in range(2)]
        staged = sem("r_staged")
        landed = [sem(f"r_landed{x}") for x in range(2)]
        NI = NT // RT
        with nc.Block() as block:
            @block.sync
            def _(sp):
                for d, n in ((valid[:, :], "valid"), (dump[:, :, :], "dump"), (triu[:, :], "triu"), (jcol[:, :], "jcol")):
                    sp.dma_start(d, A[n]).then_inc(c_in, 16)

                def load(i, x):
                    sp.dma_start(xr[:, x, :, :], W["xl"][bass.ds(i * RT * P, RT * P), :].rearrange("(j p) c -> p j c", p=P))\
                      .then_inc(x_in[x], 16)
                for x in range(2):
                    load(x, x)
                sp.wait_ge(step, ROUTE_STEPS)
                sp.dma_start(W["emap"].rearrange("a (p o) -> p (a o)", o=1), ecoli[:, :]).then_inc(e_out, 16)
                sp.wait_ge(e_out, 16)
                sp.dma_start(emap[:, :], W["emap"]).then_inc(e_out, 16)
                for i in range(2, NI):
                    sp.wait_ge(landed[i % 2], 16 * 2 * RT * (i // 2))
                    load(i, i % 2)
                for x in range(2):
                    sp.wait_ge(landed[x], 16 * 2 * RT * ((NI - x + 1) // 2))
                sp.wait_ge(e_out, 32)

            @block.vector
            def _(v):
                n = [0]

                def then(ins):
                    n[0] += 1
                    ins.then_inc(step, 1)
                    v.wait_ge(step, n[0])
                v.wait_ge(c_in, 64)
                sh = [P, NT, NEXP]
                for w, m in ((0, first), (1, second)):
                    then(v.tensor_tensor(pick[:, w, :, :], m[:, 0:NT, :], bc(valid[:, :].unsqueeze(2), sh), ALU.mult))
                then(v.tensor_tensor(both[:, :, :], pick[:, 0, :, :], pick[:, 1, :, :], ALU.add))
                then(v.memset(zero[:, :], 0.0))
                v.wait_ge(counted, 2)
                then(v.tensor_copy(tot[:, :, :], pt[:, :].rearrange("p (t e) -> p t e", e=NEXP)))
                for e in range(NEXP):
                    then(v.tensor_tensor_scan(incl[:, :, e], zero[:, :], tot[:, :, e], 0.0, ALU.add, ALU.add))
                then(v.tensor_copy(t1[:, :], incl[:, NT - 1, :]))
                then(v.tensor_scalar(t2[:, :], t1[:, :], P - 1, None, ALU.add))
                then(v.tensor_scalar(t3[:, :], t2[:, :], 7, None, ALU.logical_shift_right))
                then(v.tensor_copy(tiles[:, :], t3[:, :]))
                then(v.tensor_tensor_scan(tincl[:, :], zero[:, 0:NEXP], tiles[:, :], 0.0, ALU.add, ALU.add))
                then(v.tensor_tensor(base[:, :], tincl[:, :], tiles[:, :], ALU.subtract))
                then(v.tensor_tensor(cmp[:, :], tincl[:, :], bc(jcol[:, :], [P, NEXP]), ALU.is_le))
                then(v.tensor_reduce(ecol[:, :], cmp[:, :], AX, ALU.add))
                then(v.tensor_scalar(ecol2[:, :], ecol[:, :], float(NEXP - 1), None, ALU.min))
                then(v.tensor_copy(ecoli[:, :], ecol2[:, :]))
                assert n[0] == ROUTE_STEPS
                then(v.tensor_tensor(at0[:, :, :], incl[:, :, :], tot[:, :, :], ALU.subtract))
                then(v.tensor_tensor(at1[:, :, :], at0[:, :, :], pw[:, :].rearrange("p (t e) -> p t e", e=NEXP), ALU.add))
                then(v.scalar_tensor_tensor(out=at[:, :, :], in0=bc(base[:, :].unsqueeze(1), sh), scalar=float(P),
                                            in1=at1[:, :, :], op0=ALU.mult, op1=ALU.add))
                for w in range(2):
                    then(v.tensor_tensor(own[:, w, :, :], pick[:, w, :, :], at[:, :, :], ALU.mult))
                    then(v.tensor_reduce(slot[:, w, :], own[:, w, :, :], AX, ALU.add))
                then(v.tensor_tensor(slotd[:, :, :], slot[:, :, :], dump[:, :, :], ALU.add))
                then(v.tensor_copy(slot_i[:, :, :], slotd[:, :, :]))
                then(v.memset(slot_g[:, :, :], 0))
                then(v.tensor_copy(slot_g[:, :, 0:NT], slot[:, :, :]))
                for i in range(NI):
                    if i >= 2:
                        v.wait_ge(landed[i % 2], 16 * 2 * RT * (i // 2))
                    v.tensor_copy(ix[:, i % 2, :, :], slot_i[:, :, i * RT:(i + 1) * RT].rearrange("p w t -> p t w")).then_inc(staged, 1)

            @block.gpsimd
            def _(g):
                g.memset(ones[:, :], 1.0).then_inc(filled, 1)
                for i in range(NI):
                    x = i % 2
                    g.wait_ge(staged, i + 1)
                    g.wait_ge(x_in[x], 16 * (i // 2 + 1))
                    for s in range(RT):
                        for w in range(2):
                            g.indirect_dma_start(W["xs"], bass.IndirectOffsetOnAxis(ap=ix[:, x, s, w:w + 1], axis=0),
                                                 xr[:, x, s, :], None).then_inc(landed[x], 16)

            @block.tensor
            def _(pe):
                pe.wait_ge(filled, 1)
                pe.wait_ge(step, 3)
                m = both[:, :, :].rearrange("p t e -> p (t e)")
                pe.matmul(pw[:, :], triu[:, :], m, start=True, stop=True).then_inc(counted, 1)
                pe.matmul(pt[:, :], ones[:, :], m, start=True, stop=True).then_inc(counted, 1)


ROUTE_STEPS = 23
RT = 7
assert NT % RT == 0


def experts(nc, A, W, sem, ident, emap):
    with ExitStack() as cx:
        def sb(n, s, d=F32):
            return cx.enter_context(nc.sbuf_tensor("f_" + n, s, d))

        def ps(n, s, d=F32):
            return cx.enter_context(nc.psum_tensor("f_" + n, s, d))
        w1 = sb("w1", [P, KC, NEXP, HID])
        w2 = sb("w2", [P, HC, NEXP, C])
        b1 = sb("b1", [P, NEXP, HID])
        b2 = sb("b2", [P, NEXP, C])
        x = sb("x", [P, XR, C])
        xT = sb("xT", [P, 2, KC, P])
        hb = sb("hb", [P, 2, HID])
        h = sb("h", [P, 2, HID])
        hT = sb("hT", [P, 2, HC, P])
        y = sb("y", [P, XR, C])
        px = ps("px", [P, 2, 512])
        ph = ps("ph", [P, 2, HID])
        pt = ps("pt", [P, 2, HC, P])
        py = ps("py", [P, 2, 512])
        w_in = sem("f_w_in")
        x_in = [sem(f"f_x_in{r}") for r in range(XR)]
        x_turned = sem("f_x_turned")
        xT_done = sem("f_xT")
        up_ps = sem("f_up")
        b_done = sem("f_biased")
        h_done = sem("f_h")
        h_turned = sem("f_h_turned")
        hT_done = sem("f_hT")
        down_ps = sem("f_down")
        y_done = sem("f_y")
        stored = [sem(f"f_stored{r}") for r in range(XR)]
        with nc.Block() as block:
            @block.sync
            def _(sp):
                for d, n in ((w1, "w1"), (w2, "w2")):
                    sp.dma_start(d[:, :, :, :], A[n]).then_inc(w_in, 16)
                for d, n in ((b1, "b1"), (b2, "b2")):
                    sp.dma_start(d[:, :, :], A[n]).then_inc(w_in, 16)

                def load(t, r):
                    sp.dma_start(x[:, r, :], W["xs"][bass.ds(t * P, P), :]).then_inc(x_in[r], 16)
                for r in range(XR):
                    load(r, r)
                with sp.Fori(0, EXT // XR) as i:
                    for r in range(XR):
                        t = XR * i + r
                        sp.wait_ge(x_turned, t + 1)
                        load(t + XR, r)
                        sp.wait_ge(y_done, t + 1)
                        sp.dma_start(W["ys"][bass.ds(t * P, P), :], y[:, r, :]).then_inc(stored[r], 16)
                for r in range(XR):
                    sp.wait_ge(stored[r], 16 * (EXT // XR))
                    sp.wait_ge(x_in[r], 16 * (EXT // XR + 1))

            @block.vector
            def _(v):
                def turned(t, r):
                    v.wait_ge(x_turned, t + 1)
                    v.tensor_copy(xT[:, r % 2, :, :], px[:, r % 2, 0:C].rearrange("p (k n) -> p k n", k=KC)).then_inc(xT_done, 1)

                def biased(t, r, e):
                    v.wait_ge(up_ps, t + 1)
                    v.tensor_tensor(hb[:, r % 2, :].unsqueeze(1), ph[:, r % 2, :].unsqueeze(1), b1[:, bass.ds(e, 1), :],
                                    ALU.add).then_inc(b_done, 1)

                def four(i, es, first=False):
                    for r in range(XR):
                        t = XR * i + r
                        biased(t + 1, r + 1, es[r + 1])
                        v.wait_ge(down_ps, t + 1)
                        if not first:
                            v.wait_ge(stored[r], 16 * i)
                        v.tensor_tensor(y[:, r, :].unsqueeze(1), py[:, r % 2, 0:C].unsqueeze(1), b2[:, bass.ds(es[r], 1), :],
                                        ALU.add).then_inc(y_done, 1)
                        turned(t + 2, r + 2)
                v.wait_ge(w_in, 64)
                turned(0, 0)
                turned(1, 1)
                es = tile_experts(nc, mybir.EngineType.DVE, emap, 0)
                biased(0, 0, es[0])
                four(0, es, first=True)
                with v.Fori(1, EXT // XR) as i:
                    four(i, tile_experts(nc, mybir.EngineType.DVE, emap, i))

            @block.scalar
            def _(a):
                def gelu(t, x):
                    a.wait_ge(b_done, t + 1)
                    a.activation(h[:, x, :], hb[:, x, :], ACT.Gelu).then_inc(h_done, 1)
                gelu(0, 0)
                with a.Fori(0, EXT // 2) as i:
                    for x in range(2):
                        a.wait_ge(h_turned, 2 * i + x + 1)
                        a.copy(hT[:, x, :, :], pt[:, x, :, :]).then_inc(hT_done, 1)
                        gelu(2 * i + x + 1, 1 - x)

            @block.tensor
            def _(pe):
                def turn_x(t, r):
                    pe.wait_ge(x_in[r % XR], 16 * (t[0] + r // XR) + 16)
                    for k in range(KC):
                        m = pe.transpose(px[:, r % 2, k * P:(k + 1) * P], x[:, r % XR, k * P:(k + 1) * P], ident[:, :])
                    m.then_inc(x_turned, 1)

                def up(t, r, e):
                    pe.wait_ge(xT_done, t + 1)
                    for k in range(KC):
                        m = pe.matmul(ph[:, r % 2, :], xT[:, r % 2, k, :], w1[:, k, bass.ds(e, 1), :],
                                      start=(k == 0), stop=(k == KC - 1))
                    m.then_inc(up_ps, 1)

                def four(i, es):
                    for r in range(XR):
                        t = XR * i + r
                        pe.wait_ge(h_done, t + 1)
                        for c in range(HC):
                            m = pe.transpose(pt[:, r % 2, c, :], h[:, r % 2, c * P:(c + 1) * P], ident[:, :])
                        m.then_inc(h_turned, 1)
                        up(t + 1, r + 1, es[r + 1])
                        pe.wait_ge(hT_done, t + 1)
                        for c in range(HC):
                            m = pe.matmul(py[:, r % 2, 0:C], hT[:, r % 2, c, :], w2[:, c, bass.ds(es[r], 1), :],
                                          start=(c == 0), stop=(c == HC - 1))
                        m.then_inc(down_ps, 1)
                        turn_x((i,), r + 2)
                pe.wait_ge(w_in, 64)
                turn_x((0,), 0)
                turn_x((0,), 1)
                es = tile_experts(nc, mybir.EngineType.PE, emap, 0)
                up(0, 0, es[0])
                four(0, es)
                with pe.Fori(1, EXT // XR) as i:
                    four(i, tile_experts(nc, mybir.EngineType.PE, emap, i))


XR = 4
EXT = -(-((2 * N + NEXP * (P - 1)) // P) // XR) * XR
EXA = EXT + XR
DUMP = EXA * P
EM = P
assert EXA <= EM
XFILL = 6
XROWS = (DUMP + 2 * P) // XFILL
assert XROWS * XFILL == DUMP + 2 * P and XROWS % P == 0


def tile_experts(nc, engine, emap, i):
    return nc.values_load_multi_w_load_instructions(
        emap[0:1, bass.ds(i * XR, XR + 1)], engines=[engine], min_val=0, max_val=NEXP - 1)[1]


def finish(nc, A, W, sem, slot_g, out):
    TP = 2
    NP = NTP // TP
    with ExitStack() as cx:
        def sb(n, s, d=F32):
            return cx.enter_context(nc.sbuf_tensor("o_" + n, s, d))
        ix = sb("ix", [P, 2, 2, TP], I32)
        ya = sb("ya", [P, 2, 2, TP, C])
        x2 = sb("x2", [P, 2, TP, C])
        s1 = sb("s1", [P, 2, TP, C])
        o = sb("o", [P, 2, TP, C])
        staged = sem("o_staged")
        y_in = [sem(f"o_y_in{x}") for x in range(2)]
        x_in = [sem(f"o_x_in{x}") for x in range(2)]
        summed = sem("o_summed")
        done = sem("o_done")
        stored = [sem(f"o_stored{x}") for x in range(2)]

        def pair(ap, j):
            return ap[bass.ds(j * TP * P, TP * P), :].rearrange("(j p) c -> p j c", p=P)
        with nc.Block() as block:
            @block.sync
            def _(sp):
                for x in range(2):
                    sp.dma_start(x2[:, x, :, :], pair(W["x2"], x)).then_inc(x_in[x], 16)
                with sp.Fori(0, NP // 2 - 1) as i:
                    for x in range(2):
                        sp.wait_ge(done, 2 * i + x + 1)
                        sp.dma_start(pair(out, 2 * i + x), o[:, x, :, :]).then_inc(stored[x], 16)
                        sp.dma_start(x2[:, x, :, :], pair(W["x2"], 2 * i + x + 2)).then_inc(x_in[x], 16)
                for x in range(2):
                    sp.wait_ge(done, NP - 2 + x + 1)
                    sp.dma_start(pair(out, NP - 2 + x), o[:, x, :, :]).then_inc(stored[x], 16)
                for x in range(2):
                    sp.wait_ge(stored[x], 16 * (NP // 2))

            @block.gpsimd
            def _(g):
                want = counter(g, "o_staged_want", 1)
                with g.Fori(0, NP // 2) as i:
                    for x in range(2):
                        passed(g, staged, want, 1)
                        for w in range(2):
                            for s in range(TP):
                                g.indirect_dma_start(ya[:, x, w, s, :], None, W["ys"],
                                                     bass.IndirectOffsetOnAxis(ap=ix[:, x, w, s:s + 1], axis=0))\
                                 .then_inc(y_in[x], 16)

            @block.vector
            def _(v):
                def stage(j, x):
                    v.tensor_copy(ix[:, x, :, :], slot_g[:, :, bass.ds(j * TP, TP)]).then_inc(staged, 1)

                def one(i, x, first=False):
                    j = 2 * i + x
                    v.wait_ge(y_in[x], 16 * 2 * TP * i + 16 * 2 * TP)
                    v.tensor_tensor(s1[:, x, :, :], ya[:, x, 0, :, :], ya[:, x, 1, :, :], ALU.add).then_inc(summed, 1)
                    v.wait_ge(summed, j + 1)
                    stage(j + 2, x)
                    v.wait_ge(x_in[x], 16 * i + 16)
                    if not first:
                        v.wait_ge(stored[x], 16 * i)
                    v.tensor_tensor(o[:, x, :, :], s1[:, x, :, :], x2[:, x, :, :], ALU.add).then_inc(done, 1)
                for x in range(2):
                    stage(x, x)
                for x in range(2):
                    one(0, x, first=True)
                with v.Fori(1, NP // 2) as i:
                    for x in range(2):
                        one(i, x)


def kernel(**inputs):
    import numpy as np
    import concourse.bacc as bacc
    from concourse.bass_utils import run_bass_kernel_spmd

    a = {k: np.ascontiguousarray(v) for k, v in inputs.items()}

    def halves(w):
        return np.ascontiguousarray(w.reshape(-1, P, w.shape[1]).transpose(1, 0, 2))

    def repeat(b):
        return np.ascontiguousarray(np.broadcast_to(b[None, :], (P, b.shape[0])))

    def columns(b):
        return np.ascontiguousarray(b.reshape(-1, P).T)

    f32 = np.float32
    x = np.zeros((NPAD, C), f32)
    x[:N] = a["x"]
    qkvm = a["L0_mix_Wqkv"]
    ar = np.arange
    g = "L0_gnn_"
    is_node = (ar(NT)[None, :] * P + ar(P)[:, None] < N).astype(f32)
    arrays = {
        "x": x, "src": a["src"], "dst": a["dst"],
        "wall": halves(np.concatenate([a[g + "Wq"].T, qkvm[:, C:2 * C], a[g + "Wk"].T, a[g + "Wv"].T, qkvm[:, 2 * C:]], 1)),
        "bq": repeat(a[g + "bq"]), "bkv": repeat(np.concatenate([a[g + "bk"], a[g + "bv"]])),
        "lng": columns(a["L0_mix_ln_g"]), "lnb": columns(a["L0_mix_ln_b"]),
        "vmask": np.where(ar(NTP)[None, :] * P + ar(P)[:, None] < N, 0.0, -BIG).astype(f32),
        "ident": np.eye(P, dtype=f32), "iota": np.broadcast_to(ar(P, dtype=f32)[None, :], (P, P)).copy(),
        "triu": np.triu(np.ones((P, P), f32), 1),
        "jtile": (ar(P)[:, None] * (STM // P) + ar(STM // P)[None, :]).astype(f32),
        "bdmask": halves((ar(C)[:, None] // D == ar(C)[None, :] // D).astype(f32)),
        "wqm": halves(qkvm[:, 0:C]), "wpr": halves(a["L0_mix_Wproj"]), "wo": halves(np.ascontiguousarray(a[g + "Wo"].T)),
        "wg1": halves(a["L0_mix_Wg1"]), "wg2": a["L0_mix_Wg2"], "bg1": a["L0_mix_bg1"].reshape(GH, 1),
        "bg2": columns(a["L0_mix_bg2"]), "bo": repeat(a[g + "bo"]), "bpr": repeat(a["L0_mix_bproj"]),
        "wgt": halves(a["L0_ffn_Wg"]), "bgt": repeat(a["L0_ffn_bg"]),
        "iota8": np.broadcast_to(ar(NEXP, dtype=f32)[None, :], (P, NEXP)).copy(),
        "w1": np.ascontiguousarray(a["L0_ffn_W1"].reshape(NEXP, KC, P, HID).transpose(2, 1, 0, 3)),
        "w2": np.ascontiguousarray(a["L0_ffn_W2"].reshape(NEXP, HC, P, C).transpose(2, 1, 0, 3)),
        "b1": np.broadcast_to(a["L0_ffn_b1"][None], (P, NEXP, HID)).copy(),
        "b2": np.broadcast_to(a["L0_ffn_b2"][None], (P, NEXP, C)).copy(),
        "valid": is_node, "jcol": ar(P, dtype=f32)[:, None].copy(),
        "dump": (1 - is_node[:, None, :]) * (DUMP + ar(P)[:, None, None] + P * ar(2)[None, :, None]).astype(f32),
    }
    nc = bacc.Bacc("TRN2", target_bir_lowering=False, num_devices=1)
    A = {k: nc.dram_tensor("in_" + k, v.shape, mybir.dt.from_np(v.dtype), kind="ExternalInput").ap()
         for k, v in arrays.items()}
    out = nc.dram_tensor("out", (NPAD, C), F32, kind="ExternalOutput").ap()
    build(nc, A, out)
    r = run_bass_kernel_spmd(nc, [{"in_" + k: v for k, v in arrays.items()}], core_ids=[0])
    return np.ascontiguousarray(r.results[0]["out"][:N])
```

```python
from contextlib import ExitStack, contextmanager

import concourse.bass as bass
from concourse import mybir

F32 = mybir.dt.float32
BF16 = mybir.dt.bfloat16
I32 = mybir.dt.int32
U32 = mybir.dt.uint32
ALU = mybir.AluOpType
ACT = mybir.ActivationFunctionType
AX = mybir.AxisListType.X

P = 128
N = 6250
C = 256
H = 8
D = C // H
E = 106250
KC = C // P

NT = (N + P - 1) // P
TPG = 4
GN = TPG * P
NG = (NT + TPG - 1) // TPG
NPAD = NG * GN
NTP = NG * TPG

EL = 125
ET = E // EL
SB_ = 10
HB2 = (ET // SB_ - 1) // 2
assert ET == SB_ * (2 * HB2 + 1)
CH = 16
ST_NEED = (E + NT * (P - 1)) // P
GPC = (ST_NEED + CH - 1) // CH
ST = CH * GPC
HB = 4
NHB = ST // HB
STM = (ST + P - 1) // P * P
RING = 4
STX = ST + RING * HB
ROWPAD = 8191
BIG = 1e30
NEXP = 8
HID = 512
HC = HID // P
GH = 64
EPS = 1e-5
SCALE = float(D) ** -0.5


def rows(ap, i):
    return ap[bass.ds(i * GN, GN), :].rearrange("(j p) c -> p j c", p=P)


@contextmanager
def stage(nc):
    with ExitStack() as cx:
        used = []

        def sem(name):
            used.append(cx.enter_context(nc.semaphore(name)))
            return used[-1]
        yield sem
        with nc.Block() as block:
            @block.gpsimd
            def _(g):
                for one in used:
                    g.sem_clear(one)


def counter(eng, name, first):
    reg = eng.alloc_register(name)
    eng.reg_mov(reg, first)
    return reg


def passed(eng, semaphore, reg, step, last=None):
    if last is not None:
        eng.wait_ge(semaphore, last)
        return
    eng.wait_ge(semaphore, eng.snap(reg))
    eng.reg_add(reg, reg, step)


def node_tiles(nc, engine, tmap, hb):
    return nc.values_load_multi_w_load_instructions(
        tmap[0:1, bass.ds(hb * HB, HB)], engines=[engine], min_val=0, max_val=NT - 1)[1]


def bc(ap, shape):
    return ap.broadcast_to(shape)


def build(nc, A, out):
    ctx = ExitStack()
    with ctx:
        def sem(name):
            return ctx.enter_context(nc.semaphore(name))

        def sbp(name, shape, dt):
            return ctx.enter_context(nc.sbuf_tensor(name, shape, dt))

        def dram(name, shape, dt):
            return nc.dram_tensor(name, shape, dt).ap()

        W = dict(
            k=dram("k_tab", [NPAD, C], F32), v=dram("v_tab", [NPAD, C], F32),
            km=dram("kvmix", [NPAD, 2 * C], F32),
            xnT=dram("xnT_d", [P, KC, NPAD], F32), xmT=dram("xmT_d", [P, KC, NPAD], F32),
            sorted=dram("sorted_edges", [ST * P, 2], I32), tmap=dram("tile_map", [1, STM], I32),
            x2=dram("x2_d", [NPAD, C], F32), xl=dram("x2_normed", [NPAD, C], F32),
            xs=dram("expert_rows", [DUMP + 2 * P, C], F32), ys=dram("expert_out", [EXT * P, C], F32),
            emap=dram("tile_experts", [1, EM], I32),
            ends=dram("chunk_ends", [2, P, 3], F32), carry=dram("chunk_carry", [2, CH, H], F32),
        )
        ident = sbp("ident", [P, P], F32)
        S = {}
        s_const = sem("const_loaded")
        with nc.Block() as block:
            @block.sync
            def _(sp):
                sp.dma_start(ident[:, :], A["ident"]).then_inc(s_const, 16)
                sp.wait_ge(s_const, 16)
        ctxbd = sbp("ctxbd", [P, KC, C], F32)
        kmax = sbp("kmax", [P, C], F32)
        score = sbp("score", [P, ST, H], F32)
        rowf = sbp("row_sorted", [P, ST], F32)
        rowl = sbp("row_in_tile", [P, STX], F32)
        coli = sbp("col_sorted", [P, STX], I32)
        tmap = sbp("tile_map_sb", [1, STM], I32)
        with ExitStack() as qx:
            q3 = qx.enter_context(nc.sbuf_tensor("q_parts", [P, NTP, 3, C], BF16))
            with stage(nc) as sem:
                node_tables(nc, A, W, sem, ident, q3, kmax)
            with ExitStack() as bx:
                pos_base = bx.enter_context(nc.sbuf_tensor("pos_base", [P, NT], F32))
                rc = bx.enter_context(nc.sbuf_tensor("rowcol", [EL, ET, 2], I32))
                lo = bx.enter_context(nc.sbuf_tensor("row_lo", [EL, ET + 2 * SB_], BF16))
                hi = bx.enter_context(nc.sbuf_tensor("row_hi", [EL, ET + 2 * SB_], BF16))
                with stage(nc) as sem:
                    context_and_histogram(nc, A, W, sem, ident, kmax, ctxbd, rc, lo, hi, pos_base)
                with stage(nc) as sem:
                    sort_edges(nc, A, W, sem, ident, rc, lo, hi, pos_base)
            with stage(nc) as sem:
                load_sorted(nc, A, W, sem, ident, rowf, rowl, coli, tmap)
            with stage(nc) as sem:
                edge_scores(nc, A, W, sem, rowl, coli, tmap, q3, score)
        with stage(nc) as sem:
            softmax_edges(nc, A, W, sem, ident, rowf, score)
        first = sbp("first_expert", [P, NTP, NEXP], F32)
        second = sbp("second_expert", [P, NTP, NEXP], F32)
        with ExitStack() as ax:
            acc = ax.enter_context(nc.sbuf_tensor("acc", [P, NTP, C + H], F32))
            with stage(nc) as sem:
                aggregate(nc, A, W, sem, rowl, coli, tmap, score, acc)
            with stage(nc) as sem:
                combine(nc, A, W, sem, ident, ctxbd, acc, first, second)
        slot_i = sbp("slot_scatter", [P, 2, NT], I32)
        slot_g = sbp("slot_gather", [P, 2, NTP + 4], I32)
        emap = sbp("tile_experts_sb", [1, EM], I32)
        weights = (sbp("expert_w1", [P, KC, NEXP, HID], F32), sbp("expert_w2", [P, HC, NEXP, C], F32),
                   sbp("expert_b1", [P, NEXP, HID], F32), sbp("expert_b2", [P, NEXP, C], F32))
        with stage(nc) as sem:
            route(nc, A, W, sem, ident, first, second, slot_i, slot_g, emap, weights)
        with stage(nc) as sem:
            experts(nc, A, W, sem, ident, emap, weights)
        with stage(nc) as sem:
            finish(nc, A, W, sem, slot_g, out)


def node_tables(nc, A, W, sem, ident, q3, kmax):
    with ExitStack() as cx:
        def sb(n, s, d=F32):
            return cx.enter_context(nc.sbuf_tensor("n_" + n, s, d))

        def ps(n, s, d=F32):
            return cx.enter_context(nc.psum_tensor("n_" + n, s, d))
        wall = sb("wall", [P, KC, 5 * C])
        bq = sb("bq", [P, C])
        bkv = sb("bkv", [P, 2 * C])
        lng = sb("lng", [P, KC])
        lnb = sb("lnb", [P, KC])
        vmask = sb("vmask", [P, NTP])
        xg = sb("xg", [P, TPG, C])
        xn = sb("xn", [P, TPG, C])
        xm = sb("xm", [P, TPG, C])
        st1 = sb("st1", [P, TPG, 6])
        st2 = sb("st2", [P, TPG, 6])
        mv1 = sb("mv1", [P, TPG, 2])
        mv2 = sb("mv2", [P, TPG, 2])
        ve1 = sb("ve1", [P, TPG])
        ve2 = sb("ve2", [P, TPG])
        sd1 = sb("sd1", [P, TPG])
        sd2 = sb("sd2", [P, TPG])
        rs1 = sb("rs1", [P, TPG])
        rs2 = sb("rs2", [P, TPG])
        xnT = sb("xnT", [P, 2, KC, GN])
        xmT = sb("xmT", [P, KC, GN])
        kv = sb("kv", [P, TPG, 2 * C])
        kvm = sb("kvm", [P, TPG, 2 * C])
        qf = sb("qf", [P, TPG, C])
        qr = sb("qr", [P, TPG, C])
        pT = ps("pT", [P, KC, GN])
        pM = ps("pM", [P, KC, GN])
        pA = ps("pA", [P, 2 * C])
        pB = ps("pB", [P, 2 * C])
        pC = ps("pC", [P, C])
        w_in = sem("n_weights_in")
        x_in = sem("n_x_in")
        stats1 = sem("n_stats1")
        aggr1 = sem("n_aggr1")
        var1 = sem("n_var1")
        std1 = sem("n_std1")
        rstd1 = sem("n_rstd1")
        xn_done = sem("n_xn_done")
        stats2 = sem("n_stats2")
        aggr2 = sem("n_aggr2")
        var2 = sem("n_var2")
        std2 = sem("n_std2")
        rstd2 = sem("n_rstd2")
        xm_done = sem("n_xm_done")
        xn_turned = sem("n_xn_turned")
        xm_turned = sem("n_xm_turned")
        xnT_done = sem("n_xnT_done")
        xmT_done = sem("n_xmT_done")
        xnT_stored = sem("n_xnT_stored")
        xmT_stored = sem("n_xmT_stored")
        half_stored = [sem(f"n_half_stored{h}") for h in range(2)]
        proj_a = sem("n_proj_a")
        proj_b = sem("n_proj_b")
        proj_c = sem("n_proj_c")
        kv_done = sem("n_kv_done")
        vm_read = sem("n_vm_read")
        kmax_step = sem("n_kmax_step")
        km_done = sem("n_km_done")
        q_done = sem("n_q_done")
        q_high = sem("n_q_high")
        q_rest = sem("n_q_rest")
        q_mid = sem("n_q_mid")
        q_low = sem("n_q_low")

        with nc.Block() as block:
            @block.sync
            def _(sp):
                def load(n):
                    sp.dma_start(xg[:, :, :], rows(A["x"], n)).then_inc(x_in, 16)

                def store_xn(n, x):
                    sp.dma_start(W["xnT"][:, :, bass.ds(n * GN, GN)], xnT[:, x, :, :]).then_inc(xnT_stored, 16)

                def store_xm(n):
                    sp.wait_ge(xmT_done, KC * n + KC)
                    sp.dma_start(W["xmT"][:, :, bass.ds(n * GN, GN)], xmT[:, :, :]).then_inc(xmT_stored, 16)

                def store_half(i, h, turned=None):
                    two = slice(2 * h, 2 * h + 2)
                    if turned is not None and not isinstance(turned, int):
                        turned = sp.snap(turned)
                    sp.wait_ge(kv_done, TPG * i + 2 * h + 2)
                    sp.wait_ge(vm_read, TPG * i + 2 * h + 2)
                    sp.wait_ge(km_done, TPG * i + 2 * h + 2)
                    if turned is not None:
                        sp.wait_ge(xnT_done, turned)
                    for table, data in (("k", kv[:, two, 0:C]), ("v", kv[:, two, C:2 * C]), ("km", kvm[:, two, :])):
                        sp.dma_start(W[table][bass.ds(i * GN + 2 * h * P, 2 * P), :].rearrange("(j p) c -> p j c", p=P),
                                     data).then_inc(half_stored[h], 16)

                def group(i, x, load_next=True):
                    if load_next:
                        sp.wait_ge(xn_done, TPG * i + 2 * TPG)
                        load(i + 2)
                    store_half(i, 0)
                    store_half(i, 1, i + 2)
                    store_xn(i + 1, 1 - x)
                    store_xm(i + 1)
                load(0)
                for dst, name in ((wall, "wall"), (bq, "bq"), (bkv, "bkv"), (lng, "lng"), (lnb, "lnb"), (vmask, "vmask")):
                    d = dst[:, :, :] if name == "wall" else dst[:, :]
                    sp.dma_start(d, A[name]).then_inc(w_in, 16)
                sp.wait_ge(xn_done, TPG)
                load(1)
                sp.wait_ge(xnT_done, 1)
                store_xn(0, 0)
                store_xm(0)
                group(0, 0)
                with sp.Fori(0, (NG - 3) // 2) as k:
                    group(2 * k + 1, 1)
                    group(2 * k + 2, 0)
                group(NG - 2, 1, load_next=False)
                store_half(NG - 1, 0)
                store_half(NG - 1, 1)
                sp.wait_ge(xnT_stored, 16 * NG)
                sp.wait_ge(xmT_stored, 16 * NG)
                for h in range(2):
                    sp.wait_ge(half_stored[h], 48 * NG)

            @block.vector
            def _(v):
                v.memset(kmax[:, :], -BIG).then_inc(kmax_step, 1)
                want1 = counter(v, "stats1_want", TPG)
                want2 = counter(v, "stats2_want", TPG)

                def stats_x(n):
                    v.wait_ge(x_in, 16 * n + 16)
                    for j in range(TPG):
                        v.bn_stats(st1[:, j, :], xg[:, j, :]).then_inc(stats1, 1)
                    passed(v, stats1, want1, TPG)
                    for j in range(TPG):
                        v.bn_aggr(mv1[:, j, :], st1[:, j, :]).then_inc(aggr1, 1)
                    v.wait_ge(aggr1, TPG * n + TPG)
                    v.tensor_scalar(ve1[:, :], mv1[:, :, 1], EPS, None, ALU.add).then_inc(var1, 1)

                def norm_x(n, first=False):
                    v.wait_ge(std1, n + 1)
                    v.reciprocal(rs1[:, :], sd1[:, :]).then_inc(rstd1, 1)
                    v.wait_ge(rstd1, n + 1)
                    if not first:
                        v.wait_ge(xn_turned, n)
                    for j in range(TPG):
                        v.tensor_scalar(xn[:, j, :], xg[:, j, :], mv1[:, j, 0:1], rs1[:, j:j + 1],
                                        ALU.subtract, ALU.mult).then_inc(xn_done, 1)

                def stats_xn(n):
                    for j in range(TPG):
                        v.wait_ge(xn_done, TPG * n + j + 1)
                        v.bn_stats(st2[:, j, :], xn[:, j, :]).then_inc(stats2, 1)
                    passed(v, stats2, want2, TPG)
                    for j in range(TPG):
                        v.bn_aggr(mv2[:, j, :], st2[:, j, :]).then_inc(aggr2, 1)
                    v.wait_ge(aggr2, TPG * n + TPG)
                    v.tensor_scalar(ve2[:, :], mv2[:, :, 1], EPS, None, ALU.add).then_inc(var2, 1)

                def norm_xn(n, first=False):
                    v.wait_ge(std2, n + 1)
                    v.reciprocal(rs2[:, :], sd2[:, :]).then_inc(rstd2, 1)
                    v.wait_ge(rstd2, n + 1)
                    if not first:
                        v.wait_ge(xm_turned, n)
                    for j in range(TPG):
                        v.tensor_scalar(xm[:, j, :], xn[:, j, :], mv2[:, j, 0:1], rs2[:, j:j + 1],
                                        ALU.subtract, ALU.mult).then_inc(xm_done, 1)

                def evacuate(i, j, first=False):
                    if not first and j % 2 == 0:
                        v.wait_ge(half_stored[j // 2], 48 * i)
                    if not first and j == 0:
                        v.wait_ge(q_rest, i)
                    if not first and j == 3:
                        v.wait_ge(q_low, i)
                    v.wait_ge(proj_a, TPG * i + j + 1)
                    v.tensor_tensor(qf[:, j, :], pA[:, 0:C], bq[:, :], ALU.add).then_inc(q_done, 1)
                    v.tensor_scalar(kvm[:, j, 0:C], pA[:, C:2 * C], vmask[:, bass.ds(TPG * i + j, 1)], None,
                                    ALU.add).then_inc(km_done, 1)
                    v.wait_ge(proj_b, TPG * i + j + 1)
                    v.tensor_tensor(kv[:, j, :], pB[:, :], bkv[:, :], ALU.add).then_inc(kv_done, 1)
                    v.wait_ge(km_done, TPG * i + j + 1)
                    v.wait_ge(kmax_step, TPG * i + j + 1)
                    v.tensor_tensor(kmax[:, :], kmax[:, :], kvm[:, j, 0:C], ALU.max).then_inc(kmax_step, 1)

                def rest_of_q(i):
                    v.wait_ge(q_high, i + 1)
                    v.tensor_tensor(qr[:, :, :], qf[:, :, :], q3[:, bass.ds(TPG * i, TPG), 0, :],
                                    ALU.subtract).then_inc(q_rest, 1)

                def low_of_q(i):
                    v.wait_ge(q_mid, i + 1)
                    v.tensor_tensor(q3[:, bass.ds(TPG * i, TPG), 2, :], qr[:, :, :], q3[:, bass.ds(TPG * i, TPG), 1, :],
                                    ALU.subtract).then_inc(q_low, 1)

                def group(i, first=False, last=False):
                    if not last:
                        stats_x(i + 1)
                    if not first:
                        rest_of_q(i - 1)
                    evacuate(i, 0, first)
                    if not first:
                        low_of_q(i - 1)
                    if not last:
                        norm_x(i + 1)
                    evacuate(i, 1, first)
                    if not last:
                        stats_xn(i + 1)
                    evacuate(i, 2, first)
                    if not last:
                        norm_xn(i + 1)
                    evacuate(i, 3, first)
                stats_x(0)
                norm_x(0, first=True)
                stats_xn(0)
                norm_xn(0, first=True)
                v.wait_ge(w_in, 96)
                group(0, first=True)
                with v.Fori(1, NG - 1) as i:
                    group(i)
                group(NG - 1, last=True)
                rest_of_q(NG - 1)
                low_of_q(NG - 1)
                v.wait_ge(q_low, NG)

            @block.scalar
            def _(a):
                def std_x(n):
                    a.wait_ge(var1, n + 1)
                    a.activation(sd1[:, :], ve1[:, :], ACT.Sqrt).then_inc(std1, 1)

                def std_xn(n):
                    a.wait_ge(var2, n + 1)
                    a.activation(sd2[:, :], ve2[:, :], ACT.Sqrt).then_inc(std2, 1)

                def xn_copy(n, x):
                    a.wait_ge(xn_turned, n + 1)
                    a.copy(xnT[:, x, :, :], pT[:, :, :]).then_inc(xnT_done, 1)

                def xm_copy(n):
                    a.wait_ge(xm_turned, n + 1)
                    for k in range(KC):
                        a.activation(xmT[:, k, :], pM[:, k, :], ACT.Identity, bias=lnb[:, k:k + 1],
                                     scale=lng[:, k:k + 1]).then_inc(xmT_done, 1)

                def linear_v(i, j, first=False):
                    if not first and j % 2 == 0:
                        a.wait_ge(half_stored[j // 2], 48 * i)
                    a.wait_ge(proj_c, TPG * i + j + 1)
                    a.copy(kvm[:, j, C:2 * C], pC[:, :]).then_inc(vm_read, 1)

                def middle_of_q(i):
                    a.wait_ge(q_rest, i + 1)
                    a.copy(q3[:, bass.ds(TPG * i, TPG), 1, :], qr[:, :, :]).then_inc(q_mid, 1)

                def group(i, x, first=False, last=False):
                    if not last:
                        std_x(i + 1)
                    if not first:
                        middle_of_q(i - 1)
                    linear_v(i, 0, first)
                    linear_v(i, 1, first)
                    if not last:
                        if not first:
                            a.wait_ge(xnT_stored, 16 * i)
                        xn_copy(i + 1, 1 - x)
                        std_xn(i + 1)
                    linear_v(i, 2, first)
                    linear_v(i, 3, first)
                    a.wait_ge(q_done, TPG * i + TPG)
                    a.copy(q3[:, bass.ds(TPG * i, TPG), 0, :], qf[:, :, :]).then_inc(q_high, 1)
                    if not last:
                        a.wait_ge(xmT_stored, 16 * i + 16)
                        xm_copy(i + 1)
                std_x(0)
                xn_copy(0, 0)
                std_xn(0)
                a.wait_ge(w_in, 96)
                xm_copy(0)
                group(0, 0, first=True)
                with a.Fori(0, (NG - 3) // 2) as k:
                    group(2 * k + 1, 1)
                    group(2 * k + 2, 0)
                group(NG - 2, 1)
                group(NG - 1, 0, last=True)
                middle_of_q(NG - 1)

            @block.tensor
            def _(pe):
                def turn(dst, src, seen):
                    for j in range(TPG):
                        for k in range(KC):
                            t = pe.transpose(dst[:, k, j * P:(j + 1) * P], src[:, j, k * P:(k + 1) * P], ident[:, :])
                    t.then_inc(seen, 1)

                def project(i, x, j, first=False):
                    parts = ((pA, 0, 2 * C, proj_a, (q_done, km_done)), (pB, 2 * C, 4 * C, proj_b, (kv_done,)),
                             (pC, 4 * C, 5 * C, proj_c, (vm_read,)))
                    for dst, c0, c1, there, read in parts:
                        if j or not first:
                            for r in read:
                                pe.wait_ge(r, TPG * i + j)
                        for k in range(KC):
                            m = pe.matmul(dst[:, :], xnT[:, x, k, j * P:(j + 1) * P], wall[:, k, c0:c1],
                                          start=(k == 0), stop=(k == KC - 1))
                        m.then_inc(there, 1)

                def group(i, x, first=False, last=False):
                    pe.wait_ge(xnT_done, i + 1)
                    project(i, x, 0, first)
                    project(i, x, 1, first)
                    if not last:
                        pe.wait_ge(xn_done, TPG * i + 2 * TPG)
                        turn(pT, xn, xn_turned)
                    project(i, x, 2, first)
                    project(i, x, 3, first)
                    if not last:
                        pe.wait_ge(xmT_done, KC * i + KC)
                        pe.wait_ge(xm_done, TPG * i + 2 * TPG)
                        turn(pM, xm, xm_turned)
                pe.wait_ge(xn_done, TPG)
                turn(pT, xn, xn_turned)
                pe.wait_ge(xm_done, TPG)
                turn(pM, xm, xm_turned)
                pe.wait_ge(w_in, 96)
                group(0, 0, first=True)
                with pe.Fori(0, (NG - 3) // 2) as k:
                    group(2 * k + 1, 1)
                    group(2 * k + 2, 0)
                group(NG - 2, 1)
                group(NG - 1, 0, last=True)


def context_and_histogram(nc, A, W, sem, ident, kmax, ctxbd, rc, lo, hi, pos_base):
    with ExitStack() as cx:
        def sb(n, s, d=F32):
            return cx.enter_context(nc.sbuf_tensor("h_" + n, s, d))

        def ps(n, s, d=F32):
            return cx.enter_context(nc.psum_tensor("h_" + n, s, d))
        ones = sb("ones", [P, P])
        zero = sb("zero", [P, P])
        bd = sb("bd", [P, KC, C])
        kcol = sb("kcol", [P, KC])
        diag = sb("diag", [P, C])
        krow = sb("krow", [P, C])
        km = sb("km", [P, 2, TPG, 2 * C + 1])
        e = sb("e", [P, 2, TPG, C])
        rsum = sb("rsum", [P, KC])
        pk = ps("pk", [P, C])
        prow = ps("prow", [P, C])
        pctx = ps("pctx", [P, KC, 512])
        bd_in = sem("m_bd_in")
        filled = sem("m_filled")
        turned = sem("m_turned")
        colmax = sem("m_colmax")
        diag_done = sem("m_diag")
        row_ps = sem("m_row_ps")
        row_done = sem("m_row")
        km_in = [sem(f"m_km_in{x}") for x in range(2)]
        sub_done = sem("m_sub")
        e_done = sem("m_e")
        ctx_step = sem("m_ctx_step")
        rs_done = sem("m_rs")
        bd_done = sem("m_bd_done")
        ei = sb("ei", [EL, 2, ET], I32)
        ti = sb("ti", [EL, 2, ET], I32)
        iota = sb("iota", [P, P])
        triu = sb("triu", [P, P])
        jt = sb("jt", [P, STM // P])
        fill = sb("fill", [P, ST, 2], I32)
        iotas = sb("iotas", [EL, P, SB_], BF16)
        ohlo = sb("ohlo", [EL, 2, P, SB_], BF16)
        ohhi = sb("ohhi", [EL, 2, NT, SB_], BF16)
        cnt = sb("cnt", [P, NT])
        tot = sb("tot", [P, NT], I32)
        tot2 = sb("tot2", [P, NT], I32)
        tot3 = sb("tot3", [P, NT], I32)
        tiles = sb("tiles", [P, NT])
        incl = sb("incl", [P, NT])
        excl = sb("excl", [P, NT])
        cmp = sb("cmp", [P, STM // P, NT])
        tmf = sb("tmf", [P, STM // P])
        tmi = sb("tmi", [P, STM // P], I32)
        pcnt = ps("pcnt", [P, NT])
        ptot = ps("ptot", [P, NT])
        pbef = ps("pbef", [P, NT])
        e_in = sem("h_e_in")
        c_in = sem("h_c_in")
        fill_done = sem("h_fill")
        fill_out = sem("h_fill_out")
        bits = sem("h_bits")
        fields = sem("h_fields")
        oh = sem("h_onehots_lo")
        ohh = sem("h_onehots_hi")
        counted = sem("h_counted")
        cnt_done = sem("h_cnt")
        tot_ps = sem("h_tot_ps")
        tot_done = sem("h_tot")
        tiles_done = sem("h_tiles")
        incl_done = sem("h_incl")
        excl_done = sem("h_excl")
        base_done = sem("h_base")
        cmp_done = sem("h_cmp")
        tmf_done = sem("h_tmf")
        tmf2_done = sem("h_tmf2")
        tmi_done = sem("h_tmi")
        tm_out = sem("h_tm_out")
        with nc.Block() as block:
            @block.sync
            def _(sp):
                sp.dma_start(ei[:, 0, :], A["src"].rearrange("(p t) -> p t", p=EL)).then_inc(e_in, 16)
                sp.dma_start(ei[:, 1, :], A["dst"].rearrange("(p t) -> p t", p=EL)).then_inc(e_in, 16)
                for d, n in ((iota, "iota"), (triu, "triu"), (jt, "jtile")):
                    sp.dma_start(d[:, :], A[n]).then_inc(c_in, 16)
                sp.wait_ge(fill_done, 2)
                sp.dma_start(W["sorted"].rearrange("(p t) k -> p t k", p=P), fill[:, :, :]).then_inc(fill_out, 16)
                sp.dma_start(bd[:, :, :], A["bdmask"]).then_inc(bd_in, 16)

                def load(i, x):
                    sp.dma_start(km[:, x, :, 0:2 * C], rows(W["km"], i)).then_inc(km_in[x], 16)
                load(0, 0)
                load(1, 1)
                with sp.Fori(0, (NG - 3) // 2) as k:
                    for x in range(2):
                        sp.wait_ge(ctx_step, 2 * k + x + 1)
                        load(2 * k + x + 2, x)
                sp.wait_ge(ctx_step, NG - 2)
                load(NG - 1, 0)
                sp.wait_ge(tmi_done, 1)
                sp.dma_start(W["tmap"].rearrange("a (p c) -> p (a c)", p=P), tmi[:, :]).then_inc(tm_out, 16)
                sp.wait_ge(fill_out, 16)
                sp.wait_ge(tm_out, 16)

            @block.gpsimd
            def _(g):
                g.memset(ones[:, :], 1.0).then_inc(filled, 1)
                g.memset(zero[:, :], 0.0).then_inc(filled, 1)
                g.memset(km[:, :, :, 2 * C:2 * C + 1], 1.0).then_inc(filled, 1)
                g.memset(fill[:, :, 0], ROWPAD).then_inc(fill_done, 1)
                g.memset(fill[:, :, 1], 0).then_inc(fill_done, 1)

            @block.vector
            def _(v):
                v.wait_ge(e_in, 32)
                v.wait_ge(c_in, 48)
                v.tensor_scalar(ti[:, 0, :], ei[:, 0, :], P - 1, None, ALU.bitwise_and).then_inc(bits, 1)
                v.tensor_scalar(ti[:, 1, :], ei[:, 0, :], 7, None, ALU.logical_shift_right).then_inc(bits, 1)
                v.tensor_copy(rc[:, :, :], ei[:, :, :].rearrange("p k t -> p t k")).then_inc(fields, 1)
                v.wait_ge(bits, 2)
                v.tensor_copy(lo[:, 0:ET], ti[:, 0, :]).then_inc(fields, 1)
                v.tensor_copy(hi[:, 0:ET], ti[:, 1, :]).then_inc(fields, 1)
                v.memset(lo[:, ET:], -1.0).then_inc(fields, 1)
                v.memset(hi[:, ET:], -1.0).then_inc(fields, 1)
                v.tensor_copy(iotas[:, :, :], bc(iota[0:EL, :].unsqueeze(2), [EL, P, SB_])).then_inc(fields, 1)
                v.wait_ge(fields, 6)

                def onehots(i, x, first=False):
                    if not first:
                        v.wait_ge(counted, i - 1)
                    v.tensor_tensor(ohlo[:, x, :, :], iotas[:, :, :],
                                    bc(lo[:, bass.ds(i * SB_, SB_)].unsqueeze(1), [EL, P, SB_]),
                                    ALU.is_equal).then_inc(oh, 1)
                    v.tensor_tensor(ohhi[:, x, :, :], iotas[:, 0:NT, :],
                                    bc(hi[:, bass.ds(i * SB_, SB_)].unsqueeze(1), [EL, NT, SB_]),
                                    ALU.is_equal).then_inc(ohh, 1)
                v.wait_ge(turned, 1)
                v.tensor_reduce(kcol[:, :], pk[:, :].rearrange("p (k n) -> p k n", k=KC), AX, ALU.max).then_inc(colmax, 1)
                v.wait_ge(colmax, 1)
                for k in range(KC):
                    v.tensor_scalar(diag[:, k * P:(k + 1) * P], ident[:, :], kcol[:, k:k + 1], None,
                                    ALU.mult).then_inc(diag_done, 1)
                v.wait_ge(row_ps, 1)
                v.tensor_copy(krow[:, :], prow[:, :]).then_inc(row_done, 1)
                v.wait_ge(row_done, 1)

                def below_max(x, loads):
                    v.wait_ge(km_in[x], 16 * loads)
                    v.tensor_tensor(e[:, x, :, :], km[:, x, :, 0:C], bc(krow[:, :].unsqueeze(1), [P, TPG, C]),
                                    ALU.subtract).then_inc(sub_done, 1)
                onehots(0, 0, first=True)
                onehots(1, 1, first=True)
                below_max(0, 1)
                with v.Fori(0, (NG - 1) // 2) as k:
                    for half in range(2):
                        for b in range(HBATCH):
                            onehots(HBATCH * (2 * k + half) + b + 2, (half * HBATCH + b) % 2)
                            if b == HBATCH - 3:
                                below_max(1 - half, k + 1 + half)
                v.wait_ge(counted, ET // SB_ + 1)
                v.tensor_copy(cnt[:, :], pcnt[:, :]).then_inc(cnt_done, 1)
                v.wait_ge(tot_ps, 2)
                v.tensor_copy(tot[:, :], ptot[:, :]).then_inc(tot_done, 1)
                v.wait_ge(tot_done, 1)
                v.tensor_scalar(tot2[:, :], tot[:, :], P - 1, None, ALU.add).then_inc(tot_done, 1)
                v.wait_ge(tot_done, 2)
                v.tensor_scalar(tot3[:, :], tot2[:, :], 7, None, ALU.logical_shift_right).then_inc(tot_done, 1)
                v.wait_ge(tot_done, 3)
                v.tensor_copy(tiles[:, :], tot3[:, :]).then_inc(tiles_done, 1)
                v.wait_ge(tiles_done, 1)
                v.wait_ge(filled, 2)
                v.tensor_tensor_scan(incl[:, :], zero[:, 0:NT], tiles[:, :], 0.0, ALU.add, ALU.add).then_inc(incl_done, 1)
                v.wait_ge(incl_done, 1)
                v.tensor_tensor(excl[:, :], incl[:, :], tiles[:, :], ALU.subtract).then_inc(excl_done, 1)
                v.wait_ge(excl_done, 1)
                v.scalar_tensor_tensor(out=pos_base[:, :], in0=excl[:, :], scalar=float(P), in1=pbef[:, :],
                                       op0=ALU.mult, op1=ALU.add).then_inc(base_done, 1)
                sh = [P, STM // P, NT]
                v.tensor_tensor(cmp[:, :, :], bc(incl[:, :].unsqueeze(1), sh), bc(jt[:, :].unsqueeze(2), sh),
                                ALU.is_le).then_inc(cmp_done, 1)
                v.wait_ge(cmp_done, 1)
                v.tensor_reduce(tmf[:, :], cmp[:, :, :], AX, ALU.add).then_inc(tmf_done, 1)
                v.wait_ge(tmf_done, 1)
                v.tensor_scalar(tmf[:, :], tmf[:, :], float(NT - 1), None, ALU.min).then_inc(tmf2_done, 1)
                v.wait_ge(tmf2_done, 1)
                v.tensor_copy(tmi[:, :], tmf[:, :]).then_inc(tmi_done, 1)
                v.wait_ge(ctx_step, NG + 1)
                v.reciprocal(rsum[:, :], pctx[:, :, C]).then_inc(rs_done, 1)
                v.wait_ge(rs_done, 1)
                v.wait_ge(bd_in, 16)
                for k in range(KC):
                    v.scalar_tensor_tensor(out=ctxbd[:, k, :], in0=pctx[:, k, 0:C], scalar=rsum[:, k:k + 1],
                                           in1=bd[:, k, :], op0=ALU.mult, op1=ALU.mult).then_inc(bd_done, 1)

            @block.scalar
            def _(a):
                def exp(i, x):
                    a.wait_ge(sub_done, i + 1)
                    a.activation(e[:, x, :, :], e[:, x, :, :], ACT.Exp).then_inc(e_done, 1)
                exp(0, 0)
                with a.Fori(0, (NG - 1) // 2) as k:
                    exp(2 * k + 1, 1)
                    exp(2 * k + 2, 0)

            @block.tensor
            def _(pe):
                for k in range(KC):
                    t = pe.transpose(pk[:, k * P:(k + 1) * P], kmax[:, k * P:(k + 1) * P], ident[:, :])
                t.then_inc(turned, 1)
                pe.wait_ge(filled, 3)
                pe.wait_ge(diag_done, KC)
                pe.matmul(prow[:, :], ones[:, :], diag[:, :], start=True, stop=True).then_inc(row_ps, 1)
                for k in range(KC):
                    pe.matmul(pctx[:, k, 0:P], zero[:, :], zero[:, :], start=True, stop=False, skip_group_check=True)
                    pe.matmul(pctx[:, k, P:2 * P], zero[:, :], zero[:, :], start=False, stop=False, skip_group_check=True)
                    pe.matmul(pctx[:, k, 2 * P:2 * P + 1], zero[:, :], zero[:, 0:1], start=False, stop=False,
                              skip_group_check=True)
                pe.matmul(pcnt[:, :], zero[:, :], zero[:, 0:NT], start=True, stop=False, skip_group_check=True)

                def count(i, x):
                    pe.wait_ge(oh, i + 1)
                    pe.wait_ge(ohh, i + 1)
                    for s in range(SB_):
                        m = pe.matmul(pcnt[:, :], ohlo[:, x, :, s], ohhi[:, x, :, s], start=False, stop=False,
                                      skip_group_check=True)
                    m.then_inc(counted, 1)

                def add(i, x, j):
                    if j == 0:
                        pe.wait_ge(e_done, i + 1)
                    for k in range(KC):
                        m = pe.matmul(pctx[:, k, 0:C + 1], e[:, x, j, k * P:(k + 1) * P], km[:, x, j, C:2 * C + 1],
                                      start=False, stop=False, skip_group_check=True)
                    if j == TPG - 1:
                        m.then_inc(ctx_step, 1)
                count(0, 0)
                with pe.Fori(0, (NG - 1) // 2) as n:
                    for half in range(2):
                        for b in range(HBATCH):
                            count(HBATCH * (2 * n + half) + b + 1, (half * HBATCH + b + 1) % 2)
                            if b < TPG:
                                add(2 * n + half, half, b)
                for j in range(TPG):
                    add(NG - 1, 0, j)
                for k in range(KC):
                    m = pe.matmul(pctx[:, k, 0:1], zero[:, :], zero[:, 0:1], start=False, stop=True,
                                  skip_group_check=True)
                m.then_inc(ctx_step, 1)
                pe.matmul(pcnt[:, 0:1], zero[:, :], zero[:, 0:1], start=False, stop=True,
                          skip_group_check=True).then_inc(counted, 1)
                pe.wait_ge(cnt_done, 1)
                pe.matmul(ptot[:, :], ones[:, :], cnt[:, :], start=True, stop=True).then_inc(tot_ps, 1)
                pe.matmul(pbef[:, :], triu[:, :], cnt[:, :], start=True, stop=True).then_inc(tot_ps, 1)


HBATCH = (ET // SB_ - 1) // (NG - 1)
assert HBATCH * (NG - 1) == ET // SB_ - 1 and HBATCH >= TPG


def sort_edges(nc, A, W, sem, ident, rc, lo, hi, pos_base):
    with ExitStack() as cx:
        def sb(n, s, d=F32):
            return cx.enter_context(nc.sbuf_tensor("s_" + n, s, d))

        def ps(n, s, d=F32):
            return cx.enter_context(nc.psum_tensor("s_" + n, s, d))
        iota = sb("iota", [P, P])
        triu = sb("triu", [P, P])
        idb = sb("idb", [P, P], BF16)
        ohlo = sb("ohlo", [EL, 2, SB_, P], BF16)
        ohhi = sb("ohhi", [EL, 2, SB_, NT], BF16)
        oht = sb("oht", [P, SB_, EL], BF16)
        ohtf = sb("ohtf", [P, SB_, EL])
        before = sb("before", [EL, SB_, EL], BF16)
        seen = sb("seen", [P, SB_, NT])
        picked = sb("picked", [EL, SB_, NT])
        posf = sb("posf", [EL, SB_])
        posi = sb("posi", [EL, 2, SB_], I32)
        rcs = sb("rcs", [EL, 2, SB_, 2], I32)
        pseen = ps("pseen", [P, 512])
        pt = ps("pt", [P, 16, P], BF16)
        plo = ps("plo", [P, 12, P])
        prank = ps("prank", [P, 512])
        c_in = sem("s_c_in")
        idb_done = sem("s_idb")
        oh = sem("s_onehots")
        turned = sem("s_turned")
        oht_done = sem("s_oht")
        ohtf_done = sem("s_ohtf")
        lo_ps = sem("s_lo_ps")
        bef_done = sem("s_before")
        snap = sem("s_snap")
        step = sem("s_step")
        rank = sem("s_rank")
        pick = sem("s_pick")
        pos = sem("s_pos")
        staged = sem("s_staged")
        landed = [sem(f"s_landed{x}") for x in range(2)]
        NB = ET // SB_
        rk = prank[0:EL, 0:SB_ * NT].rearrange("p (s t) -> p s t", s=SB_)
        with nc.Block() as block:
            @block.sync
            def _(sp):
                sp.dma_start(iota[:, :], A["iota"]).then_inc(c_in, 16)
                sp.dma_start(triu[:, :], A["triu"]).then_inc(c_in, 16)
                for x in range(2):
                    sp.wait_ge(landed[x], 16 * SB_ * ((NB + 1 - x) // 2))

            @block.vector
            def _(v):
                def onehots(i, x):
                    v.tensor_tensor(ohlo[:, x, :, :], bc(iota[0:EL, :].unsqueeze(1), [EL, SB_, P]),
                                    bc(lo[:, bass.ds(i * SB_, SB_)].unsqueeze(2), [EL, SB_, P]),
                                    ALU.is_equal).then_inc(oh, 1)
                    v.tensor_tensor(ohhi[:, x, :, :], bc(iota[0:EL, 0:NT].unsqueeze(1), [EL, SB_, NT]),
                                    bc(hi[:, bass.ds(i * SB_, SB_)].unsqueeze(2), [EL, SB_, NT]),
                                    ALU.is_equal).then_inc(oh, 1)

                def earlier(i):
                    v.wait_ge(lo_ps, i + 1)
                    v.tensor_tensor(before[:, :, :], plo[0:EL, 0:SB_, 0:EL], bc(triu[0:EL, 0:EL].unsqueeze(1), [EL, SB_, EL]),
                                    ALU.mult).then_inc(bef_done, 1)

                def batch(i, x, landings):
                    v.wait_ge(rank, i + 1)
                    v.tensor_tensor(picked[:, :, :], rk, ohhi[:, x, :, :], ALU.mult).then_inc(pick, 1)
                    v.wait_ge(pick, i + 1)
                    v.tensor_reduce(posf[:, :], picked[:, :, :], AX, ALU.add).then_inc(pos, 1)
                    v.wait_ge(pos, i + 1)
                    if landings is not None:
                        v.wait_ge(landed[x], 16 * SB_ * landings)
                    v.tensor_copy(posi[:, x, :], posf[:, :]).then_inc(staged, 1)
                    v.tensor_copy(rcs[:, x, :, :], rc[:, bass.ds(i * SB_, SB_), :]).then_inc(staged, 1)
                    onehots(i + 2, x)
                    earlier(i + 1)
                v.wait_ge(c_in, 32)
                v.tensor_copy(idb[:, :], ident[:, :]).then_inc(idb_done, 1)
                onehots(0, 0)
                onehots(1, 1)
                earlier(0)
                batch(0, 0, None)
                batch(1, 1, None)
                batch(2, 0, 1)
                with v.Fori(1, HB2) as k:
                    batch(2 * k + 1, 1, k)
                    batch(2 * k + 2, 0, k + 1)

            @block.scalar
            def _(a):
                def turned_copy(i):
                    a.wait_ge(turned, i + 1)
                    a.copy(oht[:, :, :], pt[:, 0:SB_, 0:EL]).then_inc(oht_done, 1)
                turned_copy(0)
                with a.Fori(0, NB) as i:
                    for s in range(SB_):
                        a.wait_ge(step, i * SB_ + s + 1)
                        a.copy(seen[:, s, :], pseen[:, 0:NT]).then_inc(snap, 1)
                        if s == 0:
                            a.copy(ohtf[:, :, :], pt[:, 0:SB_, 0:EL]).then_inc(ohtf_done, 1)
                    turned_copy(i + 1)

            @block.gpsimd
            def _(g):
                want = counter(g, "staged_want", 2)

                def scatter(x):
                    passed(g, staged, want, 2)
                    for s in range(SB_):
                        g.indirect_dma_start(W["sorted"], bass.IndirectOffsetOnAxis(ap=posi[:, x, s:s + 1], axis=0),
                                             rcs[:, x, s, :], None).then_inc(landed[x], 16)
                scatter(0)
                with g.Fori(0, HB2) as k:
                    scatter(1)
                    scatter(0)

            @block.tensor
            def _(pe):
                def turn(x, s):
                    return pe.transpose(pt[:, s, 0:EL], ohlo[:, x, s, :], idb[0:EL, 0:EL])

                def same_low(i):
                    pe.wait_ge(oht_done, i + 1)
                    for s in range(SB_):
                        m = pe.matmul(plo[0:EL, s, 0:EL], oht[:, s, :], oht[:, s, :], start=True, stop=True)
                    m.then_inc(lo_ps, 1)

                def batch(i, x, first=False):
                    for s in range(SB_):
                        pe.wait_ge(snap, i * SB_ + s + 1)
                        pe.matmul(pseen[:, 0:NT], ohlo[:, x, s, :], ohhi[:, x, s, :], start=False, stop=False,
                                  skip_group_check=True).then_inc(step, 1)
                        if s == 0:
                            pe.wait_ge(ohtf_done, i + 1)
                            if not first:
                                pe.wait_ge(pick, i)
                        pe.matmul(rk[:, s, :], ohtf[:, s, :], seen[:, s, :], start=(s == 0), stop=False,
                                  skip_group_check=True)
                        if s == 0:
                            pe.wait_ge(oh, 2 * i + 4)
                        t = turn(1 - x, s)
                    t.then_inc(turned, 1)
                    pe.wait_ge(bef_done, i + 1)
                    for s in range(SB_):
                        m = pe.matmul(rk[:, s, :], before[:, s, :], ohhi[:, x, s, :], start=False,
                                      stop=(s == SB_ - 1), skip_group_check=True)
                    m.then_inc(rank, 1)
                    same_low(i + 1)
                pe.wait_ge(idb_done, 1)
                pe.matmul(pseen[:, 0:NT], ident[:, :], pos_base[:, :], start=True, stop=False,
                          skip_group_check=True).then_inc(step, 1)
                pe.wait_ge(oh, 2)
                for s in range(SB_):
                    t = turn(0, s)
                t.then_inc(turned, 1)
                same_low(0)
                batch(0, 0, first=True)
                with pe.Fori(0, HB2) as k:
                    batch(2 * k + 1, 1)
                    batch(2 * k + 2, 0)


def load_sorted(nc, A, W, sem, ident, rowf, rowl, coli, tmap):
    LP = ST // 8
    with ExitStack() as cx:
        def sb(n, s, d=F32):
            return cx.enter_context(nc.sbuf_tensor("l_" + n, s, d))

        def ps(n, s, d=F32):
            return cx.enter_context(nc.psum_tensor("l_" + n, s, d))
        li = sb("li", [LP, 8, 2 * P], I32)
        lf = sb("lf", [LP, 2, 8, P])
        ri = sb("ri", [P, ST], I32)
        rl = sb("rl", [P, ST], I32)
        far = sb("far", [P, ST])
        rm = sb("rm", [P, ST])
        pr = ps("pr", [P, 8, P])
        pc = ps("pc", [P, 8, P])
        s_in = sem("l_in")
        lf_done = sem("l_lf")
        turned = sem("l_turned")
        ri_done = sem("l_ri")
        rl_done = sem("l_rl")
        rm_done = sem("l_rm")
        far_done = sem("l_far")
        end = sem("l_end")
        with nc.Block() as block:
            @block.sync
            def _(sp):
                sp.dma_start(li[:, :, :], W["sorted"].rearrange("(c p e) k -> p c (e k)", c=8, p=LP)).then_inc(s_in, 16)
                sp.dma_start(tmap[:, :], W["tmap"]).then_inc(s_in, 16)
                sp.wait_ge(s_in, 32)

            @block.vector
            def _(v):
                v.wait_ge(s_in, 32)
                for k in range(2):
                    v.tensor_copy(lf[:, k, :, :], li[:, :, :].rearrange("p c (e k) -> p c e k", k=2)[:, :, :, k]).then_inc(lf_done, 1)
                v.wait_ge(turned, 1)
                v.tensor_copy(rowf[:, :].rearrange("p (c n) -> p c n", c=8), pr[:, :, 0:LP]).then_inc(ri_done, 1)
                v.tensor_copy(ri[:, :].rearrange("p (c n) -> p c n", c=8), pr[:, :, 0:LP]).then_inc(ri_done, 1)
                v.tensor_copy(coli[:, 0:ST].rearrange("p (c n) -> p c n", c=8), pc[:, :, 0:LP]).then_inc(end, 1)
                v.memset(coli[:, ST:STX], 0).then_inc(end, 1)
                v.memset(rowl[:, ST:STX], 0.0).then_inc(end, 1)
                v.wait_ge(ri_done, 2)
                v.tensor_scalar(rl[:, :], ri[:, :], P - 1, None, ALU.bitwise_and).then_inc(rl_done, 1)
                v.tensor_scalar(far[:, :], rowf[:, :], float(N), 1000.0, ALU.is_ge, ALU.mult).then_inc(far_done, 1)
                v.wait_ge(rl_done, 1)
                v.tensor_copy(rm[:, :], rl[:, :]).then_inc(rm_done, 1)
                v.wait_ge(rm_done, 1)
                v.wait_ge(far_done, 1)
                v.tensor_tensor(rowl[:, 0:ST], rm[:, :], far[:, :], ALU.add).then_inc(end, 1)

            @block.tensor
            def _(pe):
                pe.wait_ge(lf_done, 2)
                for k, dst in ((0, pr), (1, pc)):
                    for c in range(8):
                        t = pe.transpose(dst[:, c, 0:LP], lf[:, k, c, :], ident[0:LP, 0:LP])
                t.then_inc(turned, 1)


def edge_scores(nc, A, W, sem, rowl, coli, tmap, q3, score):
    with ExitStack() as cx:
        def sb(n, s, d=F32):
            return cx.enter_context(nc.sbuf_tensor("e_" + n, s, d))

        def ps(n, s, d=F32):
            return cx.enter_context(nc.psum_tensor("e_" + n, s, d))
        iota = sb("iota", [P, P])
        idf = sb("idf", [P, P])
        idb = sb("idb", [P, P], BF16)
        oh = sb("oh", [P, RING, HB, P], BF16)
        oht = sb("oht", [P, 2, HB, P], BF16)
        kb = sb("kb", [P, RING, HB, C])
        prod = sb("prod", [P, HB, C])
        idx = sb("idx", [P, RING, HB], I32)
        pt = ps("pt", [P, 2, 1024], BF16)
        pq = ps("pq", [P, 2, HB, C])
        c_in = sem("e_c_in")
        idb_done = sem("e_idb")
        ohs = sem("e_onehots")
        turned = sem("e_turned")
        oht_done = sem("e_oht")
        q_picked = sem("e_q_picked")
        k_in = [sem(f"e_k_in{r}") for r in range(RING)]
        prod_done = sem("e_prod")
        score_done = sem("e_score")
        staged = sem("e_staged")
        with nc.Block() as block:
            @block.sync
            def _(sp):
                sp.dma_start(iota[:, :], A["iota"]).then_inc(c_in, 16)
                sp.dma_start(idf[:, :], A["ident"]).then_inc(c_in, 16)

            @block.gpsimd
            def _(g):
                want = counter(g, "e_staged_want", 1)
                with g.Fori(0, NHB // RING) as i:
                    for r in range(RING):
                        passed(g, staged, want, 1)
                        for s in range(HB):
                            g.indirect_dma_start(kb[:, r, s, :], None, W["k"],
                                                 bass.IndirectOffsetOnAxis(ap=idx[:, r, s:s + 1], axis=0))\
                             .then_inc(k_in[r], 16)

            @block.vector
            def _(v):
                sh = [P, HB, P]

                def onehot(hb, x):
                    v.tensor_tensor(oh[:, x, :, :], bc(iota[:, :].unsqueeze(1), sh),
                                    bc(rowl[:, bass.ds(hb * HB, HB)].unsqueeze(2), sh), ALU.is_equal).then_inc(ohs, 1)

                def stage(hb, r):
                    v.tensor_copy(idx[:, r, :], coli[:, bass.ds(hb * HB, HB)]).then_inc(staged, 1)

                def half(i, r, first=False):
                    hb = RING * i + r
                    v.wait_ge(q_picked, hb + 1)
                    v.wait_ge(k_in[r], 16 * HB * i + 16 * HB)
                    if not first:
                        v.wait_ge(score_done, hb)
                    v.tensor_tensor(prod[:, :, :], pq[:, r % 2, :, :], kb[:, r, :, :], ALU.mult).then_inc(prod_done, 1)
                    onehot(hb + RING - 1, (r + RING - 1) % RING)
                    v.wait_ge(prod_done, hb + 1)
                    stage(hb + RING, r)
                    v.tensor_reduce(score[:, bass.ds(hb * HB, HB), :],
                                    prod[:, :, :].rearrange("p s (d h) -> p s h d", h=H), AX, ALU.add)\
                     .then_inc(score_done, 1)

                for r in range(RING):
                    stage(r, r)
                v.wait_ge(c_in, 32)
                v.tensor_copy(idb[:, :], idf[:, :]).then_inc(idb_done, 1)
                for r in range(RING - 1):
                    onehot(r, r)
                for r in range(RING):
                    half(0, r, first=(r == 0))
                with v.Fori(1, NHB // RING) as i:
                    for r in range(RING):
                        half(i, r)

            @block.scalar
            def _(a):
                with a.Fori(0, NHB // 2) as i:
                    for x in range(2):
                        a.wait_ge(turned, 2 * i + x + 1)
                        a.copy(oht[:, x, :, :], pt[:, x, 0:HB * P].rearrange("p (s n) -> p s n", s=HB)).then_inc(oht_done, 1)
                a.wait_ge(turned, NHB + 1)

            @block.tensor
            def _(pe):
                pe.wait_ge(idb_done, 1)

                def turn(hb, r):
                    x = r % 2
                    pe.wait_ge(ohs, hb + 1)
                    for s in range(HB):
                        t = pe.transpose(pt[:, x, s * P:(s + 1) * P], oh[:, r, s, :], idb[:, :])
                    t.then_inc(turned, 1)

                def half(i, r, first=False):
                    hb = RING * i + r
                    x = r % 2
                    tiles = node_tiles(nc, mybir.EngineType.PE, tmap, hb)
                    turn(hb + 1, (r + 1) % RING)
                    pe.wait_ge(oht_done, hb + 1)
                    if not (first and r < 2):
                        pe.wait_ge(prod_done, hb - 1)
                    for s in range(HB):
                        for part in range(3):
                            m = pe.matmul(pq[:, x, s, :], oht[:, x, s, :],
                                          q3[:, bass.ds(tiles[s], 1), part, :],
                                          start=(part == 0), stop=(part == 2))
                    m.then_inc(q_picked, 1)

                turn(0, 0)
                for r in range(RING):
                    half(0, r, first=True)
                with pe.Fori(1, NHB // RING) as i:
                    for r in range(RING):
                        half(i, r)


def softmax_edges(nc, A, W, sem, ident, rowf, score):
    L = GPC * P
    G = 5
    NS = GPC // G
    assert NS * G == GPC and NS % 2 == 1
    with ExitStack() as cx:
        def sb(n, s, d=F32):
            return cx.enter_context(nc.sbuf_tensor("x_" + n, s, d))

        def ps(n, s, d=F32):
            return cx.enter_context(nc.psum_tensor("x_" + n, s, d))
        sT = sb("sT", [P, L])
        rT = sb("rT", [P, L])
        cut = sb("cut", [P, L + 1])
        fwd = sb("fwd", [P, L])
        both = rT
        st_s = sb("st_s", [P, 2, G, CH, H])
        st_r = sb("st_r", [P, 2, G, CH, H])
        pack = sb("pack", [P, 2, 3])
        ch = sb("ch", [H, 2, CH, 3])
        one = sb("one", [H, 2, CH])
        link = sb("link", [H, 2, CH])
        join = sb("join", [H, 2, CH])
        gate = sb("gate", [H, 2, CH])
        lnk = sb("lnk", [H, 2, CH])
        state = sb("state", [H, 2, CH])
        car = sb("car", [H, 2, CH])
        carry = sb("carry", [P, 2])
        p_s = ps("p_s", [P, 2, G + 3, P])
        p_r = ps("p_r", [P, 2, G + 3, P])
        rows_staged = sem("x_rows_staged")
        s_staged = sem("x_s_staged")
        turned = sem("x_turned")
        sT_done = sem("x_sT")
        rT_done = sem("x_rT")
        cut_done = sem("x_cut")
        fwd_done = sem("x_fwd")
        both_done = sem("x_both")
        packed = sem("x_packed")
        ends_out = sem("x_ends_out")
        ends_in = sem("x_ends_in")
        chain = sem("x_chain")
        carry_out = sem("x_carry_out")
        carry_in = sem("x_carry_in")
        diff = sem("x_diff")
        exp_done = sem("x_exp")
        staged2 = sem("x_staged2")
        turned2 = sem("x_turned2")
        back = sem("x_back")
        s_view = score[:, :, :].rearrange("p (c g) h -> p g c h", c=CH)
        r_view = rowf[:, :].rearrange("p (c g) -> p g c", c=CH)
        with nc.Block() as block:
            @block.sync
            def _(sp):
                for w in range(2):
                    sp.wait_ge(packed, 5 + w)
                    sp.dma_start(W["ends"][w], pack[:, w, :]).then_inc(ends_out, 16)
                    sp.wait_ge(ends_out, 16 * w + 16)
                    sp.dma_start(ch[:, w, :, :], W["ends"][w].rearrange("(c h) k -> h c k", h=H)).then_inc(ends_in, 16)
                    sp.wait_ge(chain, (w + 1) * CHAIN)
                    sp.dma_start(W["carry"][w].rearrange("c h -> h c"), car[:, w, :], allow_slow_non_contiguous=True).then_inc(carry_out, 16)
                    sp.wait_ge(carry_out, 16 * w + 16)
                    sp.dma_start(carry[:, w:w + 1], W["carry"][w].rearrange("c (h o) -> (c h) o", o=1)).then_inc(carry_in, 16)
                sp.wait_ge(carry_in, 32)

            @block.vector
            def _(v):
                shr = [P, G, CH, H]

                def stage_rows(i, x):
                    v.tensor_copy(st_r[:, x, :, :, :], bc(r_view[:, bass.ds(i * G, G), :].unsqueeze(3), shr)).then_inc(rows_staged, 1)

                def keep_rows(i, x):
                    v.wait_ge(turned, i + 1)
                    v.tensor_copy(rT[:, bass.ds(i * G * P, G * P)].rearrange("p (g e) -> p g e", g=G),
                                  p_r[:, x, 0:G, :]).then_inc(rT_done, 1)

                stage_rows(0, 0)
                stage_rows(1, 1)
                with v.Fori(0, (NS - 3) // 2) as k:
                    for x in range(2):
                        keep_rows(2 * k + x, x)
                        stage_rows(2 * k + x + 2, x)
                keep_rows(NS - 3, 0)
                stage_rows(NS - 1, 0)
                keep_rows(NS - 2, 1)
                keep_rows(NS - 1, 0)
                v.memset(cut[:, 0:1], 0.0).then_inc(cut_done, 1)
                v.memset(cut[:, L:L + 1], 0.0).then_inc(cut_done, 1)
                v.wait_ge(rT_done, GPC // G)
                v.tensor_tensor(cut[:, 1:L], rT[:, 1:L], rT[:, 0:L - 1], ALU.not_equal).then_inc(cut_done, 1)
                v.wait_ge(cut_done, 3)
                v.tensor_scalar(cut[:, 1:L], cut[:, 1:L], -BIG, None, ALU.mult).then_inc(cut_done, 1)
                for w in range(2):
                    v.tensor_copy(pack[:, w, 1:2], rT[:, 0:1]).then_inc(packed, 1)
                    v.tensor_copy(pack[:, w, 2:3], rT[:, L - 1:L]).then_inc(packed, 1)
                v.wait_ge(cut_done, 4)
                v.wait_ge(sT_done, GPC // G)

                def carries(w):
                    n = [w * CHAIN]

                    def then(ins):
                        n[0] += 1
                        ins.then_inc(chain, 1)
                        v.wait_ge(chain, n[0])
                    v.wait_ge(ends_in, 16 * w + 16)
                    then(v.tensor_tensor(one[:, w, :], ch[:, w, :, 1], ch[:, w, :, 2], ALU.is_equal))
                    then(v.memset(link[:, w, 0:1], 0.0))
                    then(v.tensor_tensor(link[:, w, 1:CH], ch[:, w, 1:CH, 1], ch[:, w, 0:CH - 1, 2], ALU.is_equal))
                    then(v.tensor_scalar(lnk[:, w, :], link[:, w, :], -1.0, BIG, ALU.add, ALU.mult))
                    then(v.memset(join[:, w, :], 0.0))
                    if w == 0:
                        then(v.tensor_tensor(join[:, w, :], one[:, w, :], link[:, w, :], ALU.mult))
                    else:
                        then(v.tensor_tensor(join[:, w, 0:CH - 1], one[:, w, 0:CH - 1], link[:, w, 1:CH], ALU.mult))
                    then(v.tensor_scalar(gate[:, w, :], join[:, w, :], -1.0, BIG, ALU.add, ALU.mult))
                    then(v.memset(car[:, w, :], -BIG))
                    if w == 0:
                        then(v.tensor_tensor_scan(state[:, w, :], gate[:, w, :], ch[:, w, :, 0], -BIG, ALU.add, ALU.max))
                        then(v.tensor_tensor(car[:, w, 1:CH], state[:, w, 0:CH - 1], lnk[:, w, 1:CH], ALU.add))
                    else:
                        then(v.tensor_tensor_scan(state[:, w, ::-1], gate[:, w, ::-1], ch[:, w, ::-1, 0], -BIG,
                                                  ALU.add, ALU.max))
                        then(v.tensor_tensor(car[:, w, 0:CH - 1], state[:, w, 1:CH], lnk[:, w, 1:CH], ALU.add))
                    assert n[0] == (w + 1) * CHAIN
                    v.wait_ge(carry_in, 16 * w + 16)

                v.tensor_tensor_scan(fwd[:, :], cut[:, 0:L], sT[:, :], -BIG, ALU.add, ALU.max).then_inc(fwd_done, 1)
                v.wait_ge(fwd_done, 1)
                v.tensor_copy(pack[:, 0, 0:1], fwd[:, L - 1:L]).then_inc(packed, 1)
                v.wait_ge(packed, 5)
                carries(0)
                v.tensor_tensor_scan(fwd[:, :], cut[:, 0:L], sT[:, :], carry[:, 0:1], ALU.add, ALU.max).then_inc(fwd_done, 1)
                v.wait_ge(fwd_done, 2)
                v.tensor_tensor_scan(both[:, ::-1], cut[:, L:0:-1], fwd[:, ::-1], -BIG, ALU.add, ALU.max).then_inc(both_done, 1)
                v.wait_ge(both_done, 1)
                v.tensor_copy(pack[:, 1, 0:1], both[:, 0:1]).then_inc(packed, 1)
                v.wait_ge(packed, 6)
                carries(1)
                v.tensor_tensor_scan(both[:, ::-1], cut[:, L:0:-1], fwd[:, ::-1], carry[:, 1:2], ALU.add, ALU.max).then_inc(both_done, 1)
                v.wait_ge(both_done, 2)
                v.tensor_tensor(sT[:, :], sT[:, :], both[:, :], ALU.subtract).then_inc(diff, 1)

                def keep_exp(i, x):
                    v.wait_ge(turned2, i + 1)
                    v.tensor_copy(s_view[:, bass.ds(i * G, G), :, :],
                                  p_s[:, x, 0:G, :].rearrange("p g (c h) -> p g c h", h=H)).then_inc(back, 1)
                keep_exp(0, 0)
                with v.Fori(0, (NS - 1) // 2) as k:
                    keep_exp(2 * k + 1, 1)
                    keep_exp(2 * k + 2, 0)

            @block.scalar
            def _(a):
                def stage_scores(i, x):
                    a.copy(st_s[:, x, :, :, :], s_view[:, bass.ds(i * G, G), :, :]).then_inc(s_staged, 1)

                def keep_scores(i, x):
                    a.wait_ge(turned, i + 1)
                    a.copy(sT[:, bass.ds(i * G * P, G * P)].rearrange("p (g e) -> p g e", g=G),
                           p_s[:, x, 0:G, :]).then_inc(sT_done, 1)

                def stage_exp(i, x, first=False):
                    if not first:
                        a.wait_ge(turned2, i - 1)
                    a.copy(st_s[:, x, :, :, :].rearrange("p g c h -> p g (c h)"),
                           fwd[:, bass.ds(i * G * P, G * P)].rearrange("p (g e) -> p g e", g=G)).then_inc(staged2, 1)

                stage_scores(0, 0)
                stage_scores(1, 1)
                with a.Fori(0, (NS - 3) // 2) as k:
                    for x in range(2):
                        keep_scores(2 * k + x, x)
                        stage_scores(2 * k + x + 2, x)
                keep_scores(NS - 3, 0)
                stage_scores(NS - 1, 0)
                keep_scores(NS - 2, 1)
                keep_scores(NS - 1, 0)
                a.wait_ge(diff, 1)
                a.activation(fwd[:, :], sT[:, :], ACT.Exp, scale=SCALE).then_inc(exp_done, 1)
                a.wait_ge(exp_done, 1)
                stage_exp(0, 0, first=True)
                stage_exp(1, 1, first=True)
                stage_exp(2, 0)
                with a.Fori(1, (NS - 1) // 2) as k:
                    stage_exp(2 * k + 1, 1)
                    stage_exp(2 * k + 2, 0)

            @block.tensor
            def _(pe):
                def turn(i, x, first=False):
                    pe.wait_ge(s_staged, i + 1)
                    pe.wait_ge(rows_staged, i + 1)
                    if not first:
                        pe.wait_ge(sT_done, i - 1)
                        pe.wait_ge(rT_done, i - 1)
                    for g in range(G):
                        pe.transpose(p_s[:, x, g, :], st_s[:, x, g, :, :].rearrange("p c h -> p (c h)"), ident[:, :])
                        t = pe.transpose(p_r[:, x, g, :], st_r[:, x, g, :, :].rearrange("p c h -> p (c h)"), ident[:, :])
                    t.then_inc(turned, 1)

                def turn_back(i, x, first=False):
                    pe.wait_ge(staged2, i + 1)
                    if not first:
                        pe.wait_ge(back, i - 1)
                    for g in range(G):
                        t = pe.transpose(p_s[:, x, g, :], st_s[:, x, g, :, :].rearrange("p c h -> p (c h)"), ident[:, :])
                    t.then_inc(turned2, 1)
                for task in (turn, turn_back):
                    task(0, 0, first=True)
                    task(1, 1, first=True)
                    task(2, 0)
                    with pe.Fori(1, (NS - 1) // 2) as k:
                        task(2 * k + 1, 1)
                        task(2 * k + 2, 0)


CHAIN = 10


def aggregate(nc, A, W, sem, rowl, coli, tmap, score, acc):
    with ExitStack() as cx:
        def sb(n, s, d=F32):
            return cx.enter_context(nc.sbuf_tensor("g_" + n, s, d))

        def ps(n, s, d=F32):
            return cx.enter_context(nc.psum_tensor("g_" + n, s, d))
        iota = sb("iota", [P, P])
        oh = sb("oh", [P, 2, HB, P])
        vb = sb("vb", [P, RING, HB, C])
        w = sb("w", [P, 2, HB, C + H])
        idx = sb("idx", [P, RING, HB], I32)
        pa = ps("pa", [P, 2, HB, 512])
        c_in = sem("g_c_in")
        zeroed = sem("g_zeroed")
        ohs = sem("g_onehots")
        v_in = [sem(f"g_v_in{r}") for r in range(RING)]
        staged = sem("g_staged")
        weighted = sem("g_weighted")
        p_put = sem("g_p_put")
        summed = sem("g_summed")
        acc_done = sem("g_acc")
        with nc.Block() as block:
            @block.sync
            def _(sp):
                sp.dma_start(iota[:, :], A["iota"]).then_inc(c_in, 16)

            @block.gpsimd
            def _(g):
                want = counter(g, "g_staged_want", 1)
                with g.Fori(0, NHB // RING) as i:
                    for r in range(RING):
                        passed(g, staged, want, 1)
                        for s in range(HB):
                            g.indirect_dma_start(vb[:, r, s, :], None, W["v"],
                                                 bass.IndirectOffsetOnAxis(ap=idx[:, r, s:s + 1], axis=0))\
                             .then_inc(v_in[r], 16)

            @block.scalar
            def _(a):
                def put(i, x, first=False):
                    hb = 2 * i + x
                    if not first:
                        a.wait_ge(summed, HB * (hb - 1))
                    a.copy(w[:, x, :, C:C + H], score[:, bass.ds(hb * HB, HB), :]).then_inc(p_put, 1)
                for x in range(2):
                    put(0, x, first=True)
                with a.Fori(1, NHB // 2) as i:
                    for x in range(2):
                        put(i, x)

            @block.vector
            def _(v):
                def onehot(hb, x, s):
                    v.tensor_scalar(oh[:, x, s, :], iota[:, :], rowl[:, bass.ds(hb * HB + s, 1)], None,
                                    ALU.is_equal).then_inc(ohs, 1)

                def stage(hb, r):
                    v.tensor_copy(idx[:, r, :], coli[:, bass.ds(hb * HB, HB)]).then_inc(staged, 1)

                def weight(hb, r):
                    v.tensor_tensor(w[:, r % 2, :, 0:C].rearrange("p s (d h) -> p s d h", h=H),
                                    vb[:, r, :, :].rearrange("p s (d h) -> p s d h", h=H),
                                    bc(score[:, bass.ds(hb * HB, HB), :].unsqueeze(2), [P, HB, D, H]), ALU.mult)\
                     .then_inc(weighted, 1)

                def add(hb, x, s, tiles, first=False):
                    v.wait_ge(summed, HB * hb + s + 1)
                    if not first:
                        v.wait_ge(acc_done, HB * hb + s)
                    at = acc[:, bass.ds(tiles[s], 1), :]
                    v.tensor_tensor(at, at, pa[:, x, s, 0:C + H].unsqueeze(1), ALU.add).then_inc(acc_done, 1)

                def half(i, r, first=False):
                    hb = RING * i + r
                    v.wait_ge(v_in[r], 16 * HB * i + 16 * HB)
                    weight(hb, r)
                    late = not (first and r == 0)
                    tiles = node_tiles(nc, mybir.EngineType.DVE, tmap, hb - 1) if late else None
                    for s in range(HB):
                        if late:
                            add(hb - 1, 1 - r % 2, s, tiles, first and r == 1 and s == 0)
                        if s == 0:
                            v.wait_ge(weighted, hb + 1)
                            stage(hb + RING, r)
                        onehot(hb + 1, 1 - r % 2, s)

                for r in range(RING):
                    stage(r, r)
                v.memset(acc[:, :, :], 0.0).then_inc(zeroed, 1)
                v.wait_ge(c_in, 16)
                for s in range(HB):
                    onehot(0, 0, s)
                v.wait_ge(zeroed, 1)
                for r in range(RING):
                    half(0, r, first=True)
                with v.Fori(1, NHB // RING) as i:
                    for r in range(RING):
                        half(i, r)
                tiles = node_tiles(nc, mybir.EngineType.DVE, tmap, NHB - 1)
                for s in range(HB):
                    add(NHB - 1, 1, s, tiles)
                v.wait_ge(acc_done, HB * NHB)

            @block.tensor
            def _(pe):
                def half(i, x, first=False):
                    hb = 2 * i + x
                    pe.wait_ge(p_put, hb + 1)
                    if not first:
                        pe.wait_ge(acc_done, HB * (hb - 1))
                    pe.wait_ge(ohs, HB * hb + HB)
                    pe.wait_ge(weighted, hb + 1)
                    for s in range(HB):
                        pe.matmul(pa[:, x, s, 0:C + H], oh[:, x, s, :], w[:, x, s, :], start=True, stop=True).then_inc(summed, 1)
                for x in range(2):
                    half(0, x, first=True)
                with pe.Fori(1, NHB // 2) as i:
                    for x in range(2):
                        half(i, x)


def combine(nc, A, W, sem, ident, ctxbd, acc, first, second):
    with ExitStack() as cx:
        def sb(n, s, d=F32):
            return cx.enter_context(nc.sbuf_tensor("c_" + n, s, d))

        def ps(n, s, d=F32):
            return cx.enter_context(nc.psum_tensor("c_" + n, s, d))
        wqm = sb("wqm", [P, KC, C])
        wpr = sb("wpr", [P, KC, C])
        wo = sb("wo", [P, KC, C])
        wg1 = sb("wg1", [P, KC, GH])
        wg2 = sb("wg2", [GH, C])
        bg1 = sb("bg1", [GH, 1])
        bg2 = sb("bg2", [P, KC])
        bo = sb("bo", [P, C])
        bpr = sb("bpr", [P, C])
        wgt = sb("wgt", [P, KC, NEXP])
        bgt = sb("bgt", [P, NEXP])
        iota = sb("iota", [P, NEXP])
        bsum = sb("bsum", [P, C])
        xnT = sb("xnT", [P, KC, GN])
        xmT = sb("xmT", [P, KC, GN])
        xg = sb("xg", [P, TPG, C])
        qmT = sb("qmT", [P, KC, GN])
        hgT = sb("hgT", [GH, GN])
        gT = sb("gT", [P, KC, GN])
        prT = sb("prT", [P, KC, GN])
        z = sb("z", [P, TPG, H])
        rz = sb("rz", [P, TPG, H])
        gn = sb("gn", [P, TPG, C])
        gnT = sb("gnT", [P, KC, GN])
        xb = sb("xb", [P, TPG, C])
        x2 = sb("x2", [P, TPG, C])
        st = sb("st", [P, TPG, 6])
        mv = sb("mv", [P, TPG, 2])
        ve = sb("ve", [P, TPG])
        sd = sb("sd", [P, TPG])
        rs = sb("rs", [P, TPG])
        xl = sb("xl", [P, TPG, C])
        xlT = sb("xlT", [P, KC, GN])
        gs = sb("gs", [P, TPG, NEXP])
        top = sb("top", [P, TPG, 8])
        tidx = sb("tidx", [P, TPG, 8], U32)
        tif = sb("tif", [P, TPG, 8])
        zero = sb("zero", [P, XROWS // P, C])
        pA = ps("pA", [P, KC, GN])
        pB = ps("pB", [P, KC, GN])
        pH = ps("pH", [P, GN])
        pD = ps("pD", [P, KC, GN])
        pG = ps("pG", [P, GN])
        names = ["w_in", "t_in", "x_in", "bsum_done", "qm_ps", "qm_done", "o_ps", "hg_ps", "hg_done", "g_ps", "g_done", "pr_done",
                 "z_done", "rz_done", "gn_done", "gn_turned", "gnT_done", "y_ps", "xb_done", "x2_done", "stats", "aggr", "var",
                 "std", "rstd", "xl_done", "xl_turned", "xlT_done", "gs_ps", "gs_done", "top_done", "tidx_done", "tif_done",
                 "m1_done", "m2_done", "stored", "zero_done", "xs_filled"]
        s = {n: sem("c_" + n) for n in names}
        wnames = [(wqm, "wqm"), (wpr, "wpr"), (wo, "wo"), (wg1, "wg1"), (wg2, "wg2"), (bg1, "bg1"), (bg2, "bg2"), (bo, "bo"),
                  (bpr, "bpr"), (wgt, "wgt"), (bgt, "bgt"), (iota, "iota8")]
        with nc.Block() as block:
            @block.sync
            def _(sp):
                def load_turned(i):
                    sp.dma_start(xnT[:, :, :], W["xnT"][:, :, bass.ds(i * GN, GN)]).then_inc(s["t_in"], 16)
                    sp.dma_start(xmT[:, :, :], W["xmT"][:, :, bass.ds(i * GN, GN)]).then_inc(s["t_in"], 16)

                def load_x(i):
                    sp.dma_start(xg[:, :, :], rows(A["x"], i)).then_inc(s["x_in"], 16)

                def store(i):
                    sp.wait_ge(s["x2_done"], TPG * i + TPG)
                    sp.wait_ge(s["xl_done"], TPG * i + TPG)
                    sp.dma_start(rows(W["x2"], i), x2[:, :, :]).then_inc(s["stored"], 16)
                    sp.dma_start(rows(W["xl"], i), xl[:, :, :]).then_inc(s["stored"], 16)

                def next_inputs(i):
                    sp.wait_ge(s["xb_done"], i + 1)
                    load_x(i + 1)
                load_turned(0)
                for dst, n in wnames:
                    full = dst[:, :, :] if len(dst.shape) == 3 else dst[:, :]
                    sp.dma_start(full, A[n]).then_inc(s["w_in"], 16)
                load_x(0)
                sp.wait_ge(s["zero_done"], 1)
                for n in range(XFILL):
                    sp.dma_start(W["xs"][n * XROWS:(n + 1) * XROWS, :].rearrange("(p t) c -> p t c", p=P),
                                 zero[:, :, :]).then_inc(s["xs_filled"], 16)
                sp.wait_ge(s["hg_ps"], 1)
                load_turned(1)
                next_inputs(0)
                with sp.Fori(1, NG - 1) as i:
                    sp.wait_ge(s["hg_ps"], i + 1)
                    load_turned(i + 1)
                    store(i - 1)
                    next_inputs(i)
                store(NG - 2)
                store(NG - 1)
                sp.wait_ge(s["stored"], 32 * NG)
                sp.wait_ge(s["xs_filled"], 16 * XFILL)

            @block.vector
            def _(v):
                want_stats = counter(v, "x2_stats_want", TPG)
                want_gs = counter(v, "scores_want", 1)
                want_top = counter(v, "top_want", TPG)

                def graph_out(i, first=False):
                    v.tensor_scalar(z[:, :, :], acc[:, bass.ds(i * TPG, TPG), C:C + H], 1e-30, None,
                                    ALU.max).then_inc(s["z_done"], 1)
                    v.wait_ge(s["z_done"], i + 1)
                    if not first:
                        v.wait_ge(s["gn_done"], TPG * i)
                        v.wait_ge(s["gn_turned"], i)
                    v.reciprocal(rz[:, :, :], z[:, :, :]).then_inc(s["rz_done"], 1)
                    v.wait_ge(s["rz_done"], i + 1)
                    for j in range(TPG):
                        v.tensor_tensor(gn[:, j, :].rearrange("p (d h) -> p d h", h=H),
                                        acc[:, bass.ds(i * TPG + j, 1), 0:C].rearrange("p o (d h) -> p (o d) h", h=H),
                                        bc(rz[:, j, :].unsqueeze(1), [P, D, H]), ALU.mult).then_inc(s["gn_done"], 1)

                def gated(i):
                    v.wait_ge(s["o_ps"], i + 1)
                    v.wait_ge(s["g_done"], KC * i + KC)
                    v.tensor_tensor(prT[:, :, :], pB[:, :, :], gT[:, :, :], ALU.mult).then_inc(s["pr_done"], 1)

                def biased_x(i):
                    v.wait_ge(s["x_in"], 16 * i + 16)
                    v.tensor_tensor(xb[:, :, :], xg[:, :, :], bc(bsum[:, :].unsqueeze(1), [P, TPG, C]), ALU.add)\
                     .then_inc(s["xb_done"], 1)

                def sums_and_norm(i, first=False, last=False):
                    if not first:
                        v.wait_ge(s["stored"], 32 * i)
                    v.wait_ge(s["xb_done"], i + 1)
                    v.wait_ge(s["y_ps"], i + 1)
                    for j in range(TPG):
                        v.tensor_tensor(x2[:, j, :], xb[:, j, :], pD[:, j // 2, (j % 2) * C:(j % 2 + 1) * C], ALU.add)\
                         .then_inc(s["x2_done"], 1)
                    for j in range(TPG):
                        v.wait_ge(s["x2_done"], TPG * i + j + 1)
                        v.bn_stats(st[:, j, :], x2[:, j, :]).then_inc(s["stats"], 1)
                    passed(v, s["stats"], want_stats, TPG, TPG * (i + 1) if last else None)
                    for j in range(TPG):
                        v.bn_aggr(mv[:, j, :], st[:, j, :]).then_inc(s["aggr"], 1)
                    v.wait_ge(s["aggr"], TPG * i + TPG)
                    v.tensor_scalar(ve[:, :], mv[:, :, 1], EPS, None, ALU.add).then_inc(s["var"], 1)
                    v.wait_ge(s["std"], i + 1)
                    v.reciprocal(rs[:, :], sd[:, :]).then_inc(s["rstd"], 1)
                    v.wait_ge(s["rstd"], i + 1)
                    for j in range(TPG):
                        v.tensor_scalar(xl[:, j, :], x2[:, j, :], mv[:, j, 0:1], rs[:, j:j + 1],
                                        ALU.subtract, ALU.mult).then_inc(s["xl_done"], 1)

                def xl_copy(i):
                    v.wait_ge(s["xl_turned"], i + 1)
                    v.tensor_copy(xlT[:, :, :], pA[:, :, :]).then_inc(s["xlT_done"], 1)

                def best_two(i, last=False):
                    v.wait_ge(s["gs_ps"], i + 1)
                    v.tensor_tensor(gs[:, :, :], pG[:, 0:TPG * NEXP].rearrange("p (j e) -> p j e", j=TPG),
                                    bc(bgt[:, :].unsqueeze(1), [P, TPG, NEXP]), ALU.add).then_inc(s["gs_done"], 1)
                    passed(v, s["gs_done"], want_gs, 1, i + 1 if last else None)
                    for j in range(TPG):
                        v.max(top[:, j, :], gs[:, j, :]).then_inc(s["top_done"], 1)
                    passed(v, s["top_done"], want_top, TPG, TPG * (i + 1) if last else None)
                    for j in range(TPG):
                        v.max_index(tidx[:, j, :], top[:, j, :], gs[:, j, :]).then_inc(s["tidx_done"], 1)
                    v.wait_ge(s["tidx_done"], TPG * i + TPG)
                    v.tensor_copy(tif[:, :, :], tidx[:, :, :]).then_inc(s["tif_done"], 1)
                    v.wait_ge(s["tif_done"], i + 1)
                    sh = [P, TPG, NEXP]
                    for rank, mask, done in ((0, first, "m1_done"), (1, second, "m2_done")):
                        v.tensor_tensor(mask[:, bass.ds(i * TPG, TPG), :], bc(iota[:, :].unsqueeze(1), sh),
                                        bc(tif[:, :, rank:rank + 1], sh), ALU.is_equal).then_inc(s[done], 1)
                    v.wait_ge(s["m1_done"], i + 1)
                    v.wait_ge(s["m2_done"], i + 1)
                graph_out(0, first=True)
                v.wait_ge(s["w_in"], 16 * len(wnames))
                v.tensor_tensor(bsum[:, :], bo[:, :], bpr[:, :], ALU.add).then_inc(s["bsum_done"], 1)
                v.wait_ge(s["bsum_done"], 1)
                gated(0)
                biased_x(0)
                graph_out(1)
                sums_and_norm(0, first=True)
                xl_copy(0)
                gated(1)
                biased_x(1)
                best_two(0)
                graph_out(2)
                with v.Fori(2, NG - 1) as i:
                    sums_and_norm(i - 1)
                    xl_copy(i - 1)
                    gated(i)
                    biased_x(i)
                    best_two(i - 1)
                    graph_out(i + 1)
                sums_and_norm(NG - 2, last=True)
                xl_copy(NG - 2)
                gated(NG - 1)
                biased_x(NG - 1)
                best_two(NG - 2, last=True)
                sums_and_norm(NG - 1, last=True)
                xl_copy(NG - 1)
                best_two(NG - 1, last=True)

            @block.gpsimd
            def _(g):
                g.memset(zero[:, :, :], 0.0).then_inc(s["zero_done"], 1)

            @block.scalar
            def _(a):
                def std(i):
                    a.wait_ge(s["var"], i + 1)
                    a.activation(sd[:, :], ve[:, :], ACT.Sqrt).then_inc(s["std"], 1)

                def group(i, first=False):
                    a.wait_ge(s["qm_ps"], i + 1)
                    a.copy(qmT[:, :, :], pA[:, :, :]).then_inc(s["qm_done"], 1)
                    if not first:
                        std(i - 1)
                    a.wait_ge(s["gn_turned"], i + 1)
                    a.copy(gnT[:, :, :], pD[:, :, :]).then_inc(s["gnT_done"], 1)
                    a.wait_ge(s["hg_ps"], i + 1)
                    a.activation(hgT[:, :], pH[0:GH, :], ACT.Gelu, bias=bg1[:, 0:1]).then_inc(s["hg_done"], 1)
                    a.wait_ge(s["g_ps"], i + 1)
                    for k in range(KC):
                        a.activation(gT[:, k, :], pD[:, k, :], ACT.Sigmoid, bias=bg2[:, k:k + 1]).then_inc(s["g_done"], 1)
                a.wait_ge(s["w_in"], 16 * len(wnames))
                group(0, first=True)
                with a.Fori(1, NG) as i:
                    group(i)
                std(NG - 1)

            @block.tensor
            def _(pe):
                def turn_xl(i):
                    pe.wait_ge(s["xl_done"], TPG * i + TPG)
                    for j in range(TPG):
                        for k in range(KC):
                            t = pe.transpose(pA[:, k, j * P:(j + 1) * P], xl[:, j, k * P:(k + 1) * P], ident[:, :])
                    t.then_inc(s["xl_turned"], 1)

                def expert_scores(i):
                    pe.wait_ge(s["xlT_done"], i + 1)
                    for j in range(TPG):
                        for k in range(KC):
                            t = pe.matmul(pG[:, j * NEXP:(j + 1) * NEXP], xlT[:, k, j * P:(j + 1) * P], wgt[:, k, :],
                                          start=(k == 0), stop=(k == KC - 1))
                    t.then_inc(s["gs_ps"], 1)

                def group(i, first=False):
                    pe.wait_ge(s["t_in"], 32 * i + 32)
                    for m in range(KC):
                        for k in range(KC):
                            t = pe.matmul(pA[:, m, :], wqm[:, k, m * P:(m + 1) * P], xnT[:, k, :], start=(k == 0), stop=(k == KC - 1))
                    t.then_inc(s["qm_ps"], 1)
                    pe.wait_ge(s["gn_done"], TPG * i + TPG)
                    if not first:
                        pe.wait_ge(s["x2_done"], TPG * i)
                    for j in range(TPG):
                        for k in range(KC):
                            t = pe.transpose(pD[:, k, j * P:(j + 1) * P], gn[:, j, k * P:(k + 1) * P], ident[:, :])
                    t.then_inc(s["gn_turned"], 1)
                    for k in range(KC):
                        t = pe.matmul(pH[0:GH, :], wg1[:, k, :], xmT[:, k, :], start=(k == 0), stop=(k == KC - 1))
                    t.then_inc(s["hg_ps"], 1)
                    pe.wait_ge(s["qm_done"], i + 1)
                    for m in range(KC):
                        for k in range(KC):
                            t = pe.matmul(pB[:, m, :], ctxbd[:, k, m * P:(m + 1) * P], qmT[:, k, :], start=(k == 0), stop=(k == KC - 1))
                    t.then_inc(s["o_ps"], 1)
                    pe.wait_ge(s["gnT_done"], i + 1)
                    pe.wait_ge(s["hg_done"], i + 1)
                    for m in range(KC):
                        t = pe.matmul(pD[:, m, :], wg2[:, m * P:(m + 1) * P], hgT[:, :], start=True, stop=True)
                    t.then_inc(s["g_ps"], 1)
                    if not first:
                        turn_xl(i - 1)
                        expert_scores(i - 1)
                    pe.wait_ge(s["pr_done"], i + 1)
                    pe.wait_ge(s["g_done"], KC * i + KC)
                    for j in range(TPG):
                        o = pD[:, j // 2, (j % 2) * C:(j % 2 + 1) * C]
                        for k in range(KC):
                            pe.matmul(o, prT[:, k, j * P:(j + 1) * P], wpr[:, k, :], start=(k == 0), stop=False)
                        for k in range(KC):
                            t = pe.matmul(o, gnT[:, k, j * P:(j + 1) * P], wo[:, k, :], start=False, stop=(k == KC - 1))
                    t.then_inc(s["y_ps"], 1)
                pe.wait_ge(s["w_in"], 16 * len(wnames))
                group(0, first=True)
                with pe.Fori(1, NG) as i:
                    group(i)
                turn_xl(NG - 1)
                expert_scores(NG - 1)


def route(nc, A, W, sem, ident, first, second, slot_i, slot_g, emap, weights):
    TE = NT * NEXP
    with ExitStack() as cx:
        def sb(n, s, d=F32):
            return cx.enter_context(nc.sbuf_tensor("r_" + n, s, d))

        def ps(n, s, d=F32):
            return cx.enter_context(nc.psum_tensor("r_" + n, s, d))
        valid = sb("valid", [P, NT])
        dump = sb("dump", [P, 2, NT])
        triu = sb("triu", [P, P])
        jcol = sb("jcol", [P, 1])
        ones = sb("ones", [P, P])
        zero = sb("zero", [P, NT])
        pick = sb("pick", [P, 2, NT, NEXP])
        both = sb("both", [P, NT, NEXP])
        incl = sb("incl", [P, NT, NEXP])
        tot = sb("tot", [P, NT, NEXP])
        t1 = sb("t1", [P, NEXP], I32)
        t2 = sb("t2", [P, NEXP], I32)
        t3 = sb("t3", [P, NEXP], I32)
        tiles = sb("tiles", [P, NEXP])
        tincl = sb("tincl", [P, NEXP])
        base = sb("base", [P, NEXP])
        at0 = sb("at0", [P, NT, NEXP])
        at1 = sb("at1", [P, NT, NEXP])
        at = sb("at", [P, NT, NEXP])
        own = sb("own", [P, 2, NT, NEXP])
        slot = sb("slot", [P, 2, NT])
        slotd = sb("slotd", [P, 2, NT])
        cmp = sb("cmp", [P, NEXP])
        ecol = sb("ecol", [P, 1])
        ecol2 = sb("ecol2", [P, 1])
        ecoli = sb("ecoli", [P, 1], I32)
        xr = sb("xr", [P, 2, RT, C])
        ix = sb("ix", [P, 2, RT, 2], I32)
        pw = ps("pw", [P, TE])
        pt = ps("pt", [P, TE])
        c_in = sem("r_c_in")
        filled = sem("r_filled")
        step = sem("r_step")
        counted = sem("r_counted")
        e_out = sem("r_e_out")
        w_in = sem("r_weights_in")
        x_in = [sem(f"r_x_in{x}") for x in range(2)]
        staged = sem("r_staged")
        landed = [sem(f"r_landed{x}") for x in range(2)]
        NI = NT // RT
        with nc.Block() as block:
            @block.sync
            def _(sp):
                for d, n in ((valid[:, :], "valid"), (dump[:, :, :], "dump"), (triu[:, :], "triu"), (jcol[:, :], "jcol")):
                    sp.dma_start(d, A[n]).then_inc(c_in, 16)

                def load(i, x):
                    sp.dma_start(xr[:, x, :, :], W["xl"][bass.ds(i * RT * P, RT * P), :].rearrange("(j p) c -> p j c", p=P))\
                      .then_inc(x_in[x], 16)
                for x in range(2):
                    load(x, x)
                for d, n in zip(weights, ("w1", "w2", "b1", "b2")):
                    full = d[:, :, :, :] if len(d.shape) == 4 else d[:, :, :]
                    sp.dma_start(full, A[n]).then_inc(w_in, 16)
                sp.wait_ge(step, ROUTE_STEPS)
                sp.dma_start(W["emap"].rearrange("a (p o) -> p (a o)", o=1), ecoli[:, :]).then_inc(e_out, 16)
                sp.wait_ge(e_out, 16)
                sp.dma_start(emap[:, :], W["emap"]).then_inc(e_out, 16)
                for i in range(2, NI):
                    sp.wait_ge(landed[i % 2], 16 * 2 * RT * (i // 2))
                    load(i, i % 2)
                for x in range(2):
                    sp.wait_ge(landed[x], 16 * 2 * RT * ((NI - x + 1) // 2))
                sp.wait_ge(e_out, 32)
                sp.wait_ge(w_in, 64)

            @block.vector
            def _(v):
                n = [0]

                def then(ins):
                    n[0] += 1
                    ins.then_inc(step, 1)
                    v.wait_ge(step, n[0])
                v.wait_ge(c_in, 64)
                sh = [P, NT, NEXP]
                for w, m in ((0, first), (1, second)):
                    then(v.tensor_tensor(pick[:, w, :, :], m[:, 0:NT, :], bc(valid[:, :].unsqueeze(2), sh), ALU.mult))
                then(v.tensor_tensor(both[:, :, :], pick[:, 0, :, :], pick[:, 1, :, :], ALU.add))
                then(v.memset(zero[:, :], 0.0))
                v.wait_ge(counted, 2)
                then(v.tensor_copy(tot[:, :, :], pt[:, :].rearrange("p (t e) -> p t e", e=NEXP)))
                for e in range(NEXP):
                    then(v.tensor_tensor_scan(incl[:, :, e], zero[:, :], tot[:, :, e], 0.0, ALU.add, ALU.add))
                then(v.tensor_copy(t1[:, :], incl[:, NT - 1, :]))
                then(v.tensor_scalar(t2[:, :], t1[:, :], P - 1, None, ALU.add))
                then(v.tensor_scalar(t3[:, :], t2[:, :], 7, None, ALU.logical_shift_right))
                then(v.tensor_copy(tiles[:, :], t3[:, :]))
                then(v.tensor_tensor_scan(tincl[:, :], zero[:, 0:NEXP], tiles[:, :], 0.0, ALU.add, ALU.add))
                then(v.tensor_tensor(base[:, :], tincl[:, :], tiles[:, :], ALU.subtract))
                then(v.tensor_tensor(cmp[:, :], tincl[:, :], bc(jcol[:, :], [P, NEXP]), ALU.is_le))
                then(v.tensor_reduce(ecol[:, :], cmp[:, :], AX, ALU.add))
                then(v.tensor_scalar(ecol2[:, :], ecol[:, :], float(NEXP - 1), None, ALU.min))
                then(v.tensor_copy(ecoli[:, :], ecol2[:, :]))
                assert n[0] == ROUTE_STEPS
                then(v.tensor_tensor(at0[:, :, :], incl[:, :, :], tot[:, :, :], ALU.subtract))
                then(v.tensor_tensor(at1[:, :, :], at0[:, :, :], pw[:, :].rearrange("p (t e) -> p t e", e=NEXP), ALU.add))
                then(v.scalar_tensor_tensor(out=at[:, :, :], in0=bc(base[:, :].unsqueeze(1), sh), scalar=float(P),
                                            in1=at1[:, :, :], op0=ALU.mult, op1=ALU.add))
                for w in range(2):
                    then(v.tensor_tensor(own[:, w, :, :], pick[:, w, :, :], at[:, :, :], ALU.mult))
                    then(v.tensor_reduce(slot[:, w, :], own[:, w, :, :], AX, ALU.add))
                then(v.tensor_tensor(slotd[:, :, :], slot[:, :, :], dump[:, :, :], ALU.add))
                then(v.tensor_copy(slot_i[:, :, :], slotd[:, :, :]))
                then(v.memset(slot_g[:, :, :], 0))
                then(v.tensor_copy(slot_g[:, :, 0:NT], slot[:, :, :]))
                for i in range(NI):
                    if i >= 2:
                        v.wait_ge(landed[i % 2], 16 * 2 * RT * (i // 2))
                    v.tensor_copy(ix[:, i % 2, :, :], slot_i[:, :, i * RT:(i + 1) * RT].rearrange("p w t -> p t w")).then_inc(staged, 1)

            @block.gpsimd
            def _(g):
                g.memset(ones[:, :], 1.0).then_inc(filled, 1)
                for i in range(NI):
                    x = i % 2
                    g.wait_ge(staged, i + 1)
                    g.wait_ge(x_in[x], 16 * (i // 2 + 1))
                    for s in range(RT):
                        for w in range(2):
                            g.indirect_dma_start(W["xs"], bass.IndirectOffsetOnAxis(ap=ix[:, x, s, w:w + 1], axis=0),
                                                 xr[:, x, s, :], None).then_inc(landed[x], 16)

            @block.tensor
            def _(pe):
                pe.wait_ge(filled, 1)
                pe.wait_ge(step, 3)
                m = both[:, :, :].rearrange("p t e -> p (t e)")
                pe.matmul(pw[:, :], triu[:, :], m, start=True, stop=True).then_inc(counted, 1)
                pe.matmul(pt[:, :], ones[:, :], m, start=True, stop=True).then_inc(counted, 1)


ROUTE_STEPS = 23
RT = 7
assert NT % RT == 0


def experts(nc, A, W, sem, ident, emap, weights):
    with ExitStack() as cx:
        def sb(n, s, d=F32):
            return cx.enter_context(nc.sbuf_tensor("f_" + n, s, d))

        def ps(n, s, d=F32):
            return cx.enter_context(nc.psum_tensor("f_" + n, s, d))
        w1, w2, b1, b2 = weights
        x = sb("x", [P, XR, C])
        xT = sb("xT", [P, 2, KC, P])
        hb = sb("hb", [P, 2, HID])
        h = sb("h", [P, 2, HID])
        hT = sb("hT", [P, 2, HC, P])
        y = sb("y", [P, XR, C])
        px = ps("px", [P, 2, 512])
        ph = ps("ph", [P, 2, HID])
        pt = ps("pt", [P, 2, HC, P])
        py = ps("py", [P, 2, 512])
        x_in = [sem(f"f_x_in{r}") for r in range(XR)]
        x_turned = sem("f_x_turned")
        xT_done = sem("f_xT")
        up_ps = sem("f_up")
        b_done = sem("f_biased")
        h_done = sem("f_h")
        h_turned = sem("f_h_turned")
        hT_done = sem("f_hT")
        down_ps = sem("f_down")
        y_done = sem("f_y")
        stored = [sem(f"f_stored{r}") for r in range(XR)]
        with nc.Block() as block:
            @block.sync
            def _(sp):
                def load(t, r):
                    sp.dma_start(x[:, r, :], W["xs"][bass.ds(t * P, P), :]).then_inc(x_in[r], 16)
                for r in range(XR):
                    load(r, r)
                with sp.Fori(0, EXT // XR) as i:
                    for r in range(XR):
                        t = XR * i + r
                        sp.wait_ge(x_turned, t + 1)
                        load(t + XR, r)
                        sp.wait_ge(y_done, t + 1)
                        sp.dma_start(W["ys"][bass.ds(t * P, P), :], y[:, r, :]).then_inc(stored[r], 16)
                for r in range(XR):
                    sp.wait_ge(stored[r], 16 * (EXT // XR))
                    sp.wait_ge(x_in[r], 16 * (EXT // XR + 1))

            @block.vector
            def _(v):
                def turned(t, r):
                    v.wait_ge(x_turned, t + 1)
                    v.tensor_copy(xT[:, r % 2, :, :], px[:, r % 2, 0:C].rearrange("p (k n) -> p k n", k=KC)).then_inc(xT_done, 1)

                def biased(t, r, e):
                    v.wait_ge(up_ps, t + 1)
                    v.tensor_tensor(hb[:, r % 2, :].unsqueeze(1), ph[:, r % 2, :].unsqueeze(1), b1[:, bass.ds(e, 1), :],
                                    ALU.add).then_inc(b_done, 1)

                def four(i, es, first=False):
                    for r in range(XR):
                        t = XR * i + r
                        biased(t + 1, r + 1, es[r + 1])
                        v.wait_ge(down_ps, t + 1)
                        if not first:
                            v.wait_ge(stored[r], 16 * i)
                        v.tensor_tensor(y[:, r, :].unsqueeze(1), py[:, r % 2, 0:C].unsqueeze(1), b2[:, bass.ds(es[r], 1), :],
                                        ALU.add).then_inc(y_done, 1)
                        turned(t + 2, r + 2)
                turned(0, 0)
                turned(1, 1)
                es = tile_experts(nc, mybir.EngineType.DVE, emap, 0)
                biased(0, 0, es[0])
                four(0, es, first=True)
                with v.Fori(1, EXT // XR) as i:
                    four(i, tile_experts(nc, mybir.EngineType.DVE, emap, i))

            @block.scalar
            def _(a):
                def gelu(t, x):
                    a.wait_ge(b_done, t + 1)
                    a.activation(h[:, x, :], hb[:, x, :], ACT.Gelu).then_inc(h_done, 1)
                gelu(0, 0)
                with a.Fori(0, EXT // 2) as i:
                    for x in range(2):
                        a.wait_ge(h_turned, 2 * i + x + 1)
                        a.copy(hT[:, x, :, :], pt[:, x, :, :]).then_inc(hT_done, 1)
                        gelu(2 * i + x + 1, 1 - x)

            @block.tensor
            def _(pe):
                def turn_x(t, r):
                    pe.wait_ge(x_in[r % XR], 16 * (t[0] + r // XR) + 16)
                    for k in range(KC):
                        m = pe.transpose(px[:, r % 2, k * P:(k + 1) * P], x[:, r % XR, k * P:(k + 1) * P], ident[:, :])
                    m.then_inc(x_turned, 1)

                def up(t, r, e):
                    pe.wait_ge(xT_done, t + 1)
                    for k in range(KC):
                        m = pe.matmul(ph[:, r % 2, :], xT[:, r % 2, k, :], w1[:, k, bass.ds(e, 1), :],
                                      start=(k == 0), stop=(k == KC - 1))
                    m.then_inc(up_ps, 1)

                def four(i, es):
                    for r in range(XR):
                        t = XR * i + r
                        pe.wait_ge(h_done, t + 1)
                        for c in range(HC):
                            m = pe.transpose(pt[:, r % 2, c, :], h[:, r % 2, c * P:(c + 1) * P], ident[:, :])
                        m.then_inc(h_turned, 1)
                        up(t + 1, r + 1, es[r + 1])
                        pe.wait_ge(hT_done, t + 1)
                        for c in range(HC):
                            m = pe.matmul(py[:, r % 2, 0:C], hT[:, r % 2, c, :], w2[:, c, bass.ds(es[r], 1), :],
                                          start=(c == 0), stop=(c == HC - 1))
                        m.then_inc(down_ps, 1)
                        turn_x((i,), r + 2)
                turn_x((0,), 0)
                turn_x((0,), 1)
                es = tile_experts(nc, mybir.EngineType.PE, emap, 0)
                up(0, 0, es[0])
                four(0, es)
                with pe.Fori(1, EXT // XR) as i:
                    four(i, tile_experts(nc, mybir.EngineType.PE, emap, i))


XR = 4
EXT = -(-((2 * N + NEXP * (P - 1)) // P) // XR) * XR
EXA = EXT + XR
DUMP = EXA * P
EM = P
assert EXA <= EM
XFILL = 6
XROWS = (DUMP + 2 * P) // XFILL
assert XROWS * XFILL == DUMP + 2 * P and XROWS % P == 0


def tile_experts(nc, engine, emap, i):
    return nc.values_load_multi_w_load_instructions(
        emap[0:1, bass.ds(i * XR, XR + 1)], engines=[engine], min_val=0, max_val=NEXP - 1)[1]


def finish(nc, A, W, sem, slot_g, out):
    TP = 2
    NP = NTP // TP
    with ExitStack() as cx:
        def sb(n, s, d=F32):
            return cx.enter_context(nc.sbuf_tensor("o_" + n, s, d))
        ix = sb("ix", [P, 2, 2, TP], I32)
        ya = sb("ya", [P, 2, 2, TP, C])
        x2 = sb("x2", [P, 2, TP, C])
        s1 = sb("s1", [P, 2, TP, C])
        o = sb("o", [P, 2, TP, C])
        staged = sem("o_staged")
        y_in = [sem(f"o_y_in{x}") for x in range(2)]
        x_in = [sem(f"o_x_in{x}") for x in range(2)]
        summed = sem("o_summed")
        done = sem("o_done")
        stored = [sem(f"o_stored{x}") for x in range(2)]

        def pair(ap, j):
            return ap[bass.ds(j * TP * P, TP * P), :].rearrange("(j p) c -> p j c", p=P)
        with nc.Block() as block:
            @block.sync
            def _(sp):
                for x in range(2):
                    sp.dma_start(x2[:, x, :, :], pair(W["x2"], x)).then_inc(x_in[x], 16)
                with sp.Fori(0, NP // 2 - 1) as i:
                    for x in range(2):
                        sp.wait_ge(done, 2 * i + x + 1)
                        sp.dma_start(pair(out, 2 * i + x), o[:, x, :, :]).then_inc(stored[x], 16)
                        sp.dma_start(x2[:, x, :, :], pair(W["x2"], 2 * i + x + 2)).then_inc(x_in[x], 16)
                for x in range(2):
                    sp.wait_ge(done, NP - 2 + x + 1)
                    sp.dma_start(pair(out, NP - 2 + x), o[:, x, :, :]).then_inc(stored[x], 16)
                for x in range(2):
                    sp.wait_ge(stored[x], 16 * (NP // 2))

            @block.gpsimd
            def _(g):
                want = counter(g, "o_staged_want", 1)
                with g.Fori(0, NP // 2) as i:
                    for x in range(2):
                        passed(g, staged, want, 1)
                        for w in range(2):
                            for s in range(TP):
                                g.indirect_dma_start(ya[:, x, w, s, :], None, W["ys"],
                                                     bass.IndirectOffsetOnAxis(ap=ix[:, x, w, s:s + 1], axis=0))\
                                 .then_inc(y_in[x], 16)

            @block.vector
            def _(v):
                def stage(j, x):
                    v.tensor_copy(ix[:, x, :, :], slot_g[:, :, bass.ds(j * TP, TP)]).then_inc(staged, 1)

                def one(i, x, first=False):
                    j = 2 * i + x
                    v.wait_ge(y_in[x], 16 * 2 * TP * i + 16 * 2 * TP)
                    v.tensor_tensor(s1[:, x, :, :], ya[:, x, 0, :, :], ya[:, x, 1, :, :], ALU.add).then_inc(summed, 1)
                    v.wait_ge(summed, j + 1)
                    stage(j + 2, x)
                    v.wait_ge(x_in[x], 16 * i + 16)
                    if not first:
                        v.wait_ge(stored[x], 16 * i)
                    v.tensor_tensor(o[:, x, :, :], s1[:, x, :, :], x2[:, x, :, :], ALU.add).then_inc(done, 1)
                for x in range(2):
                    stage(x, x)
                for x in range(2):
                    one(0, x, first=True)
                with v.Fori(1, NP // 2) as i:
                    for x in range(2):
                        one(i, x)


def kernel(**inputs):
    import numpy as np
    import concourse.bacc as bacc
    from concourse.bass_utils import run_bass_kernel_spmd

    a = {k: np.ascontiguousarray(v) for k, v in inputs.items()}

    def halves(w):
        return np.ascontiguousarray(w.reshape(-1, P, w.shape[1]).transpose(1, 0, 2))

    def repeat(b):
        return np.ascontiguousarray(np.broadcast_to(b[None, :], (P, b.shape[0])))

    def columns(b):
        return np.ascontiguousarray(b.reshape(-1, P).T)

    f32 = np.float32
    x = np.zeros((NPAD, C), f32)
    x[:N] = a["x"]
    qkvm = a["L0_mix_Wqkv"]
    ar = np.arange
    g = "L0_gnn_"
    is_node = (ar(NT)[None, :] * P + ar(P)[:, None] < N).astype(f32)
    arrays = {
        "x": x, "src": a["src"], "dst": a["dst"],
        "wall": halves(np.concatenate([a[g + "Wq"].T, qkvm[:, C:2 * C], a[g + "Wk"].T, a[g + "Wv"].T, qkvm[:, 2 * C:]], 1)),
        "bq": repeat(a[g + "bq"]), "bkv": repeat(np.concatenate([a[g + "bk"], a[g + "bv"]])),
        "lng": columns(a["L0_mix_ln_g"]), "lnb": columns(a["L0_mix_ln_b"]),
        "vmask": np.where(ar(NTP)[None, :] * P + ar(P)[:, None] < N, 0.0, -BIG).astype(f32),
        "ident": np.eye(P, dtype=f32), "iota": np.broadcast_to(ar(P, dtype=f32)[None, :], (P, P)).copy(),
        "triu": np.triu(np.ones((P, P), f32), 1),
        "jtile": (ar(P)[:, None] * (STM // P) + ar(STM // P)[None, :]).astype(f32),
        "bdmask": halves((ar(C)[:, None] // D == ar(C)[None, :] // D).astype(f32)),
        "wqm": halves(qkvm[:, 0:C]), "wpr": halves(a["L0_mix_Wproj"]), "wo": halves(np.ascontiguousarray(a[g + "Wo"].T)),
        "wg1": halves(a["L0_mix_Wg1"]), "wg2": a["L0_mix_Wg2"], "bg1": a["L0_mix_bg1"].reshape(GH, 1),
        "bg2": columns(a["L0_mix_bg2"]), "bo": repeat(a[g + "bo"]), "bpr": repeat(a["L0_mix_bproj"]),
        "wgt": halves(a["L0_ffn_Wg"]), "bgt": repeat(a["L0_ffn_bg"]),
        "iota8": np.broadcast_to(ar(NEXP, dtype=f32)[None, :], (P, NEXP)).copy(),
        "w1": np.ascontiguousarray(a["L0_ffn_W1"].reshape(NEXP, KC, P, HID).transpose(2, 1, 0, 3)),
        "w2": np.ascontiguousarray(a["L0_ffn_W2"].reshape(NEXP, HC, P, C).transpose(2, 1, 0, 3)),
        "b1": np.broadcast_to(a["L0_ffn_b1"][None], (P, NEXP, HID)).copy(),
        "b2": np.broadcast_to(a["L0_ffn_b2"][None], (P, NEXP, C)).copy(),
        "valid": is_node, "jcol": ar(P, dtype=f32)[:, None].copy(),
        "dump": (1 - is_node[:, None, :]) * (DUMP + ar(P)[:, None, None] + P * ar(2)[None, :, None]).astype(f32),
    }
    nc = bacc.Bacc("TRN2", target_bir_lowering=False, num_devices=1)
    A = {k: nc.dram_tensor("in_" + k, v.shape, mybir.dt.from_np(v.dtype), kind="ExternalInput").ap()
         for k, v in arrays.items()}
    out = nc.dram_tensor("out", (NPAD, C), F32, kind="ExternalOutput").ap()
    build(nc, A, out)
    r = run_bass_kernel_spmd(nc, [{"in_" + k: v for k, v in arrays.items()}], core_ids=[0])
    return np.ascontiguousarray(r.results[0]["out"][:N])
```
